# Optimizing a Trainium2 kernel written in Bass

```python
import numpy as np
import jax
import jax.numpy as jnp

def _softmax(x, axis=-1):
    return jax.nn.softmax(x, axis=axis)

def _gelu(x):
    return jax.nn.gelu(x, approximate=True)

def _silu(x):
    return jax.nn.silu(x)

def _sigmoid(x):
    return jax.nn.sigmoid(x)

def _layernorm(x, axis=-1, eps=1e-05):
    m = jnp.mean(x, axis=axis, keepdims=True)
    v = jnp.var(x, axis=axis, keepdims=True)
    return (x - m) / jnp.sqrt(v + eps)

def _scatter_add(tgt, idx, src, axis=0):
    return tgt.at[idx].add(src)

def _segment_sum(src, seg, n):
    return jax.ops.segment_sum(src, seg, n)
kernel_name = 'mk_conv_seq_d2_conv_nhwc128_r4_c4fa64'

def setup_inputs(seed: int=0):
    np.random.seed(seed)
    _w = jnp.asarray

    def _rec_inputs():
        import jax
        import jax.numpy as jnp
        _gk = jax.random.key(seed)
        x = 7.22e-05 + 1 * jax.random.normal(jax.random.fold_in(_gk, 1), (1, 64, 64, 32), jnp.float32)
        return x
    x = _rec_inputs()

    def _L0_conv_setup():
        import jax, jax.numpy as jnp
        import numpy as np
        B, N, CZ, CH, CA, H, TN = (1, 64, 32, 32, 32, 4, 4)

        def _ln(x, w, b, eps=1e-05):
            m = jnp.mean(x, axis=-1, keepdims=True)
            v = jnp.mean(jnp.square(x - m), axis=-1, keepdims=True)
            return (x - m) * jax.lax.rsqrt(v + eps) * w + b

        def _tri_mul(z, lnw, lnb, apw, apb, agw, agb, bpw, bpb, bgw, bgb, gw, gb, lnow, lnob, zw, zb, outgoing):
            x = _ln(z, lnw, lnb)
            a = jax.nn.sigmoid(x @ agw + agb) * (x @ apw + apb)
            b = jax.nn.sigmoid(x @ bgw + bgb) * (x @ bpw + bpb)
            eq = 'bikc,bjkc->bijc' if outgoing else 'bkic,bkjc->bijc'
            t = jnp.einsum(eq, a, b)
            t = _ln(t, lnow, lnob) @ zw + zb
            return t * jax.nn.sigmoid(x @ gw + gb)

        def _tri_att(z, lnw, lnb, qw, kw, vw, bw, gw, gb, ow, ob):
            Bz, I, J, _ = z.shape
            x = _ln(z, lnw, lnb)
            bias = jnp.einsum('bijc,ch->bhij', x, bw)[:, None]
            q = (x @ qw).reshape(Bz, I, J, H, CA).transpose(0, 1, 3, 2, 4) / np.float32(np.sqrt(CA))
            k = (x @ kw).reshape(Bz, I, J, H, CA).transpose(0, 1, 3, 2, 4)
            v = (x @ vw).reshape(Bz, I, J, H, CA).transpose(0, 1, 3, 2, 4)
            a = jnp.einsum('bihqc,bihkc->bihqk', q, k) + bias
            p = jax.nn.softmax(a, axis=-1)
            o = jnp.einsum('bihqk,bihkc->bihqc', p, v).transpose(0, 1, 3, 2, 4).reshape(Bz, I, J, H * CA)
            o = o * jax.nn.sigmoid(x @ gw + gb)
            return o @ ow + ob
        key = jax.random.key(seed)
        ks = iter(jax.random.split(key, 16))

        def rn(shape, s=0.02):
            return jax.random.normal(next(ks), shape, dtype=jnp.float32) * s
        d = {'z': jax.random.normal(next(ks), (B, N, N, CZ), dtype=jnp.float32)}
        d['tm_ln_in_w'] = jnp.ones((2, CZ))
        d['tm_ln_in_b'] = jnp.zeros((2, CZ))
        for nm, shp in [('ap', (2, CZ, CH)), ('ag', (2, CZ, CH)), ('bp', (2, CZ, CH)), ('bg', (2, CZ, CH)), ('g', (2, CZ, CZ)), ('zo', (2, CH, CZ))]:
            d[f'tm_{nm}_w'] = rn(shp)
            d[f'tm_{nm}_b'] = jnp.zeros((2, shp[-1]))
        d['tm_lnout_w'] = jnp.ones((2, CH))
        d['tm_lnout_b'] = jnp.zeros((2, CH))
        d['ta_ln_w'] = jnp.ones((2, CZ))
        d['ta_ln_b'] = jnp.zeros((2, CZ))
        d['ta_q_w'] = rn((2, CZ, H * CA))
        d['ta_k_w'] = rn((2, CZ, H * CA))
        d['ta_v_w'] = rn((2, CZ, H * CA))
        d['ta_b_w'] = rn((2, CZ, H))
        d['ta_g_w'] = rn((2, CZ, H * CA))
        d['ta_g_b'] = jnp.zeros((2, H * CA))
        d['ta_o_w'] = rn((2, H * CA, CZ))
        d['ta_o_b'] = jnp.zeros((2, CZ))
        d['pt_ln_w'] = jnp.ones((CZ,))
        d['pt_ln_b'] = jnp.zeros((CZ,))
        d['pt_1_w'] = rn((CZ, TN * CZ))
        d['pt_1_b'] = jnp.zeros((TN * CZ,))
        d['pt_2_w'] = rn((TN * CZ, CZ))
        d['pt_2_b'] = jnp.zeros((CZ,))
        return d
    _L0_conv_all = _L0_conv_setup()
    _L0_conv_in = {k: v for k, v in _L0_conv_all.items() if k in ('tm_ln_in_w', 'tm_ln_in_b', 'tm_ap_w', 'tm_ap_b', 'tm_ag_w', 'tm_ag_b', 'tm_bp_w', 'tm_bp_b', 'tm_bg_w', 'tm_bg_b', 'tm_g_w', 'tm_g_b', 'tm_lnout_w', 'tm_lnout_b', 'tm_zo_w', 'tm_zo_b', 'ta_ln_w', 'ta_ln_b', 'ta_q_w', 'ta_k_w', 'ta_v_w', 'ta_b_w', 'ta_g_w', 'ta_g_b', 'ta_o_w', 'ta_o_b', 'pt_ln_w', 'pt_ln_b', 'pt_1_w', 'pt_1_b', 'pt_2_w', 'pt_2_b')}
    del _L0_conv_all

    def _L1_conv_setup():
        import jax, jax.numpy as jnp
        import numpy as np
        K = 5
        G = 8
        BN_EPS = 0.001
        key = jax.random.key(seed)
        ks = jax.random.split(key, 4)
        B, H, W, C = (8, 16, 16, 32)
        r = 4
        Cr = C // r
        x = jax.random.normal(ks[0], (B, H, W, C), jnp.float32)
        w1 = jax.random.normal(ks[1], (C, Cr), jnp.float32) * 0.05
        b1 = jnp.zeros((Cr,), jnp.float32)
        gamma = jnp.ones((Cr,), jnp.float32)
        beta = jnp.zeros((Cr,), jnp.float32)
        mean = jnp.zeros((Cr,), jnp.float32)
        var = jnp.ones((Cr,), jnp.float32)
        w2 = jax.random.normal(ks[2], (Cr, K * K * G), jnp.float32) * 0.05
        b2 = jnp.zeros((K * K * G,), jnp.float32)
        return dict(x=x, w1=w1, b1=b1, gamma=gamma, beta=beta, mean=mean, var=var, w2=w2, b2=b2)
    _L1_conv_all = _L1_conv_setup()
    _L1_conv_in = {k: v for k, v in _L1_conv_all.items() if k in ('w1', 'b1', 'gamma', 'beta', 'mean', 'var', 'w2', 'b2')}
    del _L1_conv_all
    return {'x': x, 'L0_conv_tm_ln_in_w': _L0_conv_in['tm_ln_in_w'], 'L0_conv_tm_ln_in_b': _L0_conv_in['tm_ln_in_b'], 'L0_conv_tm_ap_w': _L0_conv_in['tm_ap_w'], 'L0_conv_tm_ap_b': _L0_conv_in['tm_ap_b'], 'L0_conv_tm_ag_w': _L0_conv_in['tm_ag_w'], 'L0_conv_tm_ag_b': _L0_conv_in['tm_ag_b'], 'L0_conv_tm_bp_w': _L0_conv_in['tm_bp_w'], 'L0_conv_tm_bp_b': _L0_conv_in['tm_bp_b'], 'L0_conv_tm_bg_w': _L0_conv_in['tm_bg_w'], 'L0_conv_tm_bg_b': _L0_conv_in['tm_bg_b'], 'L0_conv_tm_g_w': _L0_conv_in['tm_g_w'], 'L0_conv_tm_g_b': _L0_conv_in['tm_g_b'], 'L0_conv_tm_lnout_w': _L0_conv_in['tm_lnout_w'], 'L0_conv_tm_lnout_b': _L0_conv_in['tm_lnout_b'], 'L0_conv_tm_zo_w': _L0_conv_in['tm_zo_w'], 'L0_conv_tm_zo_b': _L0_conv_in['tm_zo_b'], 'L0_conv_ta_ln_w': _L0_conv_in['ta_ln_w'], 'L0_conv_ta_ln_b': _L0_conv_in['ta_ln_b'], 'L0_conv_ta_q_w': _L0_conv_in['ta_q_w'], 'L0_conv_ta_k_w': _L0_conv_in['ta_k_w'], 'L0_conv_ta_v_w': _L0_conv_in['ta_v_w'], 'L0_conv_ta_b_w': _L0_conv_in['ta_b_w'], 'L0_conv_ta_g_w': _L0_conv_in['ta_g_w'], 'L0_conv_ta_g_b': _L0_conv_in['ta_g_b'], 'L0_conv_ta_o_w': _L0_conv_in['ta_o_w'], 'L0_conv_ta_o_b': _L0_conv_in['ta_o_b'], 'L0_conv_pt_ln_w': _L0_conv_in['pt_ln_w'], 'L0_conv_pt_ln_b': _L0_conv_in['pt_ln_b'], 'L0_conv_pt_1_w': _L0_conv_in['pt_1_w'], 'L0_conv_pt_1_b': _L0_conv_in['pt_1_b'], 'L0_conv_pt_2_w': _L0_conv_in['pt_2_w'], 'L0_conv_pt_2_b': _L0_conv_in['pt_2_b'], 'L1_conv_w1': _L1_conv_in['w1'], 'L1_conv_b1': _L1_conv_in['b1'], 'L1_conv_gamma': _L1_conv_in['gamma'], 'L1_conv_beta': _L1_conv_in['beta'], 'L1_conv_mean': _L1_conv_in['mean'], 'L1_conv_var': _L1_conv_in['var'], 'L1_conv_w2': _L1_conv_in['w2'], 'L1_conv_b2': _L1_conv_in['b2']}

def reference(x, L0_conv_tm_ln_in_w, L0_conv_tm_ln_in_b, L0_conv_tm_ap_w, L0_conv_tm_ap_b, L0_conv_tm_ag_w, L0_conv_tm_ag_b, L0_conv_tm_bp_w, L0_conv_tm_bp_b, L0_conv_tm_bg_w, L0_conv_tm_bg_b, L0_conv_tm_g_w, L0_conv_tm_g_b, L0_conv_tm_lnout_w, L0_conv_tm_lnout_b, L0_conv_tm_zo_w, L0_conv_tm_zo_b, L0_conv_ta_ln_w, L0_conv_ta_ln_b, L0_conv_ta_q_w, L0_conv_ta_k_w, L0_conv_ta_v_w, L0_conv_ta_b_w, L0_conv_ta_g_w, L0_conv_ta_g_b, L0_conv_ta_o_w, L0_conv_ta_o_b, L0_conv_pt_ln_w, L0_conv_pt_ln_b, L0_conv_pt_1_w, L0_conv_pt_1_b, L0_conv_pt_2_w, L0_conv_pt_2_b, L1_conv_w1, L1_conv_b1, L1_conv_gamma, L1_conv_beta, L1_conv_mean, L1_conv_var, L1_conv_w2, L1_conv_b2):
    import jax
    import jax.numpy as jnp

    def _L0_conv_ref(z, tm_ln_in_w, tm_ln_in_b, tm_ap_w, tm_ap_b, tm_ag_w, tm_ag_b, tm_bp_w, tm_bp_b, tm_bg_w, tm_bg_b, tm_g_w, tm_g_b, tm_lnout_w, tm_lnout_b, tm_zo_w, tm_zo_b, ta_ln_w, ta_ln_b, ta_q_w, ta_k_w, ta_v_w, ta_b_w, ta_g_w, ta_g_b, ta_o_w, ta_o_b, pt_ln_w, pt_ln_b, pt_1_w, pt_1_b, pt_2_w, pt_2_b):
        import jax, jax.numpy as jnp
        import numpy as np
        B, N, CZ, CH, CA, H, TN = (1, 64, 32, 32, 32, 4, 4)

        def _ln(x, w, b, eps=1e-05):
            m = jnp.mean(x, axis=-1, keepdims=True)
            v = jnp.mean(jnp.square(x - m), axis=-1, keepdims=True)
            return (x - m) * jax.lax.rsqrt(v + eps) * w + b

        def _tri_mul(z, lnw, lnb, apw, apb, agw, agb, bpw, bpb, bgw, bgb, gw, gb, lnow, lnob, zw, zb, outgoing):
            x = _ln(z, lnw, lnb)
            a = jax.nn.sigmoid(x @ agw + agb) * (x @ apw + apb)
            b = jax.nn.sigmoid(x @ bgw + bgb) * (x @ bpw + bpb)
            eq = 'bikc,bjkc->bijc' if outgoing else 'bkic,bkjc->bijc'
            t = jnp.einsum(eq, a, b)
            t = _ln(t, lnow, lnob) @ zw + zb
            return t * jax.nn.sigmoid(x @ gw + gb)

        def _tri_att(z, lnw, lnb, qw, kw, vw, bw, gw, gb, ow, ob):
            Bz, I, J, _ = z.shape
            x = _ln(z, lnw, lnb)
            bias = jnp.einsum('bijc,ch->bhij', x, bw)[:, None]
            q = (x @ qw).reshape(Bz, I, J, H, CA).transpose(0, 1, 3, 2, 4) / np.float32(np.sqrt(CA))
            k = (x @ kw).reshape(Bz, I, J, H, CA).transpose(0, 1, 3, 2, 4)
            v = (x @ vw).reshape(Bz, I, J, H, CA).transpose(0, 1, 3, 2, 4)
            a = jnp.einsum('bihqc,bihkc->bihqk', q, k) + bias
            p = jax.nn.softmax(a, axis=-1)
            o = jnp.einsum('bihqk,bihkc->bihqc', p, v).transpose(0, 1, 3, 2, 4).reshape(Bz, I, J, H * CA)
            o = o * jax.nn.sigmoid(x @ gw + gb)
            return o @ ow + ob

        def tm(zz, i, outgoing):
            return _tri_mul(zz, tm_ln_in_w[i], tm_ln_in_b[i], tm_ap_w[i], tm_ap_b[i], tm_ag_w[i], tm_ag_b[i], tm_bp_w[i], tm_bp_b[i], tm_bg_w[i], tm_bg_b[i], tm_g_w[i], tm_g_b[i], tm_lnout_w[i], tm_lnout_b[i], tm_zo_w[i], tm_zo_b[i], outgoing)

        def ta(zz, i):
            return _tri_att(zz, ta_ln_w[i], ta_ln_b[i], ta_q_w[i], ta_k_w[i], ta_v_w[i], ta_b_w[i], ta_g_w[i], ta_g_b[i], ta_o_w[i], ta_o_b[i])
        z = z + tm(z, 0, True)
        z = z + tm(z, 1, False)
        z = z + ta(z, 0)
        zt = jnp.swapaxes(z, 1, 2)
        zt = zt + ta(zt, 1)
        z = jnp.swapaxes(zt, 1, 2)
        x = _ln(z, pt_ln_w, pt_ln_b)
        z = z + (jax.nn.relu(x @ pt_1_w + pt_1_b) @ pt_2_w + pt_2_b)
        return z

    def _L1_conv_ref(x, w1, b1, gamma, beta, mean, var, w2, b2):
        import jax, jax.numpy as jnp
        import numpy as np
        K = 5
        G = 8
        BN_EPS = 0.001
        B, H, W, C = x.shape
        pad = (K - 1) // 2
        z = jnp.einsum('bhwc,cd->bhwd', x, w1) + b1
        z = gamma * (z - mean) / jnp.sqrt(var + BN_EPS) + beta
        z = jax.nn.relu(z)
        kern = jnp.einsum('bhwd,dk->bhwk', z, w2) + b2
        kern = kern.reshape(B, H, W, K * K, G)
        xp = jnp.pad(x, ((0, 0), (pad, pad), (pad, pad), (0, 0)))
        patches = jnp.stack([xp[:, i:i + H, j:j + W, :] for i in range(K) for j in range(K)], axis=3)
        patches = patches.reshape(B, H, W, K * K, C // G, G)
        out = jnp.einsum('bhwpg,bhwpng->bhwng', kern, patches)
        return out.reshape(B, H, W, C)

    def _gn(v, G=32, eps=1e-05):
        B_, H_, W_, C_ = v.shape
        g = v.reshape(B_, H_, W_, G, C_ // G)
        m = jnp.mean(g, axis=(1, 2, 4), keepdims=True)
        s = jnp.var(g, axis=(1, 2, 4), keepdims=True)
        return ((g - m) / jnp.sqrt(s + eps)).reshape(v.shape)

    def _ln_c(v, eps=1e-06):
        m = jnp.mean(v, axis=-1, keepdims=True)
        s = jnp.var(v, axis=-1, keepdims=True)
        return (v - m) / jnp.sqrt(s + eps)

    def _ln_t(v, eps=1e-05):
        m = jnp.mean(v, axis=-1, keepdims=True)
        s = jnp.var(v, axis=-1, keepdims=True)
        return (v - m) / jnp.sqrt(s + eps)

    def _to_tokens(v):
        B_, H_, W_, C_ = v.shape
        return v.reshape(B_, H_ * W_, C_)

    def _from_tokens(t, like):
        return t.reshape(like.shape)
    x = _L0_conv_ref(x, L0_conv_tm_ln_in_w, L0_conv_tm_ln_in_b, L0_conv_tm_ap_w, L0_conv_tm_ap_b, L0_conv_tm_ag_w, L0_conv_tm_ag_b, L0_conv_tm_bp_w, L0_conv_tm_bp_b, L0_conv_tm_bg_w, L0_conv_tm_bg_b, L0_conv_tm_g_w, L0_conv_tm_g_b, L0_conv_tm_lnout_w, L0_conv_tm_lnout_b, L0_conv_tm_zo_w, L0_conv_tm_zo_b, L0_conv_ta_ln_w, L0_conv_ta_ln_b, L0_conv_ta_q_w, L0_conv_ta_k_w, L0_conv_ta_v_w, L0_conv_ta_b_w, L0_conv_ta_g_w, L0_conv_ta_g_b, L0_conv_ta_o_w, L0_conv_ta_o_b, L0_conv_pt_ln_w, L0_conv_pt_ln_b, L0_conv_pt_1_w, L0_conv_pt_1_b, L0_conv_pt_2_w, L0_conv_pt_2_b)
    x = _L1_conv_ref(x, L1_conv_w1, L1_conv_b1, L1_conv_gamma, L1_conv_beta, L1_conv_mean, L1_conv_var, L1_conv_w2, L1_conv_b2)
    return x

_drawn_inputs = setup_inputs


def setup_inputs(seed=0):
    import zlib

    import numpy as np

    out = dict(_drawn_inputs(seed))
    spreads = {'L0_conv_tm_ln_in_w': (1.0, 0.6),
     'L0_conv_tm_ln_in_b': (0.0, 0.519),
     'L0_conv_tm_ap_b': (0.0, 0.1),
     'L0_conv_tm_ag_b': (0.0, 2.0),
     'L0_conv_tm_bp_b': (0.0, 0.1),
     'L0_conv_tm_bg_b': (0.0, 2.0),
     'L0_conv_tm_g_b': (0.0, 0.8),
     'L0_conv_tm_lnout_w': (1.0, 0.6),
     'L0_conv_tm_lnout_b': (0.0, 0.8),
     'L0_conv_tm_zo_b': (0.0, 0.1),
     'L0_conv_ta_ln_w': (1.0, 0.6),
     'L0_conv_ta_ln_b': (0.0, 0.8),
     'L0_conv_ta_g_b': (0.0, 0.8),
     'L0_conv_ta_o_b': (0.0, 0.1),
     'L0_conv_pt_ln_w': (1.0, 0.6),
     'L0_conv_pt_ln_b': (0.0, 0.8),
     'L0_conv_pt_1_b': (0.0, 0.682),
     'L0_conv_pt_2_b': (0.0, 0.1),
     'L1_conv_b1': (0.0, 0.1),
     'L1_conv_gamma': (1.0, 0.2),
     'L1_conv_beta': (0.0, 0.1),
     'L1_conv_mean': (0.0, 0.1),
     'L1_conv_var': (1.0, 0.2),
     'L1_conv_b2': (0.0, 0.1)}
    factors = {'L0_conv_tm_ag_w': 8.0,
     'L0_conv_tm_bg_w': 8.0,
     'L0_conv_tm_g_w': 7.869,
     'L0_conv_ta_q_w': 8.0,
     'L0_conv_ta_k_w': 8.0,
     'L0_conv_ta_v_w': 8.0,
     'L0_conv_ta_b_w': 8.0,
     'L0_conv_ta_g_w': 8.0,
     'L0_conv_ta_o_w': 8.0,
     'L0_conv_pt_1_w': 3.752,
     'L0_conv_pt_2_w': 2.723}
    for name, (base, spread) in spreads.items():
        noise = np.random.default_rng([zlib.crc32(name.encode()), seed]).standard_normal(out[name].shape)
        drawn = base * np.exp(spread * noise) if base else spread * noise
        out[name] = jnp.asarray(drawn.astype(out[name].dtype))
    for name, factor in factors.items():
        out[name] = (out[name] * factor).astype(out[name].dtype)
    return out
```

```python
from contextlib import ExitStack

import concourse.bass as bass
from concourse import mybir

ALU = mybir.AluOpType
ACT = mybir.ActivationFunctionType
F32 = mybir.dt.float32
F32R = mybir.dt.float32r
AX_X = mybir.AxisListType.X

N = 64
C = 32
GB = 128 // C
RB = N // GB
F = RB * N
HALF = F // 2
HB = RB // 2
H = 4
CH = C // 2
TAPS = 25
KS = 5
PAD = KS // 2
G8 = 8
PW = N + 2 * PAD
PH = RB + 2 * PAD

VEC = {}
for _s in range(2):
    for _n in ("lnin_w", "lnin_b", "lnout_w", "lnout_b", "zb"):
        VEC[f"tm{_s}_{_n}"] = len(VEC)
    for _n in ("ln_w", "ln_b", "ob"):
        VEC[f"ta{_s}_{_n}"] = len(VEC)
for _n in ("pt_w", "pt_b", "pt_b1", "pt_b2", "bn_b1", "bn_gamma", "bn_beta", "bn_mean", "bn_var",
           "tm0_gb", "tm1_gb", "ta0_gb", "ta1_gb",
           "eps5", "eps5x16", "eps3", "mask_g0", "mask_g1", "lo_z", "lo_w", "lo_pair", "lo_row"):
    VEC[_n] = len(VEC)
VEC["b2"] = len(VEC)
NVEC = VEC["b2"] + TAPS

CONST = ("ident", "center", "mean", "bdscale", "pair")


def build_program(nc, z_rows, z_cols, vecs, consts, selrow, tm_w, tm_rows, ta_w, ta_qk, pt_w, inv_w1, inv_w2, out):
    with ExitStack() as ctx:
        def sb(name, cols, dt=F32, parts=128):
            return ctx.enter_context(nc.sbuf_tensor(name, [parts, cols], dt))

        signals = {}
        NORMS = ("tm0_ln", "tm0_lng", "tm0_lno", "tm1_ln", "tm1_lno", "ta0_ln", "ta1_ln", "pt_ln")
        RAISES = {"abproj": 8, "abtanh": 8, "ab": 8, "t": 4, "tB_act": 1, "tB_dve": 1, "bhi": 1, "braw": 32, "bias_hop": 16,
                  "proj": 24, "proj_act": 20, "proj_dve": 12}
        RAISES.update({k: 16 for k in ("scores", "max", "shifted", "exp", "sum", "rinv", "probs", "ptrans", "PT", "av", "og")})

        def shared(name):
            for norm in NORMS:
                if name.startswith(norm + "_"):
                    return "ln_" + name[len(norm) + 1:], 2 * NORMS.index(norm)
            for kind in ("tm", "ta"):
                if name[:2] == kind and name[2] in "01" and name[3] == "_":
                    return kind + name[3:], int(name[2]) * RAISES.get(name[4:], 2)
            return name, 0

        def sig(name):
            name = shared(name)[0]
            if name not in signals:
                signals[name] = ctx.enter_context(nc.semaphore(name))
            return signals[name]

        def at(name, count):
            return shared(name)[1] + count

        bank = [ctx.enter_context(nc.psum_tensor(f"bank{i}", [128, HALF], F32)) for i in range(8)]

        z0R = sb("z0R", F)
        z0T = sb("z0T", F)
        vec = sb("vec", NVEC)
        cst = sb("cst", 128 * len(CONST))
        selraw = sb("selraw", 128, parts=4)
        tmw = sb("tmw", 2 * 768)
        taw = sb("taw", 2 * 688)
        ptw = sb("ptw", 160)
        ivw1 = sb("ivw1", 128)

        def V(name):
            return vec[:, VEC[name]:VEC[name] + 1]

        def K(name):
            i = CONST.index(name)
            return cst[:, 128 * i:128 * i + 128]

        halfgb = sb("halfgb", 4)
        selr = sb("selr", 128, F32R, parts=4)
        rows = sb("rows", 2 * 512, F32R, parts=4)
        pairr = sb("pairr", 128, F32R)
        wyh = sb("wyh", 2 * H * 128)
        wohalf = sb("wohalf", 2 * C)
        bnscale = sb("bnscale", 4)
        w2s = sb("w2s", TAPS * 128, F32R)

        Y = sb("Y", H * F)
        xbd = sb("xbd", RB * 128)
        vbd = sb("vbd", RB * GB * 2 * 64)
        gth = sb("gth", GB * F)
        og = sb("og", GB * F)
        braw = sb("braw", H * N)
        bhi = sb("bhi", H * N, F32R)
        bst = sb("bst", 2 * H * N, F32R)
        mx = sb("mx", 16 * 8)
        rsum = sb("rsum", 16 * 8)
        rinv = sb("rinv", 16 * 8)
        soft = sb("soft", 7 * HALF)
        E_ = [soft[:, i * HALF:(i + 1) * HALF] for i in range(3)]
        PN = [soft[:, i * HALF:(i + 1) * HALF] for i in (3, 4)]
        PT = [soft[:, i * HALF:(i + 1) * HALF] for i in (5, 6)]

        sq = [sb("sq", F), Y[:, 0:F]]
        std = [sb("std", F), Y[:, F:2 * F]]
        rstd = [sb("rstd", F), Y[:, 2 * F:3 * F]]
        xn = [sb("xn", F), Y[:, 3 * F:4 * F]]

        x = sb("x", F)
        y = sb("y", F)
        gate = sb("gate", F)
        gateR = sb("gateR", F)
        th = sb("th", F)
        xg = gateR
        abth = soft[:, 4 * HALF:5 * HALF]
        ab = xbd
        tP = og[0:64, 0:2 * F]
        tB = og[:, 2 * F:3 * F]
        upd = og[:, 3 * F:4 * F]
        brow = y[0:16, :]
        z1T = sb("z1T", F)
        z1R = sb("z1R", F)
        z2R = sb("z2R", F)
        z3R, z4T, z3T = z0R, z0T, z1R
        perm = [vbd[:, 0:F], vbd[:, F:2 * F], gate]
        arrive = [vbd[:, 2 * F:3 * F], vbd[:, 3 * F:4 * F], z1T]

        qk = soft[0:32, 0:2 * 2 * H * 128]
        rowraw = gate[0:4, :]
        rowhi = th[0:4, :].bitcast(F32R)
        ivw2raw = gth[:, 0:TAPS * 128]
        w2hi = Y[:, 0:TAPS * 128].bitcast(F32R)

        hid = [og[:, i * HALF:(i + 1) * HALF] for i in range(4)]
        xpad = soft[:, 0:PH * PW]
        zr = og[:, 2 * F:3 * F]
        zhi = og[:, 3 * F:4 * F].bitcast(F32R)
        zst = sb("zst", F, F32R)
        NPROD = 6
        prod = [gth[:, i * HALF:(i + 1) * HALF] for i in range(NPROD)]
        res = Y[:, 0:F]

        hop = [nc.dram_tensor(f"hop{i}", (128, F), F32, kind="Internal").ap() for i in range(3)]
        bias_hop = [nc.dram_tensor(f"bias_hop{i}", (GB * H, F), F32, kind="Internal").ap() for i in range(2)]

        def half(buf, ch):
            return buf[:, ch * HALF:(ch + 1) * HALF]

        def raw_cols(ap):
            return ap.rearrange("p (n r g) -> p n g r", n=HB, g=GB)

        def sorted_cols(ap):
            return ap.rearrange("p (n g r) -> p n g r", n=HB, g=GB)

        xpad_v = xpad[:, :].rearrange("p (a b) -> p a b", b=PW)

        def window(ch, dr, dn):
            r0 = PAD + HB * ch + dr
            return xpad_v[:, r0:r0 + HB, PAD + dn:PAD + dn + N]

        def rows8(ap):
            return ap.rearrange("p (a b) -> p a b", b=N)

        TILES = 16

        def tile_of(t):
            return t // 8, 2 * (t % 8)

        PROJ = [("y", n) for n in range(8)] + [("v", n) for n in range(8)] + [("g", n) for n in range(8)]
        PRING = (0, 1, 2, 3, 6, 7)

        def act_evicts(kind, n):
            return kind != "y" or n % 2 == 0

        def dve_evicts(kind, n):
            return kind == "v" or (kind == "y" and n % 2 == 1)

        def count_proj(evicts, m):
            return sum(1 for k in PROJ[:m] if evicts(*k))

        TAP_ORDER = sorted(range(TAPS), key=lambda p: (p % KS != PAD, p))
        KERN = [(p, ch) for p in TAP_ORDER for ch in range(2)]
        KRING = (2, 3, 4, 5, 6, 7)

        LN = {
            "tm0_ln": (z0R, x, 0, (0, 1), (2, 3), "tm0_lnin", "eps5"),
            "tm0_lng": (z0T, xg, 1, (0, 1), (2, 3), "tm0_lnin", "eps5"),
            "tm0_lno": (tB, y, 0, (0, 1), (4, 5), "tm0_lnout", "eps5x16"),
            "tm1_ln": (z1T, x, 0, (0, 1), (2, 3), "tm1_lnin", "eps5"),
            "tm1_lno": (tB, y, 0, (0, 1), (4, 5), "tm1_lnout", "eps5x16"),
            "ta0_ln": (z2R, x, 0, (0, 1), (2, 3), "ta0_ln", "eps5"),
            "ta1_ln": (arrive[2], x, 0, (0, 1), (2, 3), "ta1_ln", "eps5"),
            "pt_ln": (z4T, x, 0, (0, 1), (2, 3), "pt", "eps5"),
        }

        def received(buf, ch):
            return buf[:, :].rearrange("p (s r n) -> p r s n", s=GB, n=RB)[:, HB * ch:HB * ch + HB]

        block = ctx.enter_context(nc.Block())

        @block.sync
        def _(sp):
            sp.dma_start(z0R[:, :], z_rows).then_inc(sig("in_z0R"), 16)
            sp.dma_start(cst[:, :], consts).then_inc(sig("in_const"), 16)
            sp.dma_start(vec[:, :], vecs).then_inc(sig("in_vec"), 16)
            sp.dma_start(tmw[:, :], tm_w).then_inc(sig("in_tmw"), 16)
            sp.dma_start(z0T[:, :], z_cols).then_inc(sig("in_z0T"), 16)

            def relayout(i, name):
                sp.wait_ge(sig(f"{name}_permuted"), at(f"{name}_permuted", 1))
                sp.dma_start(hop[i][:, :], perm[i][:, :]).then_inc(sig(f"{name}_hop"), 16)
                sp.wait_ge(sig(f"{name}_hop"), at(f"{name}_hop", 16))
                for g in range(GB):
                    sp.dma_start(arrive[i][g * C:(g + 1) * C, :].rearrange("c (s f) -> c s f", s=GB),
                                 hop[i][:, g * RB * RB:(g + 1) * RB * RB].rearrange("(s c) f -> c s f", s=GB),
                                 ).then_inc(sig(f"{name}_arrived"), 16)

            relayout(0, "z1")
            relayout(1, "gate1")

            def pair_bias(st, s):
                sp.wait_ge(sig(f"{st}_brow"), at(f"{st}_brow", 2))
                sp.dma_start(bias_hop[s][:, :], brow).then_inc(sig(f"{st}_bias_hop"), 16)
                sp.wait_ge(sig(f"{st}_bias_hop"), at(f"{st}_bias_hop", 16))
                for part in range(2):
                    sp.dma_start(braw[part * N:(part + 1) * N, :].rearrange("q (h k) -> q h k", h=H),
                                 bias_hop[s].rearrange("(h g) (r k) -> (g r) h k", h=H, k=N)).then_inc(sig(f"{st}_braw"), 16)

            pair_bias("ta0", 0)
            relayout(2, "z3")
            pair_bias("ta1", 1)
            sp.wait_ge(sig("pt_z"), at("pt_z", 2))
            sp.dma_start(xpad_v[C:128, 0:PAD, :], xpad_v[0:128 - C, RB:RB + PAD, :]).then_inc(sig("halo"), 16)
            sp.dma_start(xpad_v[0:128 - C, PAD + RB:PH, :], xpad_v[C:128, PAD:2 * PAD, :]).then_inc(sig("halo"), 16)
            for ch in range(2):
                sp.wait_ge(sig("inv_result"), at("inv_result", ch + 1))
                sp.dma_start(out[:, ch * HALF:(ch + 1) * HALF], half(res, ch)).then_inc(sig("stored"), 16)
            sp.wait_ge(sig("stored"), at("stored", 32))

        @block.gpsimd
        def _(pool):
            pool.dma_start(selraw[:, :], selrow).then_inc(sig("in_rows"), 16)
            pool.dma_start(rowraw[:, :], tm_rows).then_inc(sig("in_rows"), 16)
            pool.dma_start(qk[:, :], ta_qk).then_inc(sig("in_qk"), 16)
            pool.dma_start(taw[:, :], ta_w).then_inc(sig("in_taw"), 16)
            pool.dma_start(ptw[:, :], pt_w).then_inc(sig("in_ptw"), 16)
            pool.dma_start(ivw1[:, :], inv_w1).then_inc(sig("in_ivw1"), 16)
            pool.dma_start(ivw2raw, inv_w2).then_inc(sig("in_ivw2"), 16)

            def permute(i, name, src, ready):
                pool.wait_ge(sig(ready), at(ready, 2))
                pool.tensor_copy(perm[i][:, :].rearrange("p (g n r) -> p r g n", g=GB, n=RB),
                                 src[:, :].rearrange("p (r g n) -> p r g n", g=GB, n=RB)).then_inc(sig(f"{name}_permuted"), 1)

            def settle(i, name, dst):
                pool.wait_ge(sig(f"{name}_arrived"), at(f"{name}_arrived", 16 * GB))
                pool.tensor_copy(dst[:, :].rearrange("p (r s n) -> p r s n", s=GB, n=RB),
                                 arrive[i][:, :].rearrange("p (s r n) -> p r s n", s=GB, n=RB)).then_inc(sig(f"{name}_settled"), 1)

            permute(0, "z1", z1T, "tm0_z")
            permute(1, "gate1", gate, "tm1_gate")
            settle(0, "z1", z1R)
            settle(1, "gate1", gateR)

            pool.wait_ge(sig("z1_settled"), at("z1_settled", 1))
            pool.wait_ge(sig("gate1_settled"), at("gate1_settled", 1))
            for h2 in range(2):
                off = vbd[64 * h2:64 * h2 + 64, :].rearrange("p (a h c) -> p a h c", h=2, c=C)[:, :, 1 - h2, :]
                pool.memset(off, 0.0).then_inc(sig("vbd_zero"), 1)

            def normalise(st):
                for t in range(TILES):
                    pool.wait_ge(sig(f"{st}_rinv"), at(f"{st}_rinv", t + 1))
                    if t >= 2:
                        pool.wait_ge(sig(f"{st}_ptrans"), at(f"{st}_ptrans", t - 1))
                    pool.tensor_tensor(
                        PN[t % 2][:, :].rearrange("p (a k) -> p a k", k=N),
                        E_[t % 3][:, :].rearrange("p (a k) -> p a k", k=N),
                        rinv[:, 8 * t:8 * t + 8].unsqueeze(2).broadcast_to([128, 8, N]), ALU.mult,
                    ).then_inc(sig(f"{st}_probs"), 1)

            normalise("ta0")
            permute(2, "z3", z3R, "ta0_z")
            settle(2, "z3", z3T)
            normalise("ta1")
            pool.wait_ge(sig("ta1_probs"), at("ta1_probs", TILES))
            pool.memset(xpad[:, :], 0.0).then_inc(sig("xpad_zero"), 1)

        @block.scalar
        def _(act):
            def layer_norm(name):
                src, dst, sset, cb, vb, w, eps = LN[name]
                for ch in range(2):
                    act.wait_ge(sig(f"{name}_centered"), at(f"{name}_centered", ch + 1))
                    nc.scalar.activation(half(sq[sset], ch), bank[cb[ch]][:, :], ACT.Square).then_inc(sig(f"{name}_sq"), 1)
                for ch in range(2):
                    act.wait_ge(sig(f"{name}_var"), at(f"{name}_var", ch + 1))
                    nc.scalar.activation(half(std[sset], ch), bank[vb[ch]][:, :], ACT.Sqrt, bias=V(eps)).then_inc(sig(f"{name}_std"), 1)

            act.wait_ge(sig("in_vec"), at("in_vec", 16))
            nc.scalar.activation(bnscale[:, 0:1], V("bn_var"), ACT.Sqrt, bias=V("eps3")).then_inc(sig("bn_std"), 1)
            layer_norm("tm0_ln")
            layer_norm("tm0_lng")

            def ab_tanh(st):
                for u in range(8):
                    act.wait_ge(sig(f"{st}_abproj"), at(f"{st}_abproj", u + 1))
                    if u >= 2:
                        act.wait_ge(sig(f"{st}_ab"), at(f"{st}_ab", u - 1))
                    nc.scalar.activation(
                        abth[:, (u % 2) * 256:(u % 2) * 256 + 256].rearrange("p (a k) -> p a k", k=C),
                        bank[4 + u % 4][:, :].rearrange("p (a k) -> p a k", k=2 * C)[:, :, C:2 * C],
                        ACT.Tanh, scale=0.5).then_inc(sig(f"{st}_abtanh"), 1)

            def tm_rest(st, s):
                for ch in range(2):
                    act.wait_ge(sig(f"{st}_gproj"), at(f"{st}_gproj", ch + 1))
                    act.wait_ge(sig("halfgb"), at("halfgb", 1))
                    nc.scalar.activation(half(th, ch), bank[ch][:, :], ACT.Tanh, bias=halfgb[:, s:s + 1],
                                         scale=0.5).then_inc(sig(f"{st}_gtanh"), 1)
                for b in (0, 2):
                    act.wait_ge(sig(f"{st}_t"), at(f"{st}_t", b + 1))
                    nc.scalar.activation(tP[:, :].rearrange("m (n g c) -> m c g n", g=GB, c=C)[:, 8 * b:8 * b + 8],
                                         bank[4 + b][0:64, :].rearrange("m (c g n) -> m c g n", c=8, g=GB),
                                         ACT.Copy).then_inc(sig(f"{st}_tP_act"), 1)
                act.wait_ge(sig(f"{st}_ttr"), at(f"{st}_ttr", 1))
                nc.scalar.activation(sorted_cols(half(tB, 0)), raw_cols(bank[2][:, :]), ACT.Copy).then_inc(sig(f"{st}_tB_act"), 1)

            ab_tanh("tm0")
            tm_rest("tm0", 0)
            layer_norm("tm0_lno")
            layer_norm("tm1_ln")
            ab_tanh("tm1")
            tm_rest("tm1", 1)
            layer_norm("tm1_lno")

            def attention(st, s):
                layer_norm(f"{st}_ln")
                for ch in range(2):
                    act.wait_ge(sig(f"{st}_bproj"), at(f"{st}_bproj", ch + 1))
                    nc.scalar.activation(brow[:, ch * HALF:(ch + 1) * HALF], bank[4 + ch][0:16, :],
                                         ACT.Copy).then_inc(sig(f"{st}_brow"), 1)
                act.wait_ge(sig("vbd_zero"), at("vbd_zero", 2))
                for m, (kind, n) in enumerate(PROJ):
                    if not act_evicts(kind, n):
                        continue
                    act.wait_ge(sig(f"{st}_proj"), at(f"{st}_proj", m + 1))
                    src = bank[PRING[m % 6]]
                    if kind == "y":
                        op = nc.scalar.activation(Y[:, (n // 2) * F:(n // 2 + 1) * F][:, (n % 2) * HALF:(n % 2 + 1) * HALF],
                                                  src[:, :], ACT.Copy)
                    elif kind == "v":
                        op = nc.scalar.activation(v_slot(0, n), src[0:64, :].rearrange("p (a c) -> p a c", c=C), ACT.Copy)
                    else:
                        op = nc.scalar.activation(gth[:, n * HALF:(n + 1) * HALF], src[:, :], ACT.Tanh,
                                                  bias=halfgb[:, 2 + s:3 + s], scale=0.5)
                    op.then_inc(sig(f"{st}_proj_act"), 1)
                for t in range(TILES + 2):
                    if t < TILES:
                        act.wait_ge(sig(f"{st}_shifted"), at(f"{st}_shifted", t + 1))
                        nc.scalar.activation(E_[t % 3][:, :], E_[t % 3][:, :], ACT.Exp).then_inc(sig(f"{st}_exp"), 1)
                    if t >= 2:
                        u = t - 2
                        act.wait_ge(sig(f"{st}_ptrans"), at(f"{st}_ptrans", u + 1))
                        if u >= 2:
                            act.wait_ge(sig(f"{st}_av"), at(f"{st}_av", u - 1))
                        nc.scalar.activation(PT[u % 2][:, :], bank[3 + u % 2][:, :], ACT.Copy).then_inc(sig(f"{st}_PT"), 1)

            def v_slot(h2, n):
                v = vbd[64 * h2:64 * h2 + 64, :].rearrange("p (a h c) -> p a h c", h=2, c=C)
                return v[:, 16 * n:16 * n + 16, h2, :]

            attention("ta0", 0)
            attention("ta1", 1)
            layer_norm("pt_ln")
            for n in range(0, 8, 2):
                act.wait_ge(sig("pt_hproj"), at("pt_hproj", n + 1))
                if n >= 4:
                    act.wait_ge(sig("pt_hused"), at("pt_hused", n - 3))
                nc.scalar.activation(hid[n % 4][:, :], bank[4 + n % 4][:, :], ACT.Relu, bias=V("pt_b1")).then_inc(sig("pt_hact"), 1)
            act.wait_ge(sig("bn_ready"), at("bn_ready", 1))
            for ch in range(2):
                act.wait_ge(sig("inv_zproj"), at("inv_zproj", ch + 1))
                nc.scalar.activation(half(zr, ch), bank[2 + ch][:, :], ACT.Relu, bias=bnscale[:, 3:4],
                                     scale=bnscale[:, 2:3]).then_inc(sig("inv_zr"), 1)
            for ch in range(2):
                act.wait_ge(sig("inv_acc"), at("inv_acc", 2 * TAPS - 1 + ch))
                nc.scalar.activation(half(res, ch), bank[ch][:, :], ACT.Copy).then_inc(sig("inv_result"), 1)

        @block.vector
        def _(dve):
            def layer_norm(name):
                src, dst, sset, cb, vb, w, eps = LN[name]
                for ch in range(2):
                    dve.wait_ge(sig(f"{name}_std"), at(f"{name}_std", ch + 1))
                    nc.vector.reciprocal(half(rstd[sset], ch), half(std[sset], ch)).then_inc(sig(f"{name}_rstd"), 1)
                    dve.wait_ge(sig(f"{name}_rstd"), at(f"{name}_rstd", ch + 1))
                    nc.vector.tensor_tensor(half(xn[sset], ch), bank[cb[ch]][:, :], half(rstd[sset], ch),
                                            ALU.mult).then_inc(sig(f"{name}_xn"), 1)
                    dve.wait_ge(sig(f"{name}_xn"), at(f"{name}_xn", ch + 1))
                    nc.vector.tensor_scalar(half(dst, ch), half(xn[sset], ch), V(w + "_w"), V(w + "_b"),
                                            ALU.mult, ALU.add).then_inc(sig(f"{name}_x"), 1)

            dve.wait_ge(sig("in_vec"), at("in_vec", 16))
            nc.vector.tensor_scalar(halfgb[:, :], vec[:, VEC["tm0_gb"]:VEC["tm0_gb"] + 4], 0.5, None, ALU.mult).then_inc(sig("halfgb"), 1)
            dve.wait_ge(sig("in_rows"), at("in_rows", 32))
            nc.vector.tensor_copy(selr[:, :], selraw[:, :]).then_inc(sig("rows_ready"), 1)
            nc.vector.tensor_copy(rowhi[:, :], rowraw[:, :]).then_inc(sig("rows_hi"), 1)
            dve.wait_ge(sig("rows_hi"), at("rows_hi", 1))
            nc.vector.scalar_tensor_tensor(rows[:, :], rowhi.bitcast(F32), V("lo_row")[0:4, :], rowraw[:, :],
                                           ALU.mult, ALU.add).then_inc(sig("rows_ready"), 1)
            layer_norm("tm0_ln")
            layer_norm("tm0_lng")

            def ab_product(st):
                for u in range(8):
                    dve.wait_ge(sig(f"{st}_abtanh"), at(f"{st}_abtanh", u + 1))
                    nc.vector.scalar_tensor_tensor(
                        ab[:, u * 256:u * 256 + 256].rearrange("p (a k) -> p a k", k=C),
                        abth[:, (u % 2) * 256:(u % 2) * 256 + 256].rearrange("p (a k) -> p a k", k=C), 1.0,
                        bank[4 + u % 4][:, :].rearrange("p (a k) -> p a k", k=2 * C)[:, :, 0:C],
                        ALU.add, ALU.mult).then_inc(sig(f"{st}_ab"), 1)

            def tm_rest(st, s, g, zres, znew, others):
                for ch in range(2):
                    dve.wait_ge(sig(f"{st}_gtanh"), at(f"{st}_gtanh", ch + 1))
                    nc.vector.tensor_scalar(half(gate, ch), half(th, ch), 0.5, 0.5, ALU.mult, ALU.add).then_inc(sig(f"{st}_gate"), 1)
                for b in (1, 3):
                    dve.wait_ge(sig(f"{st}_t"), at(f"{st}_t", b + 1))
                    nc.vector.tensor_copy(tP[:, :].rearrange("m (n g c) -> m c g n", g=GB, c=C)[:, 8 * b:8 * b + 8],
                                          bank[4 + b][0:64, :].rearrange("m (c g n) -> m c g n", c=8, g=GB)).then_inc(sig(f"{st}_tP_dve"), 1)
                dve.wait_ge(sig(f"{st}_ttr"), at(f"{st}_ttr", 2))
                nc.vector.tensor_copy(sorted_cols(half(tB, 1)), raw_cols(bank[3][:, :])).then_inc(sig(f"{st}_tB_dve"), 1)
                layer_norm(f"{st}_lno")
                dve.wait_ge(sig(f"{st}_gate"), at(f"{st}_gate", 2))
                for name in others:
                    dve.wait_ge(sig(name), at(name, 1))
                for ch in range(2):
                    dve.wait_ge(sig(f"{st}_zo"), at(f"{st}_zo", ch + 1))
                    nc.vector.scalar_tensor_tensor(half(upd, ch), bank[6 + ch][:, :], V(f"{st}_zb"), half(g, ch),
                                                   ALU.add, ALU.mult).then_inc(sig(f"{st}_upd"), 1)
                    dve.wait_ge(sig(f"{st}_upd"), at(f"{st}_upd", ch + 1))
                    nc.vector.tensor_tensor(half(znew, ch), half(upd, ch), half(zres, ch), ALU.add).then_inc(sig(f"{st}_z"), 1)

            ab_product("tm0")
            tm_rest("tm0", 0, gate, z0T, z1T, ())
            layer_norm("tm1_ln")
            ab_product("tm1")
            dve.wait_ge(sig("in_const"), at("in_const", 16))
            nc.vector.tensor_copy(pairr[:, :], K("pair")).then_inc(sig("pair_ready"), 1)
            for s in range(2):
                dve.wait_ge(sig("qk_product"), at("qk_product", s + 1))
                nc.vector.tensor_tensor(wyh[:, s * 512:(s + 1) * 512].rearrange("p (h m) -> p h m", h=H),
                                        bank[s][:, :].rearrange("p (h m) -> p h m", h=H),
                                        K("bdscale").unsqueeze(1).broadcast_to([128, H, 128]), ALU.mult).then_inc(sig("wyh_ready"), 1)
            dve.wait_ge(sig("in_taw"), at("in_taw", 16))
            for s in range(2):
                nc.vector.tensor_scalar(wohalf[:, s * C:(s + 1) * C], taw[:, s * 688 + 656:s * 688 + 688], 0.5, None,
                                        ALU.mult).then_inc(sig("wo_ready"), 1)
            dve.wait_ge(sig("bn_std"), at("bn_std", 1))
            nc.vector.reciprocal(bnscale[:, 1:2], bnscale[:, 0:1]).then_inc(sig("bn_a"), 1)
            dve.wait_ge(sig("bn_a"), at("bn_a", 1))
            nc.vector.tensor_tensor(bnscale[:, 2:3], bnscale[:, 1:2], V("bn_gamma"), ALU.mult).then_inc(sig("bn_b"), 1)
            nc.vector.tensor_tensor(bnscale[:, 0:1], V("bn_b1"), V("bn_mean"), ALU.subtract).then_inc(sig("bn_b"), 1)
            dve.wait_ge(sig("bn_b"), at("bn_b", 2))
            nc.vector.scalar_tensor_tensor(bnscale[:, 3:4], bnscale[:, 0:1], bnscale[:, 2:3], V("bn_beta"),
                                           ALU.mult, ALU.add).then_inc(sig("bn_ready"), 1)
            dve.wait_ge(sig("in_ivw2"), at("in_ivw2", 16))
            nc.vector.tensor_copy(w2hi, ivw2raw).then_inc(sig("w2_hi"), 1)
            dve.wait_ge(sig("w2_hi"), at("w2_hi", 1))
            nc.vector.scalar_tensor_tensor(w2s[:, :], w2hi.bitcast(F32), V("lo_w"), ivw2raw,
                                           ALU.mult, ALU.add).then_inc(sig("w2_ready"), 1)
            tm_rest("tm1", 1, gateR, z1R, z2R, ("z1_settled", "gate1_settled"))

            def attention(st, s, zres, znew, others):
                layer_norm(f"{st}_ln")
                dve.wait_ge(sig(f"{st}_ln_x"), at(f"{st}_ln_x", 2))
                xb = xbd[:, :].rearrange("p (r a q) -> p r a q", a=2, q=N)
                for g2 in range(2):
                    nc.vector.tensor_scalar(xb[:, :, g2, :], rows8(x[:, :]), V(f"mask_g{g2}"), None,
                                            ALU.mult).then_inc(sig(f"{st}_xbd"), 1)
                for m, (kind, n) in enumerate(PROJ):
                    if kind == "v" and n == 0:
                        dve.wait_ge(sig(f"{st}_braw"), at(f"{st}_braw", 32))
                        nc.vector.tensor_copy(bhi[:, :], braw[:, :]).then_inc(sig(f"{st}_bhi"), 1)
                        dve.wait_ge(sig(f"{st}_bhi"), at(f"{st}_bhi", 1))
                        for rep in range(2):
                            nc.vector.scalar_tensor_tensor(bst[:, rep * H * N:(rep + 1) * H * N], bhi[:, :].bitcast(F32),
                                                           V("lo_pair"), braw[:, :], ALU.mult, ALU.add).then_inc(sig(f"{st}_bst"), 1)
                    if not dve_evicts(kind, n):
                        continue
                    dve.wait_ge(sig(f"{st}_proj"), at(f"{st}_proj", m + 1))
                    src = bank[PRING[m % 6]]
                    if kind == "y":
                        op = nc.vector.tensor_copy(Y[:, (n // 2) * F:(n // 2 + 1) * F][:, (n % 2) * HALF:(n % 2 + 1) * HALF], src[:, :])
                    else:
                        v = vbd[64:128, :].rearrange("p (a h c) -> p a h c", h=2, c=C)
                        op = nc.vector.tensor_copy(v[:, 16 * n:16 * n + 16, 1, :], src[64:128, :].rearrange("p (a c) -> p a c", c=C))
                    op.then_inc(sig(f"{st}_proj_dve"), 1)
                for t in range(TILES + 3):
                    if t < TILES:
                        sc = bank[t % 3][:, :].rearrange("p (a k) -> p a k", k=N)
                        dve.wait_ge(sig(f"{st}_scores"), at(f"{st}_scores", t + 1))
                        nc.vector.tensor_reduce(mx[:, 8 * t:8 * t + 8], sc, AX_X, ALU.max).then_inc(sig(f"{st}_max"), 1)
                        dve.wait_ge(sig(f"{st}_max"), at(f"{st}_max", t + 1))
                        if t >= 3:
                            dve.wait_ge(sig(f"{st}_probs"), at(f"{st}_probs", t - 2))
                        nc.vector.tensor_tensor(E_[t % 3][:, :].rearrange("p (a k) -> p a k", k=N), sc,
                                                mx[:, 8 * t:8 * t + 8].unsqueeze(2).broadcast_to([128, 8, N]),
                                                ALU.subtract).then_inc(sig(f"{st}_shifted"), 1)
                    if 1 <= t <= TILES:
                        u = t - 1
                        dve.wait_ge(sig(f"{st}_exp"), at(f"{st}_exp", u + 1))
                        nc.vector.tensor_reduce(rsum[:, 8 * u:8 * u + 8], E_[u % 3][:, :].rearrange("p (a k) -> p a k", k=N),
                                                AX_X, ALU.add).then_inc(sig(f"{st}_sum"), 1)
                        dve.wait_ge(sig(f"{st}_sum"), at(f"{st}_sum", u + 1))
                        nc.vector.reciprocal(rinv[:, 8 * u:8 * u + 8], rsum[:, 8 * u:8 * u + 8]).then_inc(sig(f"{st}_rinv"), 1)
                    if t >= 3:
                        u = t - 3
                        gp, r = tile_of(u)
                        if u == 0:
                            dve.wait_ge(sig(f"{st}_proj_act"), at(f"{st}_proj_act", count_proj(act_evicts, len(PROJ))))
                        dve.wait_ge(sig(f"{st}_av"), at(f"{st}_av", u + 1))
                        pos = slice(r * N, (r + 2) * N)
                        pair = slice(2 * gp, 2 * gp + 2)
                        nc.vector.scalar_tensor_tensor(
                            og[:, :].rearrange("p (g f) -> p g f", g=GB)[:, pair, pos],
                            gth[:, :].rearrange("p (g f) -> p g f", g=GB)[:, pair, pos], 1.0,
                            bank[5 + u % 2][:, 0:256].rearrange("p (g f) -> p g f", g=2),
                            ALU.add, ALU.mult).then_inc(sig(f"{st}_og"), 1)
                for name in others:
                    dve.wait_ge(sig(name), at(name, 1))
                for ch in range(2):
                    dve.wait_ge(sig(f"{st}_oproj"), at(f"{st}_oproj", ch + 1))
                    nc.vector.scalar_tensor_tensor(half(znew, ch), bank[7 if ch else 2][:, :], V(f"{st}_ob"), half(zres, ch),
                                                   ALU.add, ALU.add).then_inc(sig(f"{st}_z"), 1)

            attention("ta0", 0, z2R, z3R, ())
            attention("ta1", 1, z3T, z4T, ("z3_settled",))
            layer_norm("pt_ln")
            for n in range(1, 8, 2):
                dve.wait_ge(sig("pt_hproj"), at("pt_hproj", n + 1))
                if n >= 4:
                    dve.wait_ge(sig("pt_hused"), at("pt_hused", n - 3))
                nc.vector.tensor_scalar(hid[n % 4][:, :], bank[4 + n % 4][:, :], V("pt_b1"), 0.0, ALU.add, ALU.max).then_inc(sig("pt_hdve"), 1)
            dve.wait_ge(sig("xpad_zero"), at("xpad_zero", 1))
            for ch in range(2):
                dve.wait_ge(sig("pt_hused"), at("pt_hused", 4 * ch + 4))
                nc.vector.scalar_tensor_tensor(window(ch, 0, 0), rows8(bank[ch][:, :]), V("pt_b2"), rows8(half(z4T, ch)),
                                               ALU.add, ALU.add).then_inc(sig("pt_z"), 1)
            for ch in range(2):
                dve.wait_ge(sig("inv_zr"), at("inv_zr", ch + 1))
                nc.vector.tensor_copy(half(zhi, ch), half(zr, ch)).then_inc(sig("inv_zhi"), 1)
                dve.wait_ge(sig("inv_zhi"), at("inv_zhi", ch + 1))
                nc.vector.scalar_tensor_tensor(half(zst, ch), half(zhi, ch).bitcast(F32), V("lo_z"), half(zr, ch),
                                               ALU.mult, ALU.add).then_inc(sig("inv_zst"), 1)
            for n, (p, ch) in enumerate(KERN):
                if p % KS != PAD:
                    dve.wait_ge(sig("halo"), at("halo", 32))
                elif n == 0:
                    dve.wait_ge(sig("pt_z"), at("pt_z", 2))
                dve.wait_ge(sig("inv_kern"), at("inv_kern", n + 1))
                if n >= NPROD:
                    dve.wait_ge(sig("inv_acc"), at("inv_acc", n - NPROD + 1))
                nc.vector.scalar_tensor_tensor(rows8(prod[n % NPROD][:, :]), rows8(bank[KRING[n % 6]][:, :]),
                                               vec[:, VEC["b2"] + p:VEC["b2"] + p + 1],
                                               window(ch, p % KS - PAD, p // KS - PAD),
                                               ALU.add, ALU.mult).then_inc(sig("inv_prod"), 1)

        @block.tensor
        def _(pe):
            mm = nc.tensor.matmul

            def layer_norm(name, waits):
                src, dst, sset, cb, vb, w, eps = LN[name]
                for ch in range(2):
                    for who, count in waits[ch]:
                        pe.wait_ge(sig(who), at(who, count))
                    if name == "ta1_ln":
                        rhs = received(src, ch)
                        o = bank[cb[ch]][:, :].rearrange("p (r s n) -> p r s n", s=GB, n=RB)
                    else:
                        rhs, o = half(src, ch), bank[cb[ch]][:, :]
                    mm(o, K("center"), rhs, start=True, stop=True).then_inc(sig(f"{name}_centered"), 1)
                for ch in range(2):
                    pe.wait_ge(sig(f"{name}_sq"), at(f"{name}_sq", ch + 1))
                    mm(bank[vb[ch]][:, :], K("mean"), half(sq[sset], ch), start=True, stop=True).then_inc(sig(f"{name}_var"), 1)

            pe.wait_ge(sig("in_const"), at("in_const", 16))
            layer_norm("tm0_ln", ([("in_z0R", 16)], []))
            layer_norm("tm0_lng", ([("in_z0T", 16), ("tm0_ln_xn", 1), ("tm0_ln_std", 2)], [("tm0_ln_xn", 2)]))

            def ab_projections(st, s):
                pe.wait_ge(sig("rows_ready"), at("rows_ready", 2))
                pe.wait_ge(sig("in_tmw"), at("in_tmw", 16))
                for u in range(8):
                    pe.wait_ge(sig(f"{st}_ln_x"), at(f"{st}_ln_x", 1 + u // 4))
                    if u >= 4:
                        pe.wait_ge(sig(f"{st}_ab"), at(f"{st}_ab", u - 3))
                    b = bank[4 + u % 4]
                    mm(b[:, :], selr[:, :], rows[:, s * 512:(s + 1) * 512], start=True, stop=False, skip_group_check=True)
                    for i2 in range(2):
                        for ch in range(2):
                            r = 2 * u + i2
                            last = mm(b[64 * ch:64 * ch + 64, 256 * i2:256 * i2 + 256], x[:, r * N:(r + 1) * N],
                                      tmw[:, s * 768 + 256 * ch:s * 768 + 256 * ch + 256], start=False, stop=True,
                                      skip_group_check=True)
                    last.then_inc(sig(f"{st}_abproj"), 1)

            def gate_projection(st, s, src, src_name, waits):
                for ch in range(2):
                    pe.wait_ge(sig(src_name), at(src_name, ch + 1))
                    for who, count in waits[ch]:
                        pe.wait_ge(sig(who), at(who, count))
                    mm(bank[ch][:, :], tmw[:, s * 768 + 512:s * 768 + 640], half(src, ch), start=True, stop=True).then_inc(sig(f"{st}_gproj"), 1)

            def triangle(st, lhs_kind):
                pe.wait_ge(sig(f"{st}_ab"), at(f"{st}_ab", 8))
                for c in range(C):
                    hf, cc = c // CH, c % CH
                    kept = ab[64 * hf:64 * hf + 64, :].rearrange("p (m k) -> p m k", k=C)
                    moved = ab[64 * hf:64 * hf + 64, :].rearrange("p (r g k) -> p g r k", g=GB, k=C)
                    last = mm(bank[4 + c // 8][0:64, (c % 8) * N:(c % 8 + 1) * N].rearrange("p (g r) -> p g r", g=GB),
                              kept[:, :, lhs_kind * CH + cc], moved[:, :, :, (1 - lhs_kind) * CH + cc], start=True, stop=True)
                    if c % 8 == 7:
                        last.then_inc(sig(f"{st}_t"), 1)

            def triangle_back(st, s):
                pe.wait_ge(sig(f"{st}_tP_act"), at(f"{st}_tP_act", 2))
                pe.wait_ge(sig(f"{st}_tP_dve"), at(f"{st}_tP_dve", 2))
                for n in range(RB):
                    last = nc.tensor.transpose(bank[2 + n // HB][:, (n % HB) * N:(n % HB + 1) * N],
                                               tP[:, n * 128:(n + 1) * 128], K("ident")[0:64, 0:64])
                    if n % HB == HB - 1:
                        last.then_inc(sig(f"{st}_ttr"), 1)
                layer_norm(f"{st}_lno", ([(f"{st}_tB_act", 1), (f"{st}_gtanh", 2)], [(f"{st}_tB_dve", 1)]))
                for ch in range(2):
                    pe.wait_ge(sig(f"{st}_lno_x"), at(f"{st}_lno_x", ch + 1))
                    mm(bank[6 + ch][:, :], tmw[:, s * 768 + 640:s * 768 + 768], half(y, ch), start=True, stop=True).then_inc(sig(f"{st}_zo"), 1)

            ab_projections("tm0", 0)
            gate_projection("tm0", 0, xg, "tm0_lng_x", ([("tm0_lng_xn", 1)], [("tm0_lng_xn", 2)]))
            triangle("tm0", 0)
            triangle_back("tm0", 0)
            layer_norm("tm1_ln", ([("tm0_z", 1), ("tm0_lno_xn", 1)], [("tm0_z", 2), ("tm0_lno_xn", 2)]))
            gate_projection("tm1", 1, x, "tm1_ln_x", ([("tm1_ln_xn", 1)], [("tm1_ln_xn", 2)]))
            ab_projections("tm1", 1)
            pe.wait_ge(sig("in_qk"), at("in_qk", 16))
            pe.wait_ge(sig("tm1_gtanh"), at("tm1_gtanh", 2))
            for s in range(2):
                for h in range(H):
                    q0 = s * 1024 + h * 128
                    last = mm(bank[s][:, h * 128:(h + 1) * 128], qk[:, q0:q0 + 128], qk[:, q0 + 512:q0 + 640], start=True, stop=True)
                last.then_inc(sig("qk_product"), 1)
            triangle("tm1", 1)
            pe.wait_ge(sig("wyh_ready"), at("wyh_ready", 2))
            triangle_back("tm1", 1)

            def attention(st, s, ln_waits):
                w0 = s * 688
                layer_norm(f"{st}_ln", ln_waits)
                pe.wait_ge(sig("in_taw"), at("in_taw", 16))
                for ch in range(2):
                    pe.wait_ge(sig(f"{st}_ln_x"), at(f"{st}_ln_x", ch + 1))
                    mm(bank[4 + ch][0:16, :], taw[:, w0 + 640:w0 + 656], half(x, ch), start=True, stop=True).then_inc(sig(f"{st}_bproj"), 1)
                for m, (kind, n) in enumerate(PROJ):
                    if m >= 6:
                        pe.wait_ge(sig(f"{st}_proj_act"), at(f"{st}_proj_act", count_proj(act_evicts, m - 5)))
                        pe.wait_ge(sig(f"{st}_proj_dve"), at(f"{st}_proj_dve", count_proj(dve_evicts, m - 5)))
                    b = bank[PRING[m % 6]]
                    if kind == "y":
                        h, ch = n // 2, n % 2
                        last = mm(b[:, :], wyh[:, s * 512 + h * 128:s * 512 + (h + 1) * 128], half(x, ch), start=True, stop=True)
                    elif kind == "v":
                        for i2 in range(2):
                            r = 2 * n + i2
                            for h2 in range(2):
                                last = mm(b[64 * h2:64 * h2 + 64, 256 * i2:256 * i2 + 256], x[:, r * N:(r + 1) * N],
                                          taw[:, w0 + 256 * h2:w0 + 256 * h2 + 256], start=True, stop=True, skip_group_check=True)
                    else:
                        g, ch = n // 2, n % 2
                        last = mm(b[:, :], taw[C * g:C * g + C, w0 + 512:w0 + 640], half(x, ch)[C * g:C * g + C, :],
                                  start=True, stop=True)
                    last.then_inc(sig(f"{st}_proj"), 1)
                pe.wait_ge(sig(f"{st}_proj_act"), at(f"{st}_proj_act", count_proj(act_evicts, len(PROJ))))
                pe.wait_ge(sig(f"{st}_proj_dve"), at(f"{st}_proj_dve", count_proj(dve_evicts, len(PROJ))))
                pe.wait_ge(sig(f"{st}_xbd"), at(f"{st}_xbd", 2))
                pe.wait_ge(sig(f"{st}_bst"), at(f"{st}_bst", 2))
                pe.wait_ge(sig("pair_ready"), at("pair_ready", 1))
                pe.wait_ge(sig(f"{st}_brow"), at(f"{st}_brow", 2))
                for t in range(TILES + 3):
                    if t < TILES:
                        gp, r0 = tile_of(t)
                        if t >= 3:
                            pe.wait_ge(sig(f"{st}_shifted"), at(f"{st}_shifted", t - 2))
                        b = bank[t % 3]
                        mm(b[:, :], pairr[:, :], bst[:, :], start=True, stop=False, skip_group_check=True)
                        for i2 in range(2):
                            r = r0 + i2
                            last = mm(b[:, 256 * i2:256 * i2 + 256].rearrange("p (h k) -> p h k", h=H),
                                      xbd[64 * gp:64 * gp + 64, r * 128:(r + 1) * 128],
                                      Y[64 * gp:64 * gp + 64, :].rearrange("p (h f) -> p h f", h=H)[:, :, r * N:(r + 1) * N],
                                      start=False, stop=True, skip_group_check=True)
                        last.then_inc(sig(f"{st}_scores"), 1)
                    if 2 <= t < TILES + 2:
                        u = t - 2
                        pe.wait_ge(sig(f"{st}_probs"), at(f"{st}_probs", u + 1))
                        if u >= 2:
                            pe.wait_ge(sig(f"{st}_PT"), at(f"{st}_PT", u - 1))
                        for k in range(4):
                            last = nc.tensor.transpose(bank[3 + u % 2][:, 128 * k:128 * k + 128],
                                                       PN[u % 2][:, 128 * k:128 * k + 128], K("ident"))
                        last.then_inc(sig(f"{st}_ptrans"), 1)
                    if t >= 3:
                        u = t - 3
                        gp, r0 = tile_of(u)
                        pe.wait_ge(sig(f"{st}_PT"), at(f"{st}_PT", u + 1))
                        if u >= 2:
                            pe.wait_ge(sig(f"{st}_og"), at(f"{st}_og", u - 1))
                        for i2 in range(2):
                            for g2 in range(2):
                                for hp in range(2):
                                    v0 = (((r0 + i2) * GB + 2 * gp + g2) * 2 + hp) * 64
                                    p0 = (i2 * 2 + hp) * 128 + g2 * 64
                                    o0 = (g2 * 2 + i2) * 64
                                    last = mm(bank[5 + u % 2][64 * hp:64 * hp + 64, o0:o0 + 64], vbd[:, v0:v0 + 64],
                                              PT[u % 2][:, p0:p0 + 64], start=True, stop=True, skip_group_check=True)
                        last.then_inc(sig(f"{st}_av"), 1)
                pe.wait_ge(sig("wo_ready"), at("wo_ready", 2))
                pe.wait_ge(sig(f"{st}_og"), at(f"{st}_og", TILES))
                for ch in range(2):
                    for g in range(GB):
                        last = mm(bank[7 if ch else 2][C * g:C * g + C, :], wohalf[:, s * C:(s + 1) * C],
                                  og[:, g * F + ch * HALF:g * F + (ch + 1) * HALF], start=True, stop=True, skip_group_check=True)
                    last.then_inc(sig(f"{st}_oproj"), 1)

            attention("ta0", 0, ([("tm1_z", 1), ("tm1_lno_xn", 1)], [("tm1_z", 2), ("tm1_lno_xn", 2)]))
            attention("ta1", 1, ([("z3_arrived", 16 * GB), ("ta0_z", 2)], []))
            layer_norm("pt_ln", ([("ta1_z", 1)], [("ta1_z", 2)]))
            pe.wait_ge(sig("in_ptw"), at("in_ptw", 16))
            pe.wait_ge(sig("pt_ln_xn"), at("pt_ln_xn", 2))
            for n in range(9):
                if n < 8:
                    ch, g = n // 4, n % 4
                    pe.wait_ge(sig("pt_ln_x"), at("pt_ln_x", ch + 1))
                    if n >= 4:
                        pe.wait_ge(sig("pt_hact"), at("pt_hact", (n - 4) // 2 + 1))
                        pe.wait_ge(sig("pt_hdve"), at("pt_hdve", (n - 3) // 2))
                    mm(bank[4 + n % 4][:, :], ptw[C * g:C * g + C, 0:128], half(x, ch)[C * g:C * g + C, :],
                       start=True, stop=True).then_inc(sig("pt_hproj"), 1)
                if n >= 1:
                    u = n - 1
                    ch, g = u // 4, u % 4
                    pe.wait_ge(sig("pt_hdve" if u % 2 else "pt_hact"), at("pt_hdve" if u % 2 else "pt_hact", u // 2 + 1))
                    mm(bank[ch][C * g:C * g + C, :], ptw[:, 128:160], hid[u % 4][:, :], start=True, stop=True,
                       skip_group_check=True).then_inc(sig("pt_hused"), 1)
            pe.wait_ge(sig("in_ivw1"), at("in_ivw1", 16))
            for ch in range(2):
                pe.wait_ge(sig("pt_z"), at("pt_z", ch + 1))
                mm(rows8(bank[2 + ch][:, :]), ivw1[:, :], window(ch, 0, 0), start=True, stop=True).then_inc(sig("inv_zproj"), 1)
            pe.wait_ge(sig("w2_ready"), at("w2_ready", 1))
            LAG = 4
            for n in range(len(KERN) + LAG):
                if n < len(KERN):
                    p, ch = KERN[n]
                    pe.wait_ge(sig("inv_zst"), at("inv_zst", ch + 1))
                    if n < 2:
                        pe.wait_ge(sig("inv_zr"), at("inv_zr", 2))
                    if n >= 6:
                        pe.wait_ge(sig("inv_prod"), at("inv_prod", n - 5))
                    mm(bank[KRING[n % 6]][:, :], w2s[:, p * 128:(p + 1) * 128], half(zst, ch), start=True, stop=True).then_inc(sig("inv_kern"), 1)
                if n >= LAG:
                    u = n - LAG
                    pe.wait_ge(sig("inv_prod"), at("inv_prod", u + 1))
                    mm(bank[u % 2][:, :], K("ident"), prod[u % NPROD][:, :], start=(u < 2), stop=(u >= len(KERN) - 2)).then_inc(sig("inv_acc"), 1)


def kernel(**inputs):
    import numpy as np
    import concourse.bacc as bacc
    from concourse.bass_utils import run_bass_kernel_spmd

    a = {k.replace("L0_conv_", "").replace("L1_conv_", "inv_"): np.asarray(v) for k, v in inputs.items()}
    f4 = a["x"].dtype

    def blocked(m):
        return np.ascontiguousarray(m.reshape(GB, RB, N, C).transpose(0, 3, 1, 2).reshape(128, F))

    def diag(w):
        o = np.zeros((GB, C, GB, w.shape[1]), f4)
        for g in range(GB):
            o[g, :, g] = w
        return o.reshape(128, -1)

    def rep(v):
        return np.tile(v, (GB,) + (1,) * (v.ndim - 1))

    z = a["x"][0]
    vecs = np.zeros((128, NVEC), f4)

    def put(name, v):
        vecs[:, VEC[name]] = v

    def zparts(v):
        return np.tile(v, 128 // G8)

    p = np.arange(128)
    for s in range(2):
        put(f"tm{s}_lnin_w", rep(a["tm_ln_in_w"][s])); put(f"tm{s}_lnin_b", rep(a["tm_ln_in_b"][s]))
        put(f"tm{s}_lnout_w", rep(a["tm_lnout_w"][s])); put(f"tm{s}_lnout_b", rep(a["tm_lnout_b"][s]))
        put(f"tm{s}_zb", rep(a["tm_zo_b"][s])); put(f"tm{s}_gb", rep(a["tm_g_b"][s]))
        put(f"ta{s}_ln_w", rep(a["ta_ln_w"][s])); put(f"ta{s}_ln_b", rep(a["ta_ln_b"][s]))
        put(f"ta{s}_ob", rep(a["ta_o_b"][s])); put(f"ta{s}_gb", a["ta_g_b"][s])
    put("pt_w", rep(a["pt_ln_w"])); put("pt_b", rep(a["pt_ln_b"]))
    put("pt_b1", a["pt_1_b"]); put("pt_b2", rep(a["pt_2_b"]))
    for n, k in (("bn_b1", "inv_b1"), ("bn_gamma", "inv_gamma"), ("bn_beta", "inv_beta"), ("bn_mean", "inv_mean"), ("bn_var", "inv_var")):
        put(n, zparts(a[k]))
    put("eps5", 1e-5); put("eps5x16", 16e-5); put("eps3", 1e-3)
    put("mask_g0", (p // C) % 2 == 0); put("mask_g1", (p // C) % 2 == 1)
    put("lo_z", -1.0 * ((p // G8) % 4 >= 2))
    put("lo_w", -1.0 * ((p // G8) % 2 == 1))
    put("lo_pair", -1.0 * (p >= N))
    put("lo_row", -1.0 * (p % 2 == 1))
    vecs[:, VEC["b2"]:VEC["b2"] + TAPS] = np.tile(a["inv_b2"].reshape(TAPS, G8).T, (128 // G8, 1))

    eye = np.eye(128, dtype=f4)
    mean = diag(np.full((C, C), 1.0 / C, f4))
    pair = (p[:, None] % N == p[None, :] % N).astype(f4)
    bdscale = diag(np.full((C, C), 1.0 / np.sqrt(C), f4))
    consts = np.concatenate([{"ident": eye, "center": eye - mean, "mean": mean, "bdscale": bdscale, "pair": pair}[k] for k in CONST], 1)
    selrow = (np.arange(4)[:, None] // 2 == p[None, :] // N).astype(f4)

    tm_w, tm_rows = [], []
    for s in range(2):
        for ch in range(2):
            cs = slice(CH * ch, CH * ch + CH)
            tm_w.append(diag(np.concatenate([a[f"tm_{k}_w"][s][:, cs] for k in ("ap", "bp", "ag", "bg")], 1)))
        tm_w += [diag(a["tm_g_w"][s]), diag(a["tm_zo_w"][s])]
        row = [np.tile(np.concatenate([a[f"tm_{k}_b"][s][CH * ch:CH * ch + CH] for k in ("ap", "bp", "ag", "bg")]), 2 * GB) for ch in range(2)]
        tm_rows.append(np.stack([row[0], row[0], row[1], row[1]]))
    ta_w, ta_qk = [], []
    for s in range(2):
        v = a["ta_v_w"][s].reshape(C, 2, 2, C)
        for h2 in range(2):
            ta_w.append(diag(v[:, :, h2].reshape(C, 2 * C)))
        pair_w = diag(a["ta_b_w"][s]).reshape(128, GB, H).transpose(0, 2, 1).reshape(128, GB * H)
        ta_w += [rep(a["ta_g_w"][s]), pair_w, a["ta_o_w"][s]]
        for k in ("ta_k_w", "ta_q_w"):
            w = a[k][s].reshape(C, H, C).transpose(2, 1, 0)
            ta_qk.append(np.tile(w[:, :, None, :], (1, 1, GB, 1)).reshape(C, H * 128))
    w2 = a["inv_w2"].reshape(G8, TAPS, G8)
    w2s = np.zeros((GB, 4, G8, TAPS, GB, 4, G8), f4)
    for g in range(GB):
        w2s[g, :, :, :, g] = w2[None, :, :, None, :]
    w1s = np.zeros((GB, C, GB, 4, G8), f4)
    for g in range(GB):
        w1s[g, :, g] = a["inv_w1"][:, None, :]

    arrays = {
        "z_rows": blocked(z), "z_cols": blocked(z.transpose(1, 0, 2)), "vecs": vecs, "consts": consts, "selrow": selrow,
        "tm_w": np.concatenate(tm_w, 1), "tm_rows": np.concatenate(tm_rows, 1),
        "ta_w": np.concatenate(ta_w, 1), "ta_qk": np.concatenate(ta_qk, 1),
        "pt_w": np.concatenate([rep(a["pt_1_w"]), a["pt_2_w"]], 1),
        "inv_w1": w1s.reshape(128, 128), "inv_w2": w2s.reshape(128, TAPS * 128),
    }
    nc = bacc.Bacc("TRN2", target_bir_lowering=False, num_devices=1)
    args = []
    for name, v in arrays.items():
        arrays[name] = np.ascontiguousarray(v)
        args.append(nc.dram_tensor(name, v.shape, F32, kind="ExternalInput").ap())
    args.append(nc.dram_tensor("result", (128, F), F32, kind="ExternalOutput").ap())
    build_program(nc, *args)
    r = run_bass_kernel_spmd(nc, [arrays], core_ids=[0]).results[0]["result"]
    return np.ascontiguousarray(r.reshape(GB, C, RB, N).transpose(3, 0, 2, 1).reshape(1, N, N, C))
```

```python
from contextlib import ExitStack

import concourse.bass as bass
from concourse import mybir

ALU = mybir.AluOpType
ACT = mybir.ActivationFunctionType
F32 = mybir.dt.float32
F32R = mybir.dt.float32r
AX_X = mybir.AxisListType.X

N = 64
C = 32
GB = 128 // C
RB = N // GB
F = RB * N
HALF = F // 2
HB = RB // 2
H = 4
CH = C // 2
TAPS = 25
KS = 5
PAD = KS // 2
G8 = 8
PW = N + 2 * PAD
PH = RB + 2 * PAD

VEC = {}
for _s in range(2):
    for _n in ("lnin_w", "lnin_b", "lnout_w", "lnout_b", "zb"):
        VEC[f"tm{_s}_{_n}"] = len(VEC)
    for _n in ("ln_w", "ln_b", "ob"):
        VEC[f"ta{_s}_{_n}"] = len(VEC)
for _n in ("pt_w", "pt_b", "pt_b1", "pt_b2", "bn_b1", "bn_gamma", "bn_beta", "bn_mean", "bn_var",
           "tm0_gb", "tm1_gb", "ta0_gb", "ta1_gb",
           "eps5", "eps5x16", "eps3", "mask_g0", "mask_g1", "lo_z", "lo_w", "lo_pair", "lo_row"):
    VEC[_n] = len(VEC)
VEC["b2"] = len(VEC)
NVEC = VEC["b2"] + TAPS

CONST = ("ident", "center", "mean", "bdscale", "pair")


def build_program(nc, z_rows, z_cols, vecs, consts, selrow, tm_w, tm_rows, ta_w, ta_qk, pt_w, inv_w1, inv_w2, out):
    with ExitStack() as ctx:
        def sb(name, cols, dt=F32, parts=128):
            return ctx.enter_context(nc.sbuf_tensor(name, [parts, cols], dt))

        signals = {}
        NORMS = ("tm0_ln", "tm0_lng", "tm0_lno", "tm1_ln", "tm1_lno", "ta0_ln", "ta1_ln", "pt_ln")
        RAISES = {"abproj": 8, "abtanh": 8, "ab": 8, "t": 4, "tB_act": 1, "tB_dve": 1, "bhi": 1, "braw": 32, "bias_hop": 16,
                  "yproj": 8, "y_act": 4, "y_dve": 4, "fill": 16, "fill_act": 16}
        RAISES.update({k: 16 for k in ("scores", "max", "shifted", "exp", "sum", "rinv", "probs", "ptrans", "PT", "av", "og")})

        def shared(name):
            for norm in NORMS:
                if name.startswith(norm + "_"):
                    return "ln_" + name[len(norm) + 1:], 2 * NORMS.index(norm)
            for kind in ("tm", "ta"):
                if name[:2] == kind and name[2] in "01" and name[3] == "_":
                    return kind + name[3:], int(name[2]) * RAISES.get(name[4:], 2)
            return name, 0

        def sig(name):
            name = shared(name)[0]
            if name not in signals:
                signals[name] = ctx.enter_context(nc.semaphore(name))
            return signals[name]

        def at(name, count):
            return shared(name)[1] + count

        psum = ctx.enter_context(nc.psum_tensor("psum", [128, 8 * HALF], F32))
        bank = [psum[:, i * HALF:(i + 1) * HALF] for i in range(8)]

        z0R = sb("z0R", F)
        z0T = sb("z0T", F)
        vec = sb("vec", NVEC)
        cst = sb("cst", 128 * len(CONST))
        selraw = sb("selraw", 128, parts=2)
        tmw = sb("tmw", 2 * 768)
        taw = sb("taw", 2 * 688)
        ptw = sb("ptw", 160)
        ivw1 = sb("ivw1", 128)

        def V(name):
            return vec[:, VEC[name]:VEC[name] + 1]

        def K(name):
            i = CONST.index(name)
            return cst[:, 128 * i:128 * i + 128]

        halfgb = sb("halfgb", 4)
        selr = sb("selr", 128, F32R, parts=2)
        rows = sb("rows", 2 * 512, F32R, parts=2)
        pairr = sb("pairr", 128, F32R)
        wyh = sb("wyh", 2 * H * 128)
        wohalf = sb("wohalf", 2 * C)
        bnscale = sb("bnscale", 4)
        w2s = sb("w2s", TAPS * 128, F32R)

        Y = sb("Y", H * F)
        xbd = sb("xbd", RB * 128)
        vbd = sb("vbd", RB * GB * 2 * 64)
        gth = sb("gth", GB * F)
        og = sb("og", GB * F)
        braw = sb("braw", H * N)
        bhi = sb("bhi", H * N, F32R)
        bst = sb("bst", 2 * H * N, F32R)
        mx = sb("mx", 16 * 8)
        rsum = sb("rsum", 16 * 8)
        rinv = sb("rinv", 16 * 8)
        NE = 4
        soft = sb("soft", 8 * HALF)
        E_ = [soft[:, i * HALF:(i + 1) * HALF] for i in range(NE)]
        PN = [soft[:, i * HALF:(i + 1) * HALF] for i in (4, 5)]
        PT = [soft[:, i * HALF:(i + 1) * HALF] for i in (6, 7)]

        sq = [sb("sq", F), Y[:, 0:F]]
        logv = [sb("logv", F), Y[:, F:2 * F]]
        rstd = [sb("rstd", F), Y[:, 2 * F:3 * F]]
        xn = [sb("xn", F), Y[:, 3 * F:4 * F]]

        x = sb("x", F)
        y = sb("y", F)
        gate = sb("gate", F)
        gateR = sb("gateR", F)
        th = sb("th", F)
        xg = gateR
        abth = soft[:, 4 * HALF:5 * HALF]
        ab = xbd
        tP = og[0:64, 0:2 * F]
        tB = og[:, 2 * F:3 * F]
        upd = og[:, 3 * F:4 * F]
        brow = y[0:16, :]
        z1T = sb("z1T", F)
        z1R = sb("z1R", F)
        z2R = sb("z2R", F)
        z2T, z4T, z3T = z0R, z0T, z1R
        perm = [vbd[:, 0:F], vbd[:, F:2 * F], gate]
        arrive = [vbd[:, 2 * F:3 * F], vbd[:, 3 * F:4 * F], z1T]

        qk = soft[0:32, 0:2 * 2 * H * 128]
        rowraw = gate[0:2, :]
        rowhi = th[0:2, :].bitcast(F32R)
        ivw2raw = gth[:, 0:TAPS * 128]
        w2hi = Y[:, 0:TAPS * 128].bitcast(F32R)

        hid = [og[:, i * HALF:(i + 1) * HALF] for i in range(4)]
        xpad = soft[:, 0:PH * PW]
        zr = og[:, 2 * F:3 * F]
        zhi = og[:, 3 * F:4 * F].bitcast(F32R)
        zst = sb("zst", F, F32R)
        NPROD, NSUM = 6, 3
        prod = [gth[:, i * F:(i + 1) * F] for i in range(4)] + [vbd[:, i * F:(i + 1) * F] for i in range(2)]
        psums = [vbd[:, i * F:(i + 1) * F] for i in range(2, 2 + NSUM)]
        res = Y[:, 0:F]

        hop = [nc.dram_tensor(f"hop{i}", (128, F), F32, kind="Internal").ap() for i in range(3)]
        bias_hop = [nc.dram_tensor(f"bias_hop{i}", (GB * H, F), F32, kind="Internal").ap() for i in range(2)]

        def half(buf, ch):
            return buf[:, ch * HALF:(ch + 1) * HALF]

        def raw_cols(ap):
            return ap.rearrange("p (n r g) -> p n g r", n=HB, g=GB)

        def sorted_cols(ap):
            return ap.rearrange("p (n g r) -> p n g r", n=HB, g=GB)

        xpad_v = xpad[:, :].rearrange("p (a b) -> p a b", b=PW)

        def window(ch, dr, dn):
            r0 = PAD + HB * ch + dr
            return xpad_v[:, r0:r0 + HB, PAD + dn:PAD + dn + N]

        def rows8(ap):
            return ap.rearrange("p (a b) -> p a b", b=N)

        TILES = 16
        LAG_P, LAG_A = 3, 4

        def tile_of(t):
            return t // 8, 2 * (t % 8)

        YRING = (0, 1, 2, 3, 6, 7)
        FILL_STEPS = (("v0", "g0"), ("v1", "g2"), ("v2",), ("v3", "g1"), ("v4", "g3"), ("v5",), ("v6", "g4"), ("v7", "g6"),
                      ("g5",), ("g7",))
        FILL = [k for step in FILL_STEPS for k in step]

        def filled(kind):
            return FILL.index(kind) + 1

        TAP_ORDER = sorted(range(TAPS), key=lambda p: (p % KS != PAD, p))
        PAIRS = 11
        SUMS = [(2 * i, 2 * i + 1) for i in range(PAIRS)] + [(i,) for i in range(2 * PAIRS, TAPS)]

        def kern_banks(i):
            return psum[:, (2 + 2 * (i % 3)) * HALF:(4 + 2 * (i % 3)) * HALF]

        LN = {
            "tm0_ln": (z0R, x, 0, (0, 1), (2, 3), "tm0_lnin", "eps5"),
            "tm0_lng": (z0T, xg, 1, (0, 1), (2, 3), "tm0_lnin", "eps5"),
            "tm0_lno": (tB, y, 0, (0, 1), (4, 5), "tm0_lnout", "eps5x16"),
            "tm1_ln": (z1T, x, 0, (0, 1), (2, 3), "tm1_lnin", "eps5"),
            "tm1_lno": (tB, y, 0, (0, 1), (4, 5), "tm1_lnout", "eps5x16"),
            "ta0_ln": (z2R, x, 0, (0, 1), (2, 3), "ta0_ln", "eps5"),
            "ta1_ln": (z3T, x, 0, (0, 1), (2, 3), "ta1_ln", "eps5"),
            "pt_ln": (z4T, x, 0, (0, 1), (2, 3), "pt", "eps5"),
        }

        block = ctx.enter_context(nc.Block())

        @block.sync
        def _(sp):
            sp.dma_start(z0R[:, :], z_rows).then_inc(sig("in_z0R"), 16)
            sp.dma_start(cst[:, :], consts).then_inc(sig("in_const"), 16)
            sp.dma_start(vec[:, :], vecs).then_inc(sig("in_vec"), 16)
            sp.dma_start(tmw[:, :], tm_w).then_inc(sig("in_tmw"), 16)
            sp.dma_start(z0T[:, :], z_cols).then_inc(sig("in_z0T"), 16)

            def relayout(i, name):
                sp.wait_ge(sig(f"{name}_permuted"), at(f"{name}_permuted", 1))
                sp.dma_start(hop[i][:, :], perm[i][:, :]).then_inc(sig(f"{name}_hop"), 16)
                sp.wait_ge(sig(f"{name}_hop"), at(f"{name}_hop", 16))
                for g in range(GB):
                    sp.dma_start(arrive[i][g * C:(g + 1) * C, :].rearrange("c (s f) -> c s f", s=GB),
                                 hop[i][:, g * RB * RB:(g + 1) * RB * RB].rearrange("(s c) f -> c s f", s=GB),
                                 ).then_inc(sig(f"{name}_arrived"), 16)

            relayout(0, "z1")
            relayout(1, "gate1")
            relayout(2, "z2")

            def pair_bias(st, s):
                sp.wait_ge(sig(f"{st}_brow"), at(f"{st}_brow", 2))
                sp.dma_start(bias_hop[s][:, :], brow).then_inc(sig(f"{st}_bias_hop"), 16)
                sp.wait_ge(sig(f"{st}_bias_hop"), at(f"{st}_bias_hop", 16))
                for part in range(2):
                    sp.dma_start(braw[part * N:(part + 1) * N, :].rearrange("q (h k) -> q h k", h=H),
                                 bias_hop[s].rearrange("(h g) (r k) -> (g r) h k", h=H, k=N)).then_inc(sig(f"{st}_braw"), 16)

            pair_bias("ta0", 0)
            
            pair_bias("ta1", 1)
            sp.wait_ge(sig("pt_z"), at("pt_z", 2))
            sp.dma_start(xpad_v[C:128, 0:PAD, :], xpad_v[0:128 - C, RB:RB + PAD, :]).then_inc(sig("halo"), 16)
            sp.dma_start(xpad_v[0:128 - C, PAD + RB:PH, :], xpad_v[C:128, PAD:2 * PAD, :]).then_inc(sig("halo"), 16)
            for ch in range(2):
                sp.wait_ge(sig("inv_result"), at("inv_result", ch + 1))
                sp.dma_start(out[:, ch * HALF:(ch + 1) * HALF], half(res, ch)).then_inc(sig("stored"), 16)
            sp.wait_ge(sig("stored"), at("stored", 32))

        @block.gpsimd
        def _(pool):
            pool.dma_start(selraw[:, :], selrow).then_inc(sig("in_rows"), 16)
            pool.dma_start(rowraw[:, :], tm_rows).then_inc(sig("in_rows"), 16)
            pool.dma_start(qk[:, :], ta_qk).then_inc(sig("in_qk"), 16)
            pool.dma_start(taw[:, :], ta_w).then_inc(sig("in_taw"), 16)
            pool.dma_start(ptw[:, :], pt_w).then_inc(sig("in_ptw"), 16)
            pool.dma_start(ivw1[:, :], inv_w1).then_inc(sig("in_ivw1"), 16)
            pool.dma_start(ivw2raw, inv_w2).then_inc(sig("in_ivw2"), 16)

            def permute(i, name, src, ready):
                pool.wait_ge(sig(ready), at(ready, 2))
                pool.tensor_copy(perm[i][:, :].rearrange("p (g n r) -> p r g n", g=GB, n=RB),
                                 src[:, :].rearrange("p (r g n) -> p r g n", g=GB, n=RB)).then_inc(sig(f"{name}_permuted"), 1)

            def settle(i, name, dst):
                pool.wait_ge(sig(f"{name}_arrived"), at(f"{name}_arrived", 16 * GB))
                pool.tensor_copy(dst[:, :].rearrange("p (r s n) -> p r s n", s=GB, n=RB),
                                 arrive[i][:, :].rearrange("p (s r n) -> p r s n", s=GB, n=RB)).then_inc(sig(f"{name}_settled"), 1)

            permute(0, "z1", z1T, "tm0_z")
            permute(1, "gate1", gate, "tm1_gate")
            settle(0, "z1", z1R)
            settle(1, "gate1", gateR)

            pool.wait_ge(sig("z1_settled"), at("z1_settled", 1))
            pool.wait_ge(sig("gate1_settled"), at("gate1_settled", 1))
            for h2 in range(2):
                off = vbd[64 * h2:64 * h2 + 64, :].rearrange("p (a h c) -> p a h c", h=2, c=C)[:, :, 1 - h2, :]
                pool.memset(off, 0.0).then_inc(sig("vbd_zero"), 1)

            def normalise(st):
                for t in range(TILES):
                    pool.wait_ge(sig(f"{st}_rinv"), at(f"{st}_rinv", t + 1))
                    if t >= 2:
                        pool.wait_ge(sig(f"{st}_ptrans"), at(f"{st}_ptrans", t - 1))
                    pool.tensor_tensor(
                        PN[t % 2][:, :].rearrange("p (a k) -> p a k", k=N),
                        E_[t % NE][:, :].rearrange("p (a k) -> p a k", k=N),
                        rinv[:, 8 * t:8 * t + 8].unsqueeze(2).broadcast_to([128, 8, N]), ALU.mult,
                    ).then_inc(sig(f"{st}_probs"), 1)

            pool.wait_ge(sig("vbd_zero"), 2)
            permute(2, "z2", z2R, "tm1_z")
            settle(2, "z2", z2T)
            normalise("ta0")
            normalise("ta1")
            pool.wait_ge(sig("ta1_probs"), at("ta1_probs", TILES))
            pool.memset(xpad[:, :], 0.0).then_inc(sig("xpad_zero"), 1)
            for i in range(PAIRS):
                pool.wait_ge(sig("inv_prod"), 2 * i + 2)
                if i >= NSUM:
                    pool.wait_ge(sig("inv_acc"), i - NSUM + 1)
                pool.tensor_tensor(psums[i % NSUM], prod[2 * i % NPROD], prod[(2 * i + 1) % NPROD], ALU.add).then_inc(sig("inv_sum"), 1)

        @block.scalar
        def _(act):
            def layer_norm(name, then_tanh=True):
                src, dst, sset, cb, vb, w, eps = LN[name]
                nc.scalar.preload_act_table_set("natural_log_exp_and_others")
                for ch in range(2):
                    act.wait_ge(sig(f"{name}_centered"), at(f"{name}_centered", ch + 1))
                    nc.scalar.activation(half(sq[sset], ch), bank[cb[ch]][:, :], ACT.Square).then_inc(sig(f"{name}_sq"), 1)
                for ch in range(2):
                    act.wait_ge(sig(f"{name}_var"), at(f"{name}_var", ch + 1))
                    nc.scalar.activation(half(logv[sset], ch), bank[vb[ch]][:, :], ACT.Ln, bias=V(eps)).then_inc(sig(f"{name}_logv"), 1)
                for ch in range(2):
                    act.wait_ge(sig(f"{name}_logv"), at(f"{name}_logv", ch + 1))
                    nc.scalar.activation(half(rstd[sset], ch), half(logv[sset], ch), ACT.Exp, scale=-0.5).then_inc(sig(f"{name}_rstd"), 1)
                if then_tanh:
                    nc.scalar.preload_act_table_set("exp_and_others")

            act.wait_ge(sig("in_vec"), at("in_vec", 16))
            nc.scalar.activation(bnscale[:, 0:1], V("bn_var"), ACT.Sqrt, bias=V("eps3")).then_inc(sig("bn_std"), 1)
            layer_norm("tm0_ln", False)
            layer_norm("tm0_lng")

            def ab_tanh(st):
                for u in range(8):
                    act.wait_ge(sig(f"{st}_abproj"), at(f"{st}_abproj", u + 1))
                    if u >= 2:
                        act.wait_ge(sig(f"{st}_ab"), at(f"{st}_ab", u - 1))
                    nc.scalar.activation(
                        abth[:, (u % 2) * 256:(u % 2) * 256 + 256].rearrange("p (g k) -> p g k", g=GB),
                        bank[4 + u % 4].rearrange("p (g k) -> p g k", g=GB)[:, :, 2 * C:4 * C],
                        ACT.Tanh, scale=0.5).then_inc(sig(f"{st}_abtanh"), 1)

            def tm_rest(st, s):
                for ch in range(2):
                    act.wait_ge(sig(f"{st}_gproj"), at(f"{st}_gproj", ch + 1))
                    act.wait_ge(sig("halfgb"), at("halfgb", 1))
                    nc.scalar.activation(half(th, ch), bank[ch][:, :], ACT.Tanh, bias=halfgb[:, s:s + 1],
                                         scale=0.5).then_inc(sig(f"{st}_gtanh"), 1)
                for b in (0, 2):
                    act.wait_ge(sig(f"{st}_t"), at(f"{st}_t", b + 1))
                    nc.scalar.activation(tP[:, :].rearrange("m (n g c) -> m c g n", g=GB, c=C)[:, 8 * b:8 * b + 8],
                                         bank[4 + b][0:64, :].rearrange("m (c g n) -> m c g n", c=8, g=GB),
                                         ACT.Copy).then_inc(sig(f"{st}_tP_act"), 1)
                act.wait_ge(sig(f"{st}_ttr"), at(f"{st}_ttr", 1))
                nc.scalar.activation(sorted_cols(half(tB, 0)), raw_cols(bank[2][:, :]), ACT.Copy).then_inc(sig(f"{st}_tB_act"), 1)

            ab_tanh("tm0")
            tm_rest("tm0", 0)
            layer_norm("tm0_lno", False)
            layer_norm("tm1_ln")
            ab_tanh("tm1")
            tm_rest("tm1", 1)
            layer_norm("tm1_lno", False)

            def attention(st, s):
                layer_norm(f"{st}_ln")
                for ch in range(2):
                    act.wait_ge(sig(f"{st}_bproj"), at(f"{st}_bproj", ch + 1))
                    nc.scalar.activation(brow[:, ch * HALF:(ch + 1) * HALF], bank[4 + ch][0:16, :],
                                         ACT.Copy).then_inc(sig(f"{st}_brow"), 1)
                for n in range(0, 8, 2):
                    act.wait_ge(sig(f"{st}_yproj"), at(f"{st}_yproj", n + 1))
                    nc.scalar.activation(Y[:, n * HALF:(n + 1) * HALF], bank[YRING[n % 6]], ACT.Copy).then_inc(sig(f"{st}_y_act"), 1)
                act.wait_ge(sig("vbd_zero"), at("vbd_zero", 2))

                def fill(kind):
                    n = int(kind[1])
                    act.wait_ge(sig(f"{st}_fill"), at(f"{st}_fill", filled(kind)))
                    src = bank[6 + FILL.index(kind) % 2]
                    if kind[0] == "g":
                        op = nc.scalar.activation(gth[:, n * HALF:(n + 1) * HALF], src, ACT.Tanh,
                                                  bias=halfgb[:, 2 + s:3 + s], scale=0.5)
                    else:
                        for i2 in range(2):
                            for h2 in range(2):
                                r0 = (2 * n + i2) * GB * 128
                                op = nc.scalar.activation(
                                    vbd[64 * h2:64 * h2 + 64, r0:r0 + GB * 128].rearrange("p (a h c) -> p a h c", h=2, c=C)[:, :, h2, :],
                                    src[64 * i2:64 * i2 + 64, :].rearrange("p (a h c) -> p a h c", h=2, c=C)[:, :, h2, :], ACT.Copy)
                    op.then_inc(sig(f"{st}_fill_act"), 1)

                for t in range(TILES + LAG_P):
                    if t < TILES:
                        act.wait_ge(sig(f"{st}_shifted"), at(f"{st}_shifted", t + 1))
                        nc.scalar.activation(E_[t % NE], E_[t % NE], ACT.Exp).then_inc(sig(f"{st}_exp"), 1)
                    if t < len(FILL_STEPS):
                        for kind in FILL_STEPS[t]:
                            fill(kind)
                    if t >= LAG_P:
                        u = t - LAG_P
                        act.wait_ge(sig(f"{st}_ptrans"), at(f"{st}_ptrans", u + 1))
                        if u >= 2:
                            act.wait_ge(sig(f"{st}_av"), at(f"{st}_av", u - 1))
                        nc.scalar.activation(PT[u % 2], bank[2 + u % 2], ACT.Copy).then_inc(sig(f"{st}_PT"), 1)

            attention("ta0", 0)
            attention("ta1", 1)
            layer_norm("pt_ln", False)
            for n in range(0, 8, 2):
                act.wait_ge(sig("pt_hproj"), at("pt_hproj", n + 1))
                if n >= 4:
                    act.wait_ge(sig("pt_hused"), at("pt_hused", n - 3))
                nc.scalar.activation(hid[n % 4][:, :], bank[4 + n % 4][:, :], ACT.Relu, bias=V("pt_b1")).then_inc(sig("pt_hact"), 1)
            act.wait_ge(sig("bn_ready"), at("bn_ready", 1))
            for ch in range(2):
                act.wait_ge(sig("inv_zproj"), at("inv_zproj", ch + 1))
                nc.scalar.activation(half(zr, ch), bank[2 + ch][:, :], ACT.Relu, bias=bnscale[:, 3:4],
                                     scale=bnscale[:, 2:3]).then_inc(sig("inv_zr"), 1)
            for ch in range(2):
                act.wait_ge(sig("inv_acc"), len(SUMS))
                nc.scalar.activation(half(res, ch), bank[ch][:, :], ACT.Copy).then_inc(sig("inv_result"), 1)

        @block.vector
        def _(dve):
            def layer_norm(name):
                src, dst, sset, cb, vb, w, eps = LN[name]
                for ch in range(2):
                    dve.wait_ge(sig(f"{name}_rstd"), at(f"{name}_rstd", ch + 1))
                    nc.vector.tensor_tensor(half(xn[sset], ch), bank[cb[ch]][:, :], half(rstd[sset], ch),
                                            ALU.mult).then_inc(sig(f"{name}_xn"), 1)
                    dve.wait_ge(sig(f"{name}_xn"), at(f"{name}_xn", ch + 1))
                    nc.vector.tensor_scalar(half(dst, ch), half(xn[sset], ch), V(w + "_w"), V(w + "_b"),
                                            ALU.mult, ALU.add).then_inc(sig(f"{name}_x"), 1)

            dve.wait_ge(sig("in_vec"), at("in_vec", 16))
            nc.vector.tensor_scalar(halfgb[:, :], vec[:, VEC["tm0_gb"]:VEC["tm0_gb"] + 4], 0.5, None, ALU.mult).then_inc(sig("halfgb"), 1)
            dve.wait_ge(sig("in_rows"), at("in_rows", 32))
            nc.vector.tensor_copy(selr[:, :], selraw[:, :]).then_inc(sig("rows_ready"), 1)
            nc.vector.tensor_copy(rowhi[:, :], rowraw[:, :]).then_inc(sig("rows_hi"), 1)
            dve.wait_ge(sig("rows_hi"), at("rows_hi", 1))
            nc.vector.scalar_tensor_tensor(rows[:, :], rowhi.bitcast(F32), V("lo_row")[0:2, :], rowraw[:, :],
                                           ALU.mult, ALU.add).then_inc(sig("rows_ready"), 1)
            layer_norm("tm0_ln")
            layer_norm("tm0_lng")

            def ab_product(st):
                for u in range(8):
                    dve.wait_ge(sig(f"{st}_abtanh"), at(f"{st}_abtanh", u + 1))
                    for i2 in range(2):
                        for ch in range(2):
                            src = slice(64 * i2, 64 * i2 + 64)
                            last = nc.vector.scalar_tensor_tensor(
                                ab[64 * ch:64 * ch + 64, (2 * u + i2) * 128:(2 * u + i2 + 1) * 128].rearrange("p (g k) -> p g k", g=GB),
                                abth[src, (u % 2) * 256:(u % 2) * 256 + 256].rearrange("p (g k) -> p g k", g=GB)[:, :, C * ch:C * ch + C], 1.0,
                                bank[4 + u % 4][src, :].rearrange("p (g k) -> p g k", g=GB)[:, :, C * ch:C * ch + C],
                                ALU.add, ALU.mult)
                    last.then_inc(sig(f"{st}_ab"), 1)

            def tm_rest(st, s, g, zres, znew, others):
                for ch in range(2):
                    dve.wait_ge(sig(f"{st}_gtanh"), at(f"{st}_gtanh", ch + 1))
                    nc.vector.tensor_scalar(half(gate, ch), half(th, ch), 0.5, 0.5, ALU.mult, ALU.add).then_inc(sig(f"{st}_gate"), 1)
                for b in (1, 3):
                    dve.wait_ge(sig(f"{st}_t"), at(f"{st}_t", b + 1))
                    nc.vector.tensor_copy(tP[:, :].rearrange("m (n g c) -> m c g n", g=GB, c=C)[:, 8 * b:8 * b + 8],
                                          bank[4 + b][0:64, :].rearrange("m (c g n) -> m c g n", c=8, g=GB)).then_inc(sig(f"{st}_tP_dve"), 1)
                dve.wait_ge(sig(f"{st}_ttr"), at(f"{st}_ttr", 2))
                nc.vector.tensor_copy(sorted_cols(half(tB, 1)), raw_cols(bank[3][:, :])).then_inc(sig(f"{st}_tB_dve"), 1)
                layer_norm(f"{st}_lno")
                dve.wait_ge(sig(f"{st}_gate"), at(f"{st}_gate", 2))
                for name in others:
                    dve.wait_ge(sig(name), at(name, 1))
                for ch in range(2):
                    dve.wait_ge(sig(f"{st}_zo"), at(f"{st}_zo", ch + 1))
                    nc.vector.scalar_tensor_tensor(half(upd, ch), bank[6 + ch][:, :], V(f"{st}_zb"), half(g, ch),
                                                   ALU.add, ALU.mult).then_inc(sig(f"{st}_upd"), 1)
                    dve.wait_ge(sig(f"{st}_upd"), at(f"{st}_upd", ch + 1))
                    nc.vector.tensor_tensor(half(znew, ch), half(upd, ch), half(zres, ch), ALU.add).then_inc(sig(f"{st}_z"), 1)

            ab_product("tm0")
            tm_rest("tm0", 0, gate, z0T, z1T, ())
            layer_norm("tm1_ln")
            ab_product("tm1")
            dve.wait_ge(sig("in_const"), at("in_const", 16))
            nc.vector.tensor_copy(pairr[:, :], K("pair")).then_inc(sig("pair_ready"), 1)
            for s in range(2):
                dve.wait_ge(sig("qk_product"), at("qk_product", s + 1))
                nc.vector.tensor_tensor(wyh[:, s * 512:(s + 1) * 512].rearrange("p (h m) -> p h m", h=H),
                                        bank[s][:, :].rearrange("p (h m) -> p h m", h=H),
                                        K("bdscale").unsqueeze(1).broadcast_to([128, H, 128]), ALU.mult).then_inc(sig("wyh_ready"), 1)
            dve.wait_ge(sig("in_taw"), at("in_taw", 16))
            for s in range(2):
                nc.vector.tensor_scalar(wohalf[:, s * C:(s + 1) * C], taw[:, s * 688 + 656:s * 688 + 688], 0.5, None,
                                        ALU.mult).then_inc(sig("wo_ready"), 1)
            dve.wait_ge(sig("bn_std"), at("bn_std", 1))
            nc.vector.reciprocal(bnscale[:, 1:2], bnscale[:, 0:1]).then_inc(sig("bn_a"), 1)
            dve.wait_ge(sig("bn_a"), at("bn_a", 1))
            nc.vector.tensor_tensor(bnscale[:, 2:3], bnscale[:, 1:2], V("bn_gamma"), ALU.mult).then_inc(sig("bn_b"), 1)
            nc.vector.tensor_tensor(bnscale[:, 0:1], V("bn_b1"), V("bn_mean"), ALU.subtract).then_inc(sig("bn_b"), 1)
            dve.wait_ge(sig("bn_b"), at("bn_b", 2))
            nc.vector.scalar_tensor_tensor(bnscale[:, 3:4], bnscale[:, 0:1], bnscale[:, 2:3], V("bn_beta"),
                                           ALU.mult, ALU.add).then_inc(sig("bn_ready"), 1)
            dve.wait_ge(sig("in_ivw2"), at("in_ivw2", 16))
            nc.vector.tensor_copy(w2hi, ivw2raw).then_inc(sig("w2_hi"), 1)
            dve.wait_ge(sig("w2_hi"), at("w2_hi", 1))
            nc.vector.scalar_tensor_tensor(w2s[:, :], w2hi.bitcast(F32), V("lo_w"), ivw2raw,
                                           ALU.mult, ALU.add).then_inc(sig("w2_ready"), 1)
            tm_rest("tm1", 1, gateR, z1R, z2R, ("z1_settled", "gate1_settled"))

            def attention(st, s, zres, znew, others):
                layer_norm(f"{st}_ln")
                dve.wait_ge(sig(f"{st}_ln_x"), at(f"{st}_ln_x", 2))
                xb = xbd[:, :].rearrange("p (r a q) -> p r a q", a=2, q=N)
                for g2 in range(2):
                    nc.vector.tensor_scalar(xb[:, :, g2, :], rows8(x[:, :]), V(f"mask_g{g2}"), None,
                                            ALU.mult).then_inc(sig(f"{st}_xbd"), 1)
                for n in range(1, 8, 2):
                    dve.wait_ge(sig(f"{st}_yproj"), at(f"{st}_yproj", n + 1))
                    nc.vector.tensor_copy(Y[:, n * HALF:(n + 1) * HALF], bank[YRING[n % 6]]).then_inc(sig(f"{st}_y_dve"), 1)
                dve.wait_ge(sig(f"{st}_braw"), at(f"{st}_braw", 32))
                nc.vector.tensor_copy(bhi[:, :], braw[:, :]).then_inc(sig(f"{st}_bhi"), 1)
                dve.wait_ge(sig(f"{st}_bhi"), at(f"{st}_bhi", 1))
                for again in range(2):
                    nc.vector.scalar_tensor_tensor(bst[:, again * H * N:(again + 1) * H * N], bhi[:, :].bitcast(F32),
                                                   V("lo_pair"), braw[:, :], ALU.mult, ALU.add).then_inc(sig(f"{st}_bst"), 1)
                for t in range(TILES + LAG_A):
                    if t < TILES:
                        sc = bank[t % 2].rearrange("p (a k) -> p a k", k=N)
                        dve.wait_ge(sig(f"{st}_scores"), at(f"{st}_scores", t + 1))
                        nc.vector.tensor_reduce(mx[:, 8 * t:8 * t + 8], sc, AX_X, ALU.max).then_inc(sig(f"{st}_max"), 1)
                        dve.wait_ge(sig(f"{st}_max"), at(f"{st}_max", t + 1))
                        if t >= NE:
                            dve.wait_ge(sig(f"{st}_probs"), at(f"{st}_probs", t - NE + 1))
                        nc.vector.tensor_tensor(E_[t % NE].rearrange("p (a k) -> p a k", k=N), sc,
                                                mx[:, 8 * t:8 * t + 8].unsqueeze(2).broadcast_to([128, 8, N]),
                                                ALU.subtract).then_inc(sig(f"{st}_shifted"), 1)
                    if 1 <= t <= TILES:
                        u = t - 1
                        dve.wait_ge(sig(f"{st}_exp"), at(f"{st}_exp", u + 1))
                        nc.vector.tensor_reduce(rsum[:, 8 * u:8 * u + 8], E_[u % NE].rearrange("p (a k) -> p a k", k=N),
                                                AX_X, ALU.add).then_inc(sig(f"{st}_sum"), 1)
                        dve.wait_ge(sig(f"{st}_sum"), at(f"{st}_sum", u + 1))
                        nc.vector.reciprocal(rinv[:, 8 * u:8 * u + 8], rsum[:, 8 * u:8 * u + 8]).then_inc(sig(f"{st}_rinv"), 1)
                    if t >= LAG_A:
                        u = t - LAG_A
                        gp, r = tile_of(u)
                        dve.wait_ge(sig(f"{st}_fill_act"), at(f"{st}_fill_act", filled(f"g{2 * (2 * gp + 1) + r // HB}")))
                        dve.wait_ge(sig(f"{st}_av"), at(f"{st}_av", u + 1))
                        pos = slice(r * N, (r + 2) * N)
                        pair = slice(2 * gp, 2 * gp + 2)
                        nc.vector.scalar_tensor_tensor(
                            og[:, :].rearrange("p (g f) -> p g f", g=GB)[:, pair, pos],
                            gth[:, :].rearrange("p (g f) -> p g f", g=GB)[:, pair, pos], 1.0,
                            bank[4 + u % 2][:, 0:256].rearrange("p (g f) -> p g f", g=2),
                            ALU.add, ALU.mult).then_inc(sig(f"{st}_og"), 1)
                for name in others:
                    dve.wait_ge(sig(name), at(name, 1))
                for ch in range(2):
                    dve.wait_ge(sig(f"{st}_oproj"), at(f"{st}_oproj", ch + 1))
                    nc.vector.scalar_tensor_tensor(half(znew, ch), bank[ch], V(f"{st}_ob"), half(zres, ch),
                                                   ALU.add, ALU.add).then_inc(sig(f"{st}_z"), 1)

            attention("ta0", 0, z2T, z3T, ("z2_settled",))
            attention("ta1", 1, z3T, z4T, ())
            layer_norm("pt_ln")
            for n in range(1, 8, 2):
                dve.wait_ge(sig("pt_hproj"), at("pt_hproj", n + 1))
                if n >= 4:
                    dve.wait_ge(sig("pt_hused"), at("pt_hused", n - 3))
                nc.vector.tensor_scalar(hid[n % 4][:, :], bank[4 + n % 4][:, :], V("pt_b1"), 0.0, ALU.add, ALU.max).then_inc(sig("pt_hdve"), 1)
            dve.wait_ge(sig("xpad_zero"), at("xpad_zero", 1))
            for ch in range(2):
                dve.wait_ge(sig("pt_hused"), at("pt_hused", 4 * ch + 4))
                nc.vector.scalar_tensor_tensor(window(ch, 0, 0), rows8(bank[ch][:, :]), V("pt_b2"), rows8(half(z4T, ch)),
                                               ALU.add, ALU.add).then_inc(sig("pt_z"), 1)
            for ch in range(2):
                dve.wait_ge(sig("inv_zr"), at("inv_zr", ch + 1))
                nc.vector.tensor_copy(half(zhi, ch), half(zr, ch)).then_inc(sig("inv_zhi"), 1)
                dve.wait_ge(sig("inv_zhi"), at("inv_zhi", ch + 1))
                nc.vector.scalar_tensor_tensor(half(zst, ch), half(zhi, ch).bitcast(F32), V("lo_z"), half(zr, ch),
                                               ALU.mult, ALU.add).then_inc(sig("inv_zst"), 1)
            for i, p in enumerate(TAP_ORDER):
                if p % KS != PAD:
                    dve.wait_ge(sig("halo"), 32)
                elif i == 0:
                    dve.wait_ge(sig("pt_z"), 2)
                dve.wait_ge(sig("inv_kern"), i + 1)
                if i >= NPROD:
                    q = i - NPROD
                    if q < 2 * PAIRS:
                        dve.wait_ge(sig("inv_sum"), q // 2 + 1)
                nc.vector.scalar_tensor_tensor(rows8(prod[i % NPROD]), rows8(kern_banks(i)),
                                               vec[:, VEC["b2"] + p:VEC["b2"] + p + 1],
                                               xpad_v[:, p % KS:p % KS + RB, p // KS:p // KS + N],
                                               ALU.add, ALU.mult).then_inc(sig("inv_prod"), 1)

        @block.tensor
        def _(pe):
            mm = nc.tensor.matmul

            def layer_norm(name, waits):
                src, dst, sset, cb, vb, w, eps = LN[name]
                for ch in range(2):
                    for who, count in waits[ch]:
                        pe.wait_ge(sig(who), at(who, count))
                    rhs, o = half(src, ch), bank[cb[ch]]
                    mm(o, K("center"), rhs, start=True, stop=True).then_inc(sig(f"{name}_centered"), 1)
                for ch in range(2):
                    pe.wait_ge(sig(f"{name}_sq"), at(f"{name}_sq", ch + 1))
                    mm(bank[vb[ch]][:, :], K("mean"), half(sq[sset], ch), start=True, stop=True).then_inc(sig(f"{name}_var"), 1)

            pe.wait_ge(sig("in_const"), at("in_const", 16))
            layer_norm("tm0_ln", ([("in_z0R", 16)], []))
            layer_norm("tm0_lng", ([("in_z0T", 16), ("tm0_ln_xn", 1), ("tm0_ln_logv", 2)], [("tm0_ln_xn", 2)]))

            def ab_projections(st, s):
                pe.wait_ge(sig("rows_ready"), at("rows_ready", 2))
                pe.wait_ge(sig("in_tmw"), at("in_tmw", 16))
                for u in range(8):
                    pe.wait_ge(sig(f"{st}_ln_x"), at(f"{st}_ln_x", 1 + u // 4))
                    if u >= 4:
                        pe.wait_ge(sig(f"{st}_ab"), at(f"{st}_ab", u - 3))
                    b = bank[4 + u % 4]
                    mm(b, selr[:, :], rows[:, s * 512:(s + 1) * 512], start=True, stop=False, skip_group_check=True)
                    mm(b, x[:, 2 * u * N:(2 * u + 2) * N], tmw[:, s * 768:s * 768 + 512], start=False, stop=True,
                       skip_group_check=True).then_inc(sig(f"{st}_abproj"), 1)

            def gate_projection(st, s, src, src_name, waits):
                for ch in range(2):
                    pe.wait_ge(sig(src_name), at(src_name, ch + 1))
                    for who, count in waits[ch]:
                        pe.wait_ge(sig(who), at(who, count))
                    mm(bank[ch][:, :], tmw[:, s * 768 + 512:s * 768 + 640], half(src, ch), start=True, stop=True).then_inc(sig(f"{st}_gproj"), 1)

            def triangle(st, lhs_kind):
                pe.wait_ge(sig(f"{st}_ab"), at(f"{st}_ab", 8))
                for c in range(C):
                    hf, cc = c // CH, c % CH
                    kept = ab[64 * hf:64 * hf + 64, :].rearrange("p (m k) -> p m k", k=C)
                    moved = ab[64 * hf:64 * hf + 64, :].rearrange("p (r g k) -> p g r k", g=GB, k=C)
                    last = mm(bank[4 + c // 8][0:64, (c % 8) * N:(c % 8 + 1) * N].rearrange("p (g r) -> p g r", g=GB),
                              kept[:, :, lhs_kind * CH + cc], moved[:, :, :, (1 - lhs_kind) * CH + cc], start=True, stop=True)
                    if c % 8 == 7:
                        last.then_inc(sig(f"{st}_t"), 1)

            def triangle_back(st, s):
                pe.wait_ge(sig(f"{st}_tP_act"), at(f"{st}_tP_act", 2))
                pe.wait_ge(sig(f"{st}_tP_dve"), at(f"{st}_tP_dve", 2))
                for n in range(RB):
                    last = nc.tensor.transpose(bank[2 + n // HB][:, (n % HB) * N:(n % HB + 1) * N],
                                               tP[:, n * 128:(n + 1) * 128], K("ident")[0:64, 0:64])
                    if n % HB == HB - 1:
                        last.then_inc(sig(f"{st}_ttr"), 1)
                layer_norm(f"{st}_lno", ([(f"{st}_tB_act", 1), (f"{st}_gtanh", 2)], [(f"{st}_tB_dve", 1)]))
                for ch in range(2):
                    pe.wait_ge(sig(f"{st}_lno_x"), at(f"{st}_lno_x", ch + 1))
                    mm(bank[6 + ch][:, :], tmw[:, s * 768 + 640:s * 768 + 768], half(y, ch), start=True, stop=True).then_inc(sig(f"{st}_zo"), 1)

            ab_projections("tm0", 0)
            gate_projection("tm0", 0, xg, "tm0_lng_x", ([("tm0_lng_xn", 1)], [("tm0_lng_xn", 2)]))
            triangle("tm0", 0)
            triangle_back("tm0", 0)
            layer_norm("tm1_ln", ([("tm0_z", 1), ("tm0_lno_xn", 1)], [("tm0_z", 2), ("tm0_lno_xn", 2)]))
            gate_projection("tm1", 1, x, "tm1_ln_x", ([("tm1_ln_xn", 1)], [("tm1_ln_xn", 2)]))
            ab_projections("tm1", 1)
            pe.wait_ge(sig("in_qk"), at("in_qk", 16))
            pe.wait_ge(sig("tm1_gtanh"), at("tm1_gtanh", 2))
            for s in range(2):
                for h in range(H):
                    q0 = s * 1024 + h * 128
                    last = mm(bank[s][:, h * 128:(h + 1) * 128], qk[:, q0:q0 + 128], qk[:, q0 + 512:q0 + 640], start=True, stop=True)
                last.then_inc(sig("qk_product"), 1)
            triangle("tm1", 1)
            pe.wait_ge(sig("wyh_ready"), at("wyh_ready", 2))
            triangle_back("tm1", 1)

            def attention(st, s, swap, ln_waits):
                w0 = s * 688
                layer_norm(f"{st}_ln", ln_waits)
                pe.wait_ge(sig("in_taw"), at("in_taw", 16))
                for ch in range(2):
                    pe.wait_ge(sig(f"{st}_ln_x"), at(f"{st}_ln_x", ch + 1))
                    mm(bank[4 + ch][0:16, :], taw[:, w0 + 640:w0 + 656], half(x, ch), start=True, stop=True).then_inc(sig(f"{st}_bproj"), 1)
                for n in range(8):
                    if n >= 6:
                        pe.wait_ge(sig(f"{st}_y_act"), at(f"{st}_y_act", 1))
                        pe.wait_ge(sig(f"{st}_y_dve"), at(f"{st}_y_dve", n - 6))
                    mm(bank[YRING[n % 6]], wyh[:, s * 512 + (n // 2) * 128:s * 512 + (n // 2 + 1) * 128], half(x, n % 2),
                       start=True, stop=True).then_inc(sig(f"{st}_yproj"), 1)

                def fill(kind):
                    m, n = FILL.index(kind), int(kind[1])
                    if m >= 2:
                        pe.wait_ge(sig(f"{st}_fill_act"), at(f"{st}_fill_act", m - 1))
                    b = bank[6 + m % 2]
                    if kind[0] == "v":
                        mm(b, x[:, 2 * n * N:(2 * n + 2) * N], taw[:, w0:w0 + 512], start=True, stop=True).then_inc(sig(f"{st}_fill"), 1)
                    else:
                        g, ch = n // 2, n % 2
                        mm(b, taw[C * g:C * g + C, w0 + 512:w0 + 640], half(x, ch)[C * g:C * g + C, :],
                           start=True, stop=True).then_inc(sig(f"{st}_fill"), 1)

                pe.wait_ge(sig(f"{st}_y_act"), at(f"{st}_y_act", 4))
                pe.wait_ge(sig(f"{st}_y_dve"), at(f"{st}_y_dve", 4))
                pe.wait_ge(sig(f"{st}_xbd"), at(f"{st}_xbd", 2))
                pe.wait_ge(sig(f"{st}_bst"), at(f"{st}_bst", 2))
                pe.wait_ge(sig("pair_ready"), at("pair_ready", 1))
                pe.wait_ge(sig(f"{st}_brow"), at(f"{st}_brow", 2))
                for t in range(TILES + LAG_A):
                    if t < TILES:
                        gp, r0 = tile_of(t)
                        if t >= 2:
                            pe.wait_ge(sig(f"{st}_shifted"), at(f"{st}_shifted", t - 1))
                        b = bank[t % 2]
                        mm(b, pairr[:, :], bst[:, :], start=True, stop=False, skip_group_check=True)
                        for i2 in range(2):
                            r = r0 + i2
                            last = mm(b[:, 256 * i2:256 * i2 + 256].rearrange("p (h k) -> p h k", h=H),
                                      xbd[64 * gp:64 * gp + 64, r * 128:(r + 1) * 128],
                                      Y[64 * gp:64 * gp + 64, :].rearrange("p (h f) -> p h f", h=H)[:, :, r * N:(r + 1) * N],
                                      start=False, stop=True, skip_group_check=True)
                        last.then_inc(sig(f"{st}_scores"), 1)
                    if t < len(FILL_STEPS):
                        for kind in FILL_STEPS[t]:
                            fill(kind)
                    if LAG_P <= t < TILES + LAG_P:
                        u = t - LAG_P
                        pe.wait_ge(sig(f"{st}_probs"), at(f"{st}_probs", u + 1))
                        if u >= 2:
                            pe.wait_ge(sig(f"{st}_PT"), at(f"{st}_PT", u - 1))
                        for k in range(4):
                            last = nc.tensor.transpose(bank[2 + u % 2][:, 128 * k:128 * k + 128],
                                                       PN[u % 2][:, 128 * k:128 * k + 128], K("ident"))
                        last.then_inc(sig(f"{st}_ptrans"), 1)
                    if t >= LAG_A:
                        u = t - LAG_A
                        gp, r0 = tile_of(u)
                        pe.wait_ge(sig(f"{st}_PT"), at(f"{st}_PT", u + 1))
                        pe.wait_ge(sig(f"{st}_fill_act"), at(f"{st}_fill_act", filled(f"v{u % 8}")))
                        if u >= 2:
                            pe.wait_ge(sig(f"{st}_og"), at(f"{st}_og", u - 1))
                        for i2 in range(2):
                            for g2 in range(2):
                                for hp in range(2):
                                    v0 = (((r0 + i2) * GB + 2 * gp + g2) * 2 + hp) * 64
                                    p0 = (i2 * 2 + hp) * 128 + g2 * 64
                                    o0 = (g2 * 2 + i2) * 64
                                    last = mm(bank[4 + u % 2][64 * hp:64 * hp + 64, o0:o0 + 64], vbd[:, v0:v0 + 64],
                                              PT[u % 2][:, p0:p0 + 64], start=True, stop=True, skip_group_check=True)
                        last.then_inc(sig(f"{st}_av"), 1)
                pe.wait_ge(sig("wo_ready"), at("wo_ready", 2))
                pe.wait_ge(sig(f"{st}_og"), at(f"{st}_og", TILES))
                for ch in range(2):
                    for b in range(GB):
                        if swap:
                            q = og[:, :].rearrange("p (g r q) -> p q g r", g=GB, r=RB)[:, b * RB + ch * HB:b * RB + (ch + 1) * HB]
                            o = bank[ch][C * b:C * b + C, :].rearrange("p (q g r) -> p q g r", g=GB, r=RB)
                        else:
                            q, o = og[:, b * F + ch * HALF:b * F + (ch + 1) * HALF], bank[ch][C * b:C * b + C, :]
                        last = mm(o, wohalf[:, s * C:(s + 1) * C], q, start=True, stop=True, skip_group_check=True)
                    last.then_inc(sig(f"{st}_oproj"), 1)

            attention("ta0", 0, True, ([("tm1_z", 1), ("tm1_lno_xn", 1)], [("tm1_z", 2), ("tm1_lno_xn", 2)]))
            attention("ta1", 1, False, ([("ta0_z", 1)], [("ta0_z", 2)]))
            layer_norm("pt_ln", ([("ta1_z", 1)], [("ta1_z", 2)]))
            pe.wait_ge(sig("in_ptw"), at("in_ptw", 16))
            pe.wait_ge(sig("pt_ln_xn"), at("pt_ln_xn", 2))
            for n in range(9):
                if n < 8:
                    ch, g = n // 4, n % 4
                    pe.wait_ge(sig("pt_ln_x"), at("pt_ln_x", ch + 1))
                    if n >= 4:
                        pe.wait_ge(sig("pt_hact"), at("pt_hact", (n - 4) // 2 + 1))
                        pe.wait_ge(sig("pt_hdve"), at("pt_hdve", (n - 3) // 2))
                    mm(bank[4 + n % 4][:, :], ptw[C * g:C * g + C, 0:128], half(x, ch)[C * g:C * g + C, :],
                       start=True, stop=True).then_inc(sig("pt_hproj"), 1)
                if n >= 1:
                    u = n - 1
                    ch, g = u // 4, u % 4
                    pe.wait_ge(sig("pt_hdve" if u % 2 else "pt_hact"), at("pt_hdve" if u % 2 else "pt_hact", u // 2 + 1))
                    mm(bank[ch][C * g:C * g + C, :], ptw[:, 128:160], hid[u % 4][:, :], start=True, stop=True,
                       skip_group_check=True).then_inc(sig("pt_hused"), 1)
            pe.wait_ge(sig("in_ivw1"), at("in_ivw1", 16))
            for ch in range(2):
                pe.wait_ge(sig("pt_z"), at("pt_z", ch + 1))
                mm(rows8(bank[2 + ch][:, :]), ivw1[:, :], window(ch, 0, 0), start=True, stop=True).then_inc(sig("inv_zproj"), 1)
            pe.wait_ge(sig("w2_ready"), at("w2_ready", 1))
            pe.wait_ge(sig("inv_zst"), 2)
            pe.wait_ge(sig("inv_zr"), 2)
            AHEAD = 3
            kern = 0
            for j, taps in enumerate(SUMS):
                while kern < min(TAPS, taps[-1] + 1 + AHEAD):
                    p = TAP_ORDER[kern]
                    if kern >= 3:
                        pe.wait_ge(sig("inv_prod"), kern - 2)
                    for ch in range(2):
                        last = mm(half(kern_banks(kern), ch), w2s[:, p * 128:(p + 1) * 128], half(zst, ch), start=True, stop=True)
                    last.then_inc(sig("inv_kern"), 1)
                    kern += 1
                if len(taps) == 2:
                    pe.wait_ge(sig("inv_sum"), j + 1)
                    term = psums[j % NSUM]
                else:
                    pe.wait_ge(sig("inv_prod"), taps[0] + 1)
                    term = prod[taps[0] % NPROD]
                for ch in range(2):
                    last = mm(bank[ch], K("ident"), half(term, ch), start=(j == 0), stop=(j == len(SUMS) - 1))
                last.then_inc(sig("inv_acc"), 1)


def kernel(**inputs):
    import numpy as np
    import concourse.bacc as bacc
    from concourse.bass_utils import run_bass_kernel_spmd

    a = {k.replace("L0_conv_", "").replace("L1_conv_", "inv_"): np.asarray(v) for k, v in inputs.items()}
    f4 = a["x"].dtype

    def blocked(m):
        return np.ascontiguousarray(m.reshape(GB, RB, N, C).transpose(0, 3, 1, 2).reshape(128, F))

    def diag(w):
        o = np.zeros((GB, C, GB, w.shape[1]), f4)
        for g in range(GB):
            o[g, :, g] = w
        return o.reshape(128, -1)

    def rep(v):
        return np.tile(v, (GB,) + (1,) * (v.ndim - 1))

    z = a["x"][0]
    vecs = np.zeros((128, NVEC), f4)

    def put(name, v):
        vecs[:, VEC[name]] = v

    def zparts(v):
        return np.tile(v, 128 // G8)

    p = np.arange(128)
    for s in range(2):
        put(f"tm{s}_lnin_w", rep(a["tm_ln_in_w"][s])); put(f"tm{s}_lnin_b", rep(a["tm_ln_in_b"][s]))
        put(f"tm{s}_lnout_w", rep(a["tm_lnout_w"][s])); put(f"tm{s}_lnout_b", rep(a["tm_lnout_b"][s]))
        put(f"tm{s}_zb", rep(a["tm_zo_b"][s])); put(f"tm{s}_gb", rep(a["tm_g_b"][s]))
        put(f"ta{s}_ln_w", rep(a["ta_ln_w"][s])); put(f"ta{s}_ln_b", rep(a["ta_ln_b"][s]))
        put(f"ta{s}_ob", rep(a["ta_o_b"][s])); put(f"ta{s}_gb", a["ta_g_b"][s])
    put("pt_w", rep(a["pt_ln_w"])); put("pt_b", rep(a["pt_ln_b"]))
    put("pt_b1", a["pt_1_b"]); put("pt_b2", rep(a["pt_2_b"]))
    for n, k in (("bn_b1", "inv_b1"), ("bn_gamma", "inv_gamma"), ("bn_beta", "inv_beta"), ("bn_mean", "inv_mean"), ("bn_var", "inv_var")):
        put(n, zparts(a[k]))
    put("eps5", 1e-5); put("eps5x16", 16e-5); put("eps3", 1e-3)
    put("mask_g0", (p // C) % 2 == 0); put("mask_g1", (p // C) % 2 == 1)
    put("lo_z", -1.0 * ((p // G8) % 4 >= 2))
    put("lo_w", -1.0 * ((p // G8) % 2 == 1))
    put("lo_pair", -1.0 * (p >= N))
    put("lo_row", -1.0 * (p % 2 == 1))
    vecs[:, VEC["b2"]:VEC["b2"] + TAPS] = np.tile(a["inv_b2"].reshape(TAPS, G8).T, (128 // G8, 1))

    eye = np.eye(128, dtype=f4)
    mean = diag(np.full((C, C), 1.0 / C, f4))
    pair = (p[:, None] % N == p[None, :] % N).astype(f4)
    bdscale = diag(np.full((C, C), 1.0 / np.sqrt(C), f4))
    consts = np.concatenate([{"ident": eye, "center": eye - mean, "mean": mean, "bdscale": bdscale, "pair": pair}[k] for k in CONST], 1)
    selrow = np.ones((2, 128), f4)

    tm_w, tm_rows = [], []
    for s in range(2):
        def columns(w):
            halves = [w[k][..., CH * ch:CH * ch + CH] for kinds in (("ap", "bp"), ("ag", "bg")) for ch in range(2) for k in kinds]
            return np.concatenate(halves, -1)

        tm_w.append(diag(columns({k: a[f"tm_{k}_w"][s] for k in ("ap", "bp", "ag", "bg")})))
        tm_w += [diag(a["tm_g_w"][s]), diag(a["tm_zo_w"][s])]
        row = np.tile(columns({k: a[f"tm_{k}_b"][s] for k in ("ap", "bp", "ag", "bg")}), GB)
        tm_rows.append(np.stack([row, row]))
    ta_w, ta_qk = [], []
    for s in range(2):
        ta_w.append(diag(a["ta_v_w"][s]))
        pair_w = diag(a["ta_b_w"][s]).reshape(128, GB, H).transpose(0, 2, 1).reshape(128, GB * H)
        ta_w += [rep(a["ta_g_w"][s]), pair_w, a["ta_o_w"][s]]
        for k in ("ta_k_w", "ta_q_w"):
            w = a[k][s].reshape(C, H, C).transpose(2, 1, 0)
            ta_qk.append(np.tile(w[:, :, None, :], (1, 1, GB, 1)).reshape(C, H * 128))
    w2 = a["inv_w2"].reshape(G8, TAPS, G8)
    w2s = np.zeros((GB, 4, G8, TAPS, GB, 4, G8), f4)
    for g in range(GB):
        w2s[g, :, :, :, g] = w2[None, :, :, None, :]
    w1s = np.zeros((GB, C, GB, 4, G8), f4)
    for g in range(GB):
        w1s[g, :, g] = a["inv_w1"][:, None, :]

    arrays = {
        "z_rows": blocked(z), "z_cols": blocked(z.transpose(1, 0, 2)), "vecs": vecs, "consts": consts, "selrow": selrow,
        "tm_w": np.concatenate(tm_w, 1), "tm_rows": np.concatenate(tm_rows, 1),
        "ta_w": np.concatenate(ta_w, 1), "ta_qk": np.concatenate(ta_qk, 1),
        "pt_w": np.concatenate([rep(a["pt_1_w"]), a["pt_2_w"]], 1),
        "inv_w1": w1s.reshape(128, 128), "inv_w2": w2s.reshape(128, TAPS * 128),
    }
    nc = bacc.Bacc("TRN2", target_bir_lowering=False, num_devices=1)
    args = []
    for name, v in arrays.items():
        arrays[name] = np.ascontiguousarray(v)
        args.append(nc.dram_tensor(name, v.shape, F32, kind="ExternalInput").ap())
    args.append(nc.dram_tensor("result", (128, F), F32, kind="ExternalOutput").ap())
    build_program(nc, *args)
    r = run_bass_kernel_spmd(nc, [arrays], core_ids=[0]).results[0]["result"]
    return np.ascontiguousarray(r.reshape(GB, C, RB, N).transpose(3, 0, 2, 1).reshape(1, N, N, C))
```

```python
from contextlib import ExitStack

import concourse.bass as bass
from concourse import mybir

ALU = mybir.AluOpType
ACT = mybir.ActivationFunctionType
F32 = mybir.dt.float32
F32R = mybir.dt.float32r
AX_X = mybir.AxisListType.X

N = 64
C = 32
GB = 128 // C
RB = N // GB
F = RB * N
HALF = F // 2
HB = RB // 2
H = 4
CH = C // 2
TAPS = 25
KS = 5
PAD = KS // 2
G8 = 8
PW = N + 2 * PAD
PH = RB + 2 * PAD

VEC = {}
for _s in range(2):
    for _n in ("lnin_w", "lnin_b", "lnout_w", "lnout_b"):
        VEC[f"tm{_s}_{_n}"] = len(VEC)
    for _n in ("ln_w", "ln_b", "ob"):
        VEC[f"ta{_s}_{_n}"] = len(VEC)
for _n in ("pt_w", "pt_b", "pt_b2", "fold_tm0", "fold_tm1", "fold_pt", "bn_b1", "bn_gamma", "bn_beta", "bn_mean", "bn_var",
           "tm0_gb", "tm1_gb", "ta0_gb", "ta1_gb",
           "eps5", "eps5x16", "eps3", "mask_g0", "mask_g1", "lo_z", "lo_w", "lo_q", "lo_pair", "lo_row"):
    VEC[_n] = len(VEC)
VEC["b2"] = len(VEC)
NVEC = VEC["b2"] + TAPS

TAW = 2 * 128 + GB * H + C

CONST = ("center", "mean", "ident", "bdscale", "pair")


def build_program(nc, z_rows, z_cols, vecs, consts, selrow, tm_w, tm_rows, ta_w, ta_qk, pt_w, inv_w1, inv_w2, out):
    with ExitStack() as ctx:
        def sb(name, cols, dt=F32, parts=128):
            return ctx.enter_context(nc.sbuf_tensor(name, [parts, cols], dt))

        signals = {}
        NORMS = ("tm0_ln", "tm0_lng", "tm0_lno", "tm1_ln", "tm1_lno", "ta0_ln", "ta1_ln", "pt_ln")
        RAISES = {"abproj": 8, "abtanh": 8, "ab": 8, "t": 4, "tB_act": 1, "tB_dve": 1, "bhi": 1, "braw": 32, "bias_hop": 16,
                  "yproj": 8, "y_act": 4, "y_dve": 4, "fill": 16, "fill_act": 16, "opened": 8, "xhi": 1, "xlo": 1, "xstacked": 16 * GB * 4}
        RAISES.update({k: 16 for k in ("scores", "max", "shifted", "exp", "sum", "rinv", "probs", "ptrans", "PT", "av", "og")})
        RAISES["avout"] = 15

        def shared(name):
            for norm in NORMS:
                if name == norm + "_xn":
                    return "ln_xn", 2 * [n for n in NORMS if n not in LN_BIAS_FOLDED].index(norm)
                if name.startswith(norm + "_"):
                    return "ln_" + name[len(norm) + 1:], 2 * NORMS.index(norm)
            for kind in ("tm", "ta"):
                if name[:2] == kind and name[2] in "01" and name[3] == "_":
                    return kind + name[3:], int(name[2]) * RAISES.get(name[4:], 2)
            return name, 0

        def sig(name):
            name = shared(name)[0]
            if name not in signals:
                signals[name] = ctx.enter_context(nc.semaphore(name))
            return signals[name]

        def at(name, count):
            return shared(name)[1] + count

        psum = ctx.enter_context(nc.psum_tensor("psum", [128, 8 * HALF], F32))
        bank = [psum[:, i * HALF:(i + 1) * HALF] for i in range(8)]

        z0R = sb("z0R", F)
        z0T = sb("z0T", F)
        vec = sb("vec", NVEC)
        cst = sb("cst", 128 * len(CONST))
        selraw = sb("selraw", 128, parts=2)
        tmw = sb("tmw", 2 * 768)
        taw = sb("taw", 2 * TAW)
        ptw = sb("ptw", 4 * 128 + C)
        ivw1 = sb("ivw1", 128)

        def V(name):
            return vec[:, VEC[name]:VEC[name] + 1]

        def K(name):
            i = CONST.index(name)
            return cst[:, 128 * i:128 * i + 128]

        halfgb = sb("halfgb", 4)
        selr = sb("selr", 128, F32R, parts=2)
        rows = sb("rows", 2 * 512, F32R, parts=2)
        pairr = sb("pairr", 128, F32R)
        wyh = sb("wyh", 2 * H * 128)
        wohalf = sb("wohalf", 2 * C)
        wvg = sb("wvg", 2 * 256, F32R)
        bnscale = sb("bnscale", 4)
        folded = sb("folded", 3)
        w2s = sb("w2s", TAPS * 128, F32R)

        xstack = sb("xstack", GB * F, F32R)
        Y = sb("Y", H * F)
        xbd = sb("xbd", RB * 128)
        vals = sb("vals", 8 * HALF)
        gth = sb("gth", GB * F)
        og = sb("og", GB * F)
        braw = sb("braw", H * N)
        bhi = sb("bhi", H * N, F32R)
        bst = sb("bst", 2 * H * N, F32R)
        mx = sb("mx", 16 * 8)
        rsum = sb("rsum", 16 * 8)
        rinv = sb("rinv", 16 * 8)
        NE = 4
        soft = sb("soft", 8 * HALF)
        E_ = [soft[:, i * HALF:(i + 1) * HALF] for i in range(NE)]
        PN = [soft[:, i * HALF:(i + 1) * HALF] for i in (4, 5)]
        PT = [soft[:, i * HALF:(i + 1) * HALF] for i in (6, 7)]

        lnroom = sb("lnroom", 4 * F)
        sq, logv, rstd, xn = [[room[:, i * F:(i + 1) * F] for room in (lnroom, Y)] for i in range(4)]

        x = sb("x", F)
        y = sb("y", F)
        gate = sb("gate", F)
        gateR = sb("gateR", F)
        th = sb("th", F)
        xg = gateR
        xhi, xlo = th[:, :].bitcast(F32R), gateR[:, :].bitcast(F32R)
        wvghi = xstack[:, 0:512]
        abth = soft[:, 4 * HALF:5 * HALF]
        ab = xbd
        tP = og[0:64, 0:2 * F]
        tB = og[:, 2 * F:3 * F]
        upd = og[:, 3 * F:4 * F]
        brow = y[0:16, :]
        avout = [y[:, i * 256:(i + 1) * 256] for i in range(2)]
        z1T = sb("z1T", F)
        z1R = sb("z1R", F)
        z2R = sb("z2R", F)
        z2T, z4T, z3T = z0R, z0T, z1R
        perm = [vals[:, 0:F], vals[:, F:2 * F], gate]
        arrive = [vals[:, 2 * F:3 * F], vals[:, 3 * F:4 * F], z1T]

        qk = soft[0:32, 0:2 * 2 * H * 128]
        rowraw = gate[0:2, :]
        rowhi = th[0:2, :].bitcast(F32R)
        ivw2raw = gth[:, 0:TAPS * 128]
        w2hi = Y[:, 0:TAPS * 128].bitcast(F32R)

        hid = [og[:, i * HALF:(i + 1) * HALF] for i in range(8)]
        xpad = soft[:, 0:PH * PW]
        zr = x
        zhi = gateR[:, :].bitcast(F32R)
        zst = sb("zst", F, F32R)
        NPROD, NSUM = 8, 4
        prod = [gth[:, i * F:(i + 1) * F] for i in range(4)] + [vals[:, i * F:(i + 1) * F] for i in range(4)]
        psums = [lnroom[:, i * F:(i + 1) * F] for i in range(NSUM)]
        res = Y[:, 0:F]

        hop = [nc.dram_tensor(f"hop{i}", (128, F), F32, kind="Internal").ap() for i in range(3)]
        bias_hop = [nc.dram_tensor(f"bias_hop{i}", (GB * H, F), F32, kind="Internal").ap() for i in range(2)]

        def half(buf, ch):
            return buf[:, ch * HALF:(ch + 1) * HALF]

        def raw_cols(ap):
            return ap.rearrange("p (n r g) -> p n g r", n=HB, g=GB)

        def sorted_cols(ap):
            return ap.rearrange("p (n g r) -> p n g r", n=HB, g=GB)

        xpad_v = xpad[:, :].rearrange("p (a b) -> p a b", b=PW)

        def window(ch, dr, dn):
            r0 = PAD + HB * ch + dr
            return xpad_v[:, r0:r0 + HB, PAD + dn:PAD + dn + N]

        def rows8(ap):
            return ap.rearrange("p (a b) -> p a b", b=N)

        TILES = 16
        LAG_P, LAG_A = 3, 4

        def tile_of(t):
            return t // 8, 2 * (t % 8)

        YBANKS = ((2, 3, 6, 7), (0, 1, 4, 5))
        FILL_STEPS = ((), (), (), ("v0", "g0"), ("v1", "g2"), ("v2",), ("v3", "g1"), ("v4", "g3"), ("v5",),
                      ("v6", "g4"), ("v7", "g6"), ("g5",), ("g7",))
        OUT_PARTS = {True: ((0, 2, 0, RB, 8), (2, GB, 0, HB, 12), (2, GB, HB, RB, TILES)),
                     False: ((0, 2, 0, HB, 4), (0, 2, HB, RB, 8), (2, GB, 0, HB, 12), (2, GB, HB, RB, TILES))}
        OUT_STEPS = {True: (16, 18, None), False: (16, 17, 18, None)}
        FILL = [k for step in FILL_STEPS for k in step]

        def filled(kind):
            return FILL.index(kind) + 1

        def opened(kind):
            return [k for k in FILL if k[0] == "g"].index(kind) + 1

        TAP_ORDER = sorted(range(TAPS), key=lambda p: (p % KS != PAD, p))
        HEAD_SINGLES, PAIRS = 1, 12
        SUMS = [(i,) for i in range(HEAD_SINGLES)]
        SUMS += [(HEAD_SINGLES + 2 * i, HEAD_SINGLES + 2 * i + 1) for i in range(PAIRS)]
        SUMS += [(i,) for i in range(HEAD_SINGLES + 2 * PAIRS, TAPS)]

        def term_of(tap):
            return [tap in taps for taps in SUMS].index(True)

        def kern_banks(i):
            return psum[:, (2 + 2 * (i % 3)) * HALF:(4 + 2 * (i % 3)) * HALF]

        WARM_START, WARM_LN, WARM_HOP, WARM_HEAD = 3, 5, 4, 1
        WARM_TAIL, WARM_END = (0, 0, 0, 0), 2
        WARM_STEP = [1 if t in (3, 4) else 0 for t in range(TILES + LAG_P)]
        WARM_TRIANGLE, WARM_KERNEL = 2, 4

        LN = {
            "tm0_ln": (z0R, x, 0, (0, 1), (2, 3), "tm0_lnin", "eps5"),
            "tm0_lng": (z0T, xg, 1, (0, 1), (2, 3), "tm0_lnin", "eps5"),
            "tm0_lno": (tB, y, 0, (6, 7), (4, 5), "tm0_lnout", "eps5x16"),
            "tm1_ln": (upd, x, 0, (0, 1), (2, 3), "tm1_lnin", "eps5"),
            "tm1_lno": (tB, y, 0, (6, 7), (4, 5), "tm1_lnout", "eps5x16"),
            "ta0_ln": (upd, x, 0, (0, 1), (2, 3), "ta0_ln", "eps5"),
            "ta1_ln": (z3T, x, 0, (0, 1), (2, 3), "ta1_ln", "eps5"),
            "pt_ln": (z4T, x, 0, (0, 1), (2, 3), "pt", "eps5"),
        }

        LN_OF_SUM = ("tm1_ln", "ta0_ln")
        LN_BIAS_FOLDED = ("tm0_lno", "tm1_lno", "pt_ln")

        block = ctx.enter_context(nc.Block())

        @block.sync
        def _(sp):
            sp.dma_start(cst[:, 0:256], consts[:, 0:256]).then_inc(sig("in_stats"), 16)
            for ch in range(2):
                sp.dma_start(half(z0R, ch), z_rows[:, ch * HALF:(ch + 1) * HALF]).then_inc(sig(f"in_z0R_{ch}"), 16)
            sp.dma_start(vec[:, :], vecs).then_inc(sig("in_vec"), 16)
            sp.dma_start(cst[:, 256:], consts[:, 256:]).then_inc(sig("in_const"), 16)
            sp.dma_start(tmw[:, :], tm_w).then_inc(sig("in_tmw"), 16)
            sp.dma_start(z0T[:, :], z_cols).then_inc(sig("in_z0T"), 16)

            def relayout(i, name):
                sp.wait_ge(sig(f"{name}_permuted"), at(f"{name}_permuted", 1))
                sp.dma_start(hop[i][:, :], perm[i][:, :]).then_inc(sig(f"{name}_hop"), 16)
                sp.wait_ge(sig(f"{name}_hop"), at(f"{name}_hop", 16))
                for g in range(GB):
                    sp.dma_start(arrive[i][g * C:(g + 1) * C, :].rearrange("c (s f) -> c s f", s=GB),
                                 hop[i][:, g * RB * RB:(g + 1) * RB * RB].rearrange("(s c) f -> c s f", s=GB),
                                 ).then_inc(sig(f"{name}_arrived"), 16)

            relayout(0, "z1")
            relayout(1, "gate1")
            relayout(2, "z2")

            def stack(st, parts, blocks=range(GB)):
                for part in parts:
                    src, ready = (xhi, "xhi") if part < 2 else (xlo, "xlo")
                    sp.wait_ge(sig(f"{st}_{ready}"), at(f"{st}_{ready}", 1))
                    for g in blocks:
                        sp.dma_start(xstack[part * C:(part + 1) * C, g * F:(g + 1) * F].bitcast(F32),
                                     src[g * C:(g + 1) * C, :].bitcast(F32)).then_inc(sig(f"{st}_xstacked"), 16)

            def attention(st, s):
                stack(st, (0,), (0, 1))
                sp.wait_ge(sig(f"{st}_brow"), at(f"{st}_brow", 2))
                sp.dma_start(bias_hop[s][:, :], brow).then_inc(sig(f"{st}_bias_hop"), 16)
                stack(st, (0,), (2, 3))
                sp.wait_ge(sig(f"{st}_bias_hop"), at(f"{st}_bias_hop", 16))
                for part in range(2):
                    sp.dma_start(braw[part * N:(part + 1) * N, :].rearrange("q (h k) -> q h k", h=H),
                                 bias_hop[s].rearrange("(h g) (r k) -> (g r) h k", h=H, k=N)).then_inc(sig(f"{st}_braw"), 16)
                stack(st, (1, 2, 3))

            attention("ta0", 0)
            attention("ta1", 1)
            sp.wait_ge(sig("pt_z"), at("pt_z", 2))
            sp.dma_start(xpad_v[C:128, 0:PAD, :], xpad_v[0:128 - C, RB:RB + PAD, :]).then_inc(sig("halo"), 16)
            sp.dma_start(xpad_v[0:128 - C, PAD + RB:PH, :], xpad_v[C:128, PAD:2 * PAD, :]).then_inc(sig("halo"), 16)
            for ch in range(2):
                sp.wait_ge(sig("inv_result"), at("inv_result", ch + 1))
                sp.dma_start(out[:, ch * HALF:(ch + 1) * HALF], half(res, ch)).then_inc(sig("stored"), 16)
            sp.wait_ge(sig("stored"), at("stored", 32))

        @block.gpsimd
        def _(pool):
            pool.dma_start(selraw[:, :], selrow).then_inc(sig("in_rows"), 16)
            pool.dma_start(rowraw[:, :], tm_rows).then_inc(sig("in_rows"), 16)
            pool.dma_start(qk[:, :], ta_qk).then_inc(sig("in_qk"), 16)
            pool.dma_start(taw[:, :], ta_w).then_inc(sig("in_taw"), 16)
            pool.dma_start(ptw[:, :], pt_w).then_inc(sig("in_ptw"), 16)
            pool.dma_start(ivw1[:, :], inv_w1).then_inc(sig("in_ivw1"), 16)
            pool.dma_start(ivw2raw, inv_w2).then_inc(sig("in_ivw2"), 16)

            def permute(i, name, src, ready):
                pool.wait_ge(sig(ready), at(ready, 2))
                pool.tensor_copy(perm[i][:, :].rearrange("p (g n r) -> p r g n", g=GB, n=RB),
                                 src[:, :].rearrange("p (r g n) -> p r g n", g=GB, n=RB)).then_inc(sig(f"{name}_permuted"), 1)

            def settle(i, name, dst, is_gate=False):
                pool.wait_ge(sig(f"{name}_arrived"), at(f"{name}_arrived", 16 * GB))
                src = arrive[i][:, :].rearrange("p (s r n) -> p r s n", s=GB, n=RB)
                dst = dst[:, :].rearrange("p (r s n) -> p r s n", s=GB, n=RB)
                if is_gate:
                    op = pool.tensor_scalar(dst, src, 0.5, 0.5, ALU.mult, ALU.add)
                else:
                    op = pool.tensor_copy(dst, src)
                op.then_inc(sig(f"{name}_settled"), 1)

            permute(0, "z1", z1T, "tm0_z")
            permute(1, "gate1", th, "tm1_gtanh")
            settle(0, "z1", z1R)
            settle(1, "gate1", gateR, is_gate=True)

            def attention(st):
                for t in range(TILES + LAG_A):
                    if t < TILES:
                        pool.wait_ge(sig(f"{st}_rinv"), at(f"{st}_rinv", t + 1))
                        if t >= 2:
                            pool.wait_ge(sig(f"{st}_ptrans"), at(f"{st}_ptrans", t - 1))
                        pool.tensor_tensor(
                            PN[t % 2][:, :].rearrange("p (a k) -> p a k", k=N),
                            E_[t % NE][:, :].rearrange("p (a k) -> p a k", k=N),
                            rinv[:, 8 * t:8 * t + 8].unsqueeze(2).broadcast_to([128, 8, N]), ALU.mult,
                        ).then_inc(sig(f"{st}_probs"), 1)
                    if LAG_A <= t < TILES + LAG_A - 1:
                        u = t - LAG_A
                        gp, r = tile_of(u)
                        pos = slice(r * N, (r + 2) * N)
                        pair = slice(2 * gp, 2 * gp + 2)
                        pool.wait_ge(sig(f"{st}_opened"), at(f"{st}_opened", opened(f"g{2 * (2 * gp + 1) + r // HB}")))
                        pool.wait_ge(sig(f"{st}_avout"), at(f"{st}_avout", u + 1))
                        pool.tensor_tensor(
                            og[:, :].rearrange("p (g f) -> p g f", g=GB)[:, pair, pos],
                            gth[:, :].rearrange("p (g f) -> p g f", g=GB)[:, pair, pos],
                            avout[u % 2][:, :].rearrange("p (g f) -> p g f", g=2), ALU.mult).then_inc(sig(f"{st}_og"), 1)

            permute(2, "z2", z2R, "tm1_z")
            settle(2, "z2", z2T)
            attention("ta0")
            attention("ta1")
            pool.wait_ge(sig("ta1_probs"), at("ta1_probs", TILES))
            pool.memset(xpad[:, :], 0.0).then_inc(sig("xpad_zero"), 1)
            for i in range(PAIRS):
                j = HEAD_SINGLES + i
                pool.wait_ge(sig("inv_prod"), SUMS[j][1] + 1)
                if i >= NSUM:
                    pool.wait_ge(sig("inv_acc"), j - NSUM + 1)
                pool.tensor_tensor(psums[i % NSUM], prod[SUMS[j][0] % NPROD], prod[SUMS[j][1] % NPROD], ALU.add).then_inc(sig("inv_sum"), 1)

        @block.scalar
        def _(act):
            def squares(name):
                src, dst, sset, cb, vb, w, eps = LN[name]
                for ch in range(2):
                    act.wait_ge(sig(f"{name}_centered"), at(f"{name}_centered", ch + 1))
                    nc.scalar.activation(half(sq[sset], ch), bank[cb[ch]][:, :], ACT.Square).then_inc(sig(f"{name}_sq"), 1)

            def log_variance(name, ch):
                src, dst, sset, cb, vb, w, eps = LN[name]
                act.wait_ge(sig(f"{name}_var"), at(f"{name}_var", ch + 1))
                nc.scalar.activation(half(logv[sset], ch), bank[vb[ch]][:, :], ACT.Ln, bias=V(eps)).then_inc(sig(f"{name}_logv"), 1)

            def inverse_deviation(name, ch):
                sset = LN[name][2]
                act.wait_ge(sig(f"{name}_logv"), at(f"{name}_logv", ch + 1))
                nc.scalar.activation(half(rstd[sset], ch), half(logv[sset], ch), ACT.Exp, scale=-0.5).then_inc(sig(f"{name}_rstd"), 1)

            def deviations(name):
                for ch in range(2):
                    log_variance(name, ch)
                    inverse_deviation(name, ch)

            def layer_norm(name, then_tanh=True):
                nc.scalar.preload_act_table_set("natural_log_exp_and_others")
                squares(name)
                deviations(name)
                if then_tanh:
                    nc.scalar.preload_act_table_set("exp_and_others")

            nc.scalar.preload_act_table_set("natural_log_exp_and_others")
            squares("tm0_ln")
            act.wait_ge(sig("in_vec"), at("in_vec", 16))
            deviations("tm0_ln")
            nc.scalar.activation(bnscale[:, 0:1], V("bn_var"), ACT.Ln, bias=V("eps3")).then_inc(sig("bn_log"), 1)
            act.wait_ge(sig("bn_log"), at("bn_log", 1))
            nc.scalar.activation(bnscale[:, 1:2], bnscale[:, 0:1], ACT.Exp, scale=-0.5).then_inc(sig("bn_a"), 1)
            nc.scalar.preload_act_table_set("exp_and_others")

            def ab_tanh(st, tiles):
                for u in tiles:
                    act.wait_ge(sig(f"{st}_abproj"), at(f"{st}_abproj", u + 1))
                    if u >= 2:
                        act.wait_ge(sig(f"{st}_ab"), at(f"{st}_ab", u - 1))
                    nc.scalar.activation(
                        abth[:, (u % 2) * 256:(u % 2) * 256 + 256].rearrange("p (g k) -> p g k", g=GB),
                        bank[4 + u % 4].rearrange("p (g k) -> p g k", g=GB)[:, :, 2 * C:4 * C],
                        ACT.Tanh, scale=0.5).then_inc(sig(f"{st}_abtanh"), 1)

            def gate_tanh(st, s):
                for ch in range(2):
                    act.wait_ge(sig(f"{st}_gproj"), at(f"{st}_gproj", ch + 1))
                    act.wait_ge(sig("halfgb"), at("halfgb", 1))
                    nc.scalar.activation(half(th, ch), bank[(2, 0)[s] + ch], ACT.Tanh, bias=halfgb[:, s:s + 1],
                                         scale=0.5).then_inc(sig(f"{st}_gtanh"), 1)

            def t_out(st):
                for b in (0, 2):
                    act.wait_ge(sig(f"{st}_t"), at(f"{st}_t", b + 1))
                    nc.scalar.activation(tP[:, :].rearrange("m (n g c) -> m c g n", g=GB, c=C)[:, 8 * b:8 * b + 8],
                                         bank[4 + b][0:64, :].rearrange("m (c g n) -> m c g n", c=8, g=GB),
                                         ACT.Copy).then_inc(sig(f"{st}_tP_act"), 1)

            def t_back(st):
                act.wait_ge(sig(f"{st}_ttr"), at(f"{st}_ttr", 1))
                nc.scalar.activation(sorted_cols(half(tB, 0)), raw_cols(bank[2][:, :]), ACT.Copy).then_inc(sig(f"{st}_tB_act"), 1)

            ab_tanh("tm0", range(0, 4))
            squares("tm0_lng")
            ab_tanh("tm0", range(4, 8))
            nc.scalar.preload_act_table_set("natural_log_exp_and_others")
            for ch in range(2):
                log_variance("tm0_lng", ch)
            t_out("tm0")
            for ch in range(2):
                inverse_deviation("tm0_lng", ch)
            t_back("tm0")
            layer_norm("tm0_lno")
            gate_tanh("tm0", 0)
            layer_norm("tm1_ln")
            ab_tanh("tm1", range(8))
            gate_tanh("tm1", 1)
            t_out("tm1")
            t_back("tm1")
            layer_norm("tm1_lno", False)

            def attention(st, s):
                layer_norm(f"{st}_ln")
                for ch in range(2):
                    act.wait_ge(sig(f"{st}_bproj"), at(f"{st}_bproj", ch + 1))
                    nc.scalar.activation(brow[:, ch * HALF:(ch + 1) * HALF], bank[4 + ch][0:16, :],
                                         ACT.Copy).then_inc(sig(f"{st}_brow"), 1)
                for ch in range(2):
                    for h in (0, 2):
                        act.wait_ge(sig(f"{st}_yproj"), at(f"{st}_yproj", 4 * ch + h + 1))
                        nc.scalar.activation(half(Y[:, h * F:(h + 1) * F], ch), bank[YBANKS[ch][h]],
                                             ACT.Copy).then_inc(sig(f"{st}_y_act"), 1)

                def fill(kind):
                    n = int(kind[1])
                    act.wait_ge(sig(f"{st}_fill"), at(f"{st}_fill", filled(kind)))
                    src = bank[6 + FILL.index(kind) % 2]
                    if kind[0] == "g":
                        op = nc.scalar.activation(gth[:, n * HALF:(n + 1) * HALF], src, ACT.Tanh,
                                                  bias=halfgb[:, 2 + s:3 + s], scale=0.5)
                    else:
                        op = nc.scalar.activation(vals[:, n * HALF:(n + 1) * HALF], src, ACT.Copy)
                    op.then_inc(sig(f"{st}_fill_act"), 1)

                def values_out(u):
                    act.wait_ge(sig(f"{st}_av"), at(f"{st}_av", u + 1))
                    if u >= 2:
                        act.wait_ge(sig(f"{st}_og"), at(f"{st}_og", u - 1))
                    nc.scalar.activation(
                        avout[u % 2][:, :].rearrange("p (g a q) -> p a g q", g=2, a=2),
                        psum[:, 4 * HALF:6 * HALF].rearrange("p (a f) -> p a f", a=2)[:, :, 0:128].rearrange("p a (g q) -> p a g q", g=2),
                        ACT.Copy).then_inc(sig(f"{st}_avout"), 1)

                def transposed_out(u):
                    act.wait_ge(sig(f"{st}_ptrans"), at(f"{st}_ptrans", u + 1))
                    if u >= 2:
                        act.wait_ge(sig(f"{st}_av"), at(f"{st}_av", u - 1))
                    nc.scalar.activation(PT[u % 2], bank[2 + u % 2], ACT.Copy).then_inc(sig(f"{st}_PT"), 1)

                for t in range(TILES + LAG_A):
                    if t < len(FILL_STEPS):
                        for kind in FILL_STEPS[t]:
                            fill(kind)
                    if LAG_P <= t < TILES + LAG_P:
                        transposed_out(t - LAG_P)
                    if t < TILES:
                        act.wait_ge(sig(f"{st}_shifted"), at(f"{st}_shifted", t + 1))
                        nc.scalar.activation(E_[t % NE], E_[t % NE], ACT.Exp).then_inc(sig(f"{st}_exp"), 1)
                    if LAG_A <= t < TILES + LAG_A - 1:
                        values_out(t - LAG_A)

            attention("ta0", 0)
            attention("ta1", 1)
            layer_norm("pt_ln", False)
            act.wait_ge(sig("folded"), 1)
            for n in range(0, 8, 2):
                act.wait_ge(sig("pt_hproj"), at("pt_hproj", n + 1))
                nc.scalar.activation(hid[n], bank[4 + n % 4], ACT.Relu, bias=folded[:, 2:3]).then_inc(sig("pt_hact"), 1)
            act.wait_ge(sig("bn_ready"), at("bn_ready", 1))
            for ch in range(2):
                act.wait_ge(sig("inv_zproj"), at("inv_zproj", ch + 1))
                nc.scalar.activation(half(zr, ch), bank[2 + ch][:, :], ACT.Relu, bias=bnscale[:, 3:4],
                                     scale=bnscale[:, 2:3]).then_inc(sig("inv_zr"), 1)
            for ch in range(2):
                act.wait_ge(sig("inv_acc"), len(SUMS))
                nc.scalar.activation(half(res, ch), bank[ch][:, :], ACT.Copy).then_inc(sig("inv_result"), 1)

        @block.vector
        def _(dve):
            def layer_norm(name):
                src, dst, sset, cb, vb, w, eps = LN[name]
                if name in LN_BIAS_FOLDED:
                    for ch in range(2):
                        dve.wait_ge(sig(f"{name}_rstd"), at(f"{name}_rstd", ch + 1))
                        nc.vector.scalar_tensor_tensor(half(dst, ch), bank[cb[ch]], V(w + "_w"), half(rstd[sset], ch),
                                                       ALU.mult, ALU.mult).then_inc(sig(f"{name}_x"), 1)
                    return
                for ch in range(2):
                    dve.wait_ge(sig(f"{name}_rstd"), at(f"{name}_rstd", ch + 1))
                    nc.vector.tensor_tensor(half(xn[sset], ch), bank[cb[ch]][:, :], half(rstd[sset], ch),
                                            ALU.mult).then_inc(sig(f"{name}_xn"), 1)
                    dve.wait_ge(sig(f"{name}_xn"), at(f"{name}_xn", ch + 1))
                    nc.vector.tensor_scalar(half(dst, ch), half(xn[sset], ch), V(w + "_w"), V(w + "_b"),
                                            ALU.mult, ALU.add).then_inc(sig(f"{name}_x"), 1)

            nc.vector.memset(sq[0][:, 0:256], 0.0).then_inc(sig("blank"), 1)
            dve.wait_ge(sig("in_vec"), at("in_vec", 16))
            nc.vector.tensor_scalar(halfgb[:, :], vec[:, VEC["tm0_gb"]:VEC["tm0_gb"] + 4], 0.5, None, ALU.mult).then_inc(sig("halfgb"), 1)
            dve.wait_ge(sig("in_rows"), at("in_rows", 32))
            nc.vector.tensor_copy(selr[:, :], selraw[:, :]).then_inc(sig("rows_ready"), 1)
            nc.vector.tensor_copy(rowhi[:, :], rowraw[:, :]).then_inc(sig("rows_hi"), 1)
            dve.wait_ge(sig("rows_hi"), at("rows_hi", 1))
            nc.vector.scalar_tensor_tensor(rows[:, :], rowhi.bitcast(F32), V("lo_row")[0:2, :], rowraw[:, :],
                                           ALU.mult, ALU.add).then_inc(sig("rows_ready"), 1)
            layer_norm("tm0_ln")
            dve.wait_ge(sig("in_const"), at("in_const", 16))
            nc.vector.tensor_copy(pairr[:, :], K("pair")).then_inc(sig("pair_ready"), 1)
            for s in range(2):
                dve.wait_ge(sig("qk_product"), at("qk_product", s + 1))
                nc.vector.tensor_tensor(wyh[:, s * 512:(s + 1) * 512].rearrange("p (h m) -> p h m", h=H),
                                        bank[6 + s][:, :].rearrange("p (h m) -> p h m", h=H),
                                        K("bdscale").unsqueeze(1).broadcast_to([128, H, 128]), ALU.mult).then_inc(sig("wyh_ready"), 1)

            def involution_weights():
                dve.wait_ge(sig("in_ivw2"), at("in_ivw2", 16))
                nc.vector.tensor_copy(w2hi, ivw2raw).then_inc(sig("w2_hi"), 1)

            def other_weights():
                dve.wait_ge(sig("w2_hi"), at("w2_hi", 1))
                nc.vector.scalar_tensor_tensor(w2s[:, :], w2hi.bitcast(F32), V("lo_w"), ivw2raw,
                                               ALU.mult, ALU.add).then_inc(sig("w2_ready"), 1)

            def attention_weights():
                dve.wait_ge(sig("in_taw"), at("in_taw", 16))
                for s in range(2):
                    nc.vector.tensor_scalar(wohalf[:, s * C:(s + 1) * C], taw[:, s * TAW + 272:s * TAW + 304], 0.5, None,
                                            ALU.mult).then_inc(sig("wo_ready"), 1)
                nc.vector.tensor_copy(wvghi.rearrange("p (s m) -> p s m", s=2),
                                      taw[:, :].rearrange("p (s m) -> p s m", s=2)[:, :, 0:256]).then_inc(sig("wvg_hi"), 1)
                dve.wait_ge(sig("wvg_hi"), at("wvg_hi", 1))
                nc.vector.scalar_tensor_tensor(wvg[:, :].rearrange("p (s m) -> p s m", s=2),
                                               wvghi.bitcast(F32).rearrange("p (s m) -> p s m", s=2), V("lo_q"),
                                               taw[:, :].rearrange("p (s m) -> p s m", s=2)[:, :, 0:256],
                                               ALU.mult, ALU.add).then_inc(sig("wvg_ready"), 1)
                dve.wait_ge(sig("bn_a"), at("bn_a", 1))
                nc.vector.tensor_tensor(bnscale[:, 2:3], bnscale[:, 1:2], V("bn_gamma"), ALU.mult).then_inc(sig("bn_b"), 1)
                nc.vector.tensor_tensor(bnscale[:, 0:1], V("bn_b1"), V("bn_mean"), ALU.subtract).then_inc(sig("bn_b"), 1)
                dve.wait_ge(sig("bn_b"), at("bn_b", 2))
                nc.vector.scalar_tensor_tensor(bnscale[:, 3:4], bnscale[:, 0:1], bnscale[:, 2:3], V("bn_beta"),
                                               ALU.mult, ALU.add).then_inc(sig("bn_ready"), 1)

            def ab_product(st):
                for u in range(8):
                    dve.wait_ge(sig(f"{st}_abtanh"), at(f"{st}_abtanh", u + 1))
                    for i2 in range(2):
                        for ch in range(2):
                            src = slice(64 * i2, 64 * i2 + 64)
                            last = nc.vector.scalar_tensor_tensor(
                                ab[64 * ch:64 * ch + 64, (2 * u + i2) * 128:(2 * u + i2 + 1) * 128].rearrange("p (g k) -> p g k", g=GB),
                                abth[src, (u % 2) * 256:(u % 2) * 256 + 256].rearrange("p (g k) -> p g k", g=GB)[:, :, C * ch:C * ch + C], 1.0,
                                bank[4 + u % 4][src, :].rearrange("p (g k) -> p g k", g=GB)[:, :, C * ch:C * ch + C],
                                ALU.add, ALU.mult)
                    last.then_inc(sig(f"{st}_ab"), 1)

            def tm_rest(st, s, g, zres, znew, others, weights):
                for b in (1, 3):
                    dve.wait_ge(sig(f"{st}_t"), at(f"{st}_t", b + 1))
                    nc.vector.tensor_copy(tP[:, :].rearrange("m (n g c) -> m c g n", g=GB, c=C)[:, 8 * b:8 * b + 8],
                                          bank[4 + b][0:64, :].rearrange("m (c g n) -> m c g n", c=8, g=GB)).then_inc(sig(f"{st}_tP_dve"), 1)
                if st == "tm0":
                    dve.wait_ge(sig("bias_products"), 1)
                    nc.vector.tensor_tensor(folded[:, :], bank[3][:, 0:3], vec[:, VEC["fold_tm0"]:VEC["fold_tm0"] + 3],
                                            ALU.add).then_inc(sig("folded"), 1)
                dve.wait_ge(sig(f"{st}_ttr"), at(f"{st}_ttr", 2))
                nc.vector.tensor_copy(sorted_cols(half(tB, 1)), raw_cols(bank[3][:, :])).then_inc(sig(f"{st}_tB_dve"), 1)
                if st == "tm0":
                    layer_norm("tm0_lng")
                weights()
                layer_norm(f"{st}_lno")
                if st == "tm0":
                    for ch in range(2):
                        dve.wait_ge(sig("tm0_gtanh"), at("tm0_gtanh", ch + 1))
                        nc.vector.tensor_scalar(half(gate, ch), half(th, ch), 0.5, 0.5, ALU.mult, ALU.add).then_inc(sig("tm0_gate"), 1)
                    dve.wait_ge(sig("tm0_gate"), 2)
                dve.wait_ge(sig("folded"), 1)
                for name in others:
                    dve.wait_ge(sig(name), at(name, 1))
                if st == "tm0":
                    dve.wait_ge(sig("in_z0T"), at("in_z0T", 16))
                for ch in range(2):
                    dve.wait_ge(sig(f"{st}_zo"), at(f"{st}_zo", ch + 1))
                    nc.vector.scalar_tensor_tensor(half(upd, ch), bank[6 + ch][:, :], folded[:, s:s + 1], half(g, ch),
                                                   ALU.add, ALU.mult).then_inc(sig(f"{st}_upd"), 1)
                for ch in range(2):
                    dve.wait_ge(sig(f"{st}_upd"), at(f"{st}_upd", ch + 1))
                    nc.vector.tensor_tensor(half(znew, ch), half(upd, ch), half(zres, ch), ALU.add).then_inc(sig(f"{st}_z"), 1)

            ab_product("tm0")
            tm_rest("tm0", 0, gate, z0T, z1T, (), involution_weights)
            layer_norm("tm1_ln")
            ab_product("tm1")
            tm_rest("tm1", 1, gateR, z1R, z2R, ("z1_settled", "gate1_settled"), other_weights)

            def attention(st, s, zres, znew, others, z_steps):
                layer_norm(f"{st}_ln")

                def residual(ch):
                    for name in others:
                        dve.wait_ge(sig(name), at(name, 1))
                    dve.wait_ge(sig(f"{st}_oproj"), at(f"{st}_oproj", ch + 1))
                    nc.vector.scalar_tensor_tensor(half(znew, ch), bank[6 + ch], V(f"{st}_ob"), half(zres, ch),
                                                   ALU.add, ALU.add).then_inc(sig(f"{st}_z"), 1)

                dve.wait_ge(sig(f"{st}_ln_x"), at(f"{st}_ln_x", 2))
                nc.vector.tensor_copy(xhi, x[:, :]).then_inc(sig(f"{st}_xhi"), 1)
                dve.wait_ge(sig(f"{st}_xhi"), at(f"{st}_xhi", 1))
                nc.vector.tensor_tensor(xlo, x[:, :], xhi.bitcast(F32), ALU.subtract).then_inc(sig(f"{st}_xlo"), 1)
                xb = xbd[:, :].rearrange("p (r a q) -> p r a q", a=2, q=N)
                for g2 in range(2):
                    nc.vector.tensor_scalar(xb[:, :, g2, :], rows8(x[:, :]), V(f"mask_g{g2}"), None,
                                            ALU.mult).then_inc(sig(f"{st}_xbd"), 1)
                for ch in range(2):
                    for h in (1, 3):
                        dve.wait_ge(sig(f"{st}_yproj"), at(f"{st}_yproj", 4 * ch + h + 1))
                        nc.vector.tensor_copy(half(Y[:, h * F:(h + 1) * F], ch), bank[YBANKS[ch][h]]).then_inc(sig(f"{st}_y_dve"), 1)
                dve.wait_ge(sig(f"{st}_braw"), at(f"{st}_braw", 32))
                nc.vector.tensor_copy(bhi[:, :], braw[:, :]).then_inc(sig(f"{st}_bhi"), 1)
                dve.wait_ge(sig(f"{st}_bhi"), at(f"{st}_bhi", 1))
                for again in range(2):
                    nc.vector.scalar_tensor_tensor(bst[:, :].rearrange("p (h a k) -> p h a k", h=H, a=2)[:, :, again, :],
                                                   bhi[:, :].bitcast(F32).rearrange("p (h k) -> p h k", h=H), V("lo_pair"),
                                                   braw[:, :].rearrange("p (h k) -> p h k", h=H), ALU.mult, ALU.add).then_inc(sig(f"{st}_bst"), 1)
                for t in range(TILES + LAG_A):
                    if t < TILES:
                        sc = bank[t % 2].rearrange("p (a k) -> p a k", k=N)
                        dve.wait_ge(sig(f"{st}_scores"), at(f"{st}_scores", t + 1))
                        nc.vector.tensor_reduce(mx[:, 8 * t:8 * t + 8], sc, AX_X, ALU.max).then_inc(sig(f"{st}_max"), 1)
                        dve.wait_ge(sig(f"{st}_max"), at(f"{st}_max", t + 1))
                        if t >= NE:
                            dve.wait_ge(sig(f"{st}_probs"), at(f"{st}_probs", t - NE + 1))
                        nc.vector.tensor_tensor(E_[t % NE].rearrange("p (a k) -> p a k", k=N), sc,
                                                mx[:, 8 * t:8 * t + 8].unsqueeze(2).broadcast_to([128, 8, N]),
                                                ALU.subtract).then_inc(sig(f"{st}_shifted"), 1)
                    if 1 <= t <= TILES:
                        u = t - 1
                        dve.wait_ge(sig(f"{st}_exp"), at(f"{st}_exp", u + 1))
                        nc.vector.tensor_reduce(rsum[:, 8 * u:8 * u + 8], E_[u % NE].rearrange("p (a k) -> p a k", k=N),
                                                AX_X, ALU.add).then_inc(sig(f"{st}_sum"), 1)
                        dve.wait_ge(sig(f"{st}_sum"), at(f"{st}_sum", u + 1))
                        nc.vector.reciprocal(rinv[:, 8 * u:8 * u + 8], rsum[:, 8 * u:8 * u + 8]).then_inc(sig(f"{st}_rinv"), 1)
                    for kind in FILL_STEPS[t - 1] if 1 <= t <= len(FILL_STEPS) else ():
                        if kind[0] == "g":
                            n = int(kind[1])
                            dve.wait_ge(sig(f"{st}_fill_act"), at(f"{st}_fill_act", filled(kind)))
                            nc.vector.tensor_scalar(gth[:, n * HALF:(n + 1) * HALF], gth[:, n * HALF:(n + 1) * HALF], 1.0, None,
                                                    ALU.add).then_inc(sig(f"{st}_opened"), 1)
                    if t == TILES + LAG_A - 1:
                        u = TILES - 1
                        gp, r = tile_of(u)
                        pair = slice(2 * gp, 2 * gp + 2)
                        dve.wait_ge(sig(f"{st}_av"), at(f"{st}_av", TILES))
                        for i2 in range(2):
                            pos = slice((r + i2) * N, (r + i2 + 1) * N)
                            last = nc.vector.tensor_tensor(
                                og[:, :].rearrange("p (g f) -> p g f", g=GB)[:, pair, pos],
                                gth[:, :].rearrange("p (g f) -> p g f", g=GB)[:, pair, pos],
                                bank[4 + i2][:, 0:128].rearrange("p (g f) -> p g f", g=2), ALU.mult)
                        last.then_inc(sig(f"{st}_og"), 1)
                    for ch in range(2):
                        if t == z_steps[ch]:
                            residual(ch)

            attention_weights()
            attention("ta0", 0, z2T, z3T, ("z2_settled",), (TILES + LAG_A - 1, TILES + LAG_A - 1))
            attention("ta1", 1, z3T, z4T, (), (TILES + LAG_A - 2, TILES + LAG_A - 1))
            layer_norm("pt_ln")
            def relu(n):
                dve.wait_ge(sig("pt_hproj"), at("pt_hproj", n + 1))
                nc.vector.tensor_scalar(hid[n], bank[4 + n % 4], folded[:, 2:3], 0.0, ALU.add, ALU.max).then_inc(sig("pt_hdve"), 1)

            def padded_result(ch):
                dve.wait_ge(sig("xpad_zero"), at("xpad_zero", 1))
                dve.wait_ge(sig("pt_hused"), at("pt_hused", ch + 1))
                nc.vector.scalar_tensor_tensor(window(ch, 0, 0), rows8(bank[ch][:, :]), V("pt_b2"), rows8(half(z4T, ch)),
                                               ALU.add, ALU.add).then_inc(sig("pt_z"), 1)

            for n in (1, 3):
                relu(n)
            padded_result(0)
            for n in (5, 7):
                relu(n)
            padded_result(1)
            for ch in range(2):
                dve.wait_ge(sig("inv_zr"), at("inv_zr", ch + 1))
                nc.vector.tensor_copy(half(zhi, ch), half(zr, ch)).then_inc(sig("inv_zhi"), 1)
                dve.wait_ge(sig("inv_zhi"), at("inv_zhi", ch + 1))
                nc.vector.scalar_tensor_tensor(half(zst, ch), half(zhi, ch).bitcast(F32), V("lo_z"), half(zr, ch),
                                               ALU.mult, ALU.add).then_inc(sig("inv_zst"), 1)
            for i, p in enumerate(TAP_ORDER):
                if p % KS != PAD:
                    dve.wait_ge(sig("halo"), 32)
                elif i == 0:
                    dve.wait_ge(sig("pt_z"), 2)
                dve.wait_ge(sig("inv_kern"), i + 1)
                if i >= NPROD:
                    j = term_of(i - NPROD)
                    if len(SUMS[j]) == 2:
                        dve.wait_ge(sig("inv_sum"), j - HEAD_SINGLES + 1)
                    else:
                        dve.wait_ge(sig("inv_acc"), j + 1)
                nc.vector.scalar_tensor_tensor(rows8(prod[i % NPROD]), rows8(kern_banks(i)),
                                               vec[:, VEC["b2"] + p:VEC["b2"] + p + 1],
                                               xpad_v[:, p % KS:p % KS + RB, p // KS:p // KS + N],
                                               ALU.add, ALU.mult).then_inc(sig("inv_prod"), 1)

        @block.tensor
        def _(pe):
            mm = nc.tensor.matmul

            def keep_warm(b, n, operand=cst):
                for _ in range(n):
                    mm(bank[b][:, 0:256], operand[:, 0:128], operand[:, 0:256], start=True, stop=True, skip_group_check=True)

            def centre(name, waits):
                src, dst, sset, cb, vb, w, eps = LN[name]
                for ch in range(2):
                    for who, count in waits[ch]:
                        pe.wait_ge(sig(who), at(who, count))
                    mm(bank[cb[ch]], K("center"), half(src, ch), start=name not in LN_OF_SUM, stop=True,
                       skip_group_check=True).then_inc(sig(f"{name}_centered"), 1)

            def centre_residual(name, residual):
                for ch in range(2):
                    mm(bank[LN[name][3][ch]], K("center"), half(residual, ch), start=True, stop=False, skip_group_check=True)

            def variance(name):
                src, dst, sset, cb, vb, w, eps = LN[name]
                for ch in range(2):
                    pe.wait_ge(sig(f"{name}_sq"), at(f"{name}_sq", ch + 1))
                    mm(bank[vb[ch]], K("mean"), half(sq[sset], ch), start=True, stop=True).then_inc(sig(f"{name}_var"), 1)

            def layer_norm(name, waits, warm=None):
                centre(name, waits)
                variance(name)
                if warm is None:
                    warm = WARM_LN - 1 if name in LN_BIAS_FOLDED else WARM_LN
                keep_warm(2 if name.endswith("lno") else 4, warm)

            pe.wait_ge(sig("blank"), at("blank", 1))
            keep_warm(4, WARM_START, sq[0])
            pe.wait_ge(sig("in_stats"), at("in_stats", 16))
            layer_norm("tm0_ln", ([("in_z0R_0", 16)], [("in_z0R_1", 16)]), 0)
            pe.wait_ge(sig("in_const"), at("in_const", 16))
            pe.wait_ge(sig("in_qk"), at("in_qk", 16))
            for s in range(2):
                for h in range(H):
                    q0 = s * 1024 + h * 128
                    last = mm(bank[6 + s][:, h * 128:(h + 1) * 128], qk[:, q0:q0 + 128], qk[:, q0 + 512:q0 + 640], start=True, stop=True)
                last.then_inc(sig("qk_product"), 1)

            def ab_projections(st, s, tiles):
                pe.wait_ge(sig("rows_ready"), at("rows_ready", 2))
                pe.wait_ge(sig("in_tmw"), at("in_tmw", 16))
                for u in tiles:
                    pe.wait_ge(sig(f"{st}_ln_x"), at(f"{st}_ln_x", 1 + u // 4))
                    if u >= 4:
                        pe.wait_ge(sig(f"{st}_ab"), at(f"{st}_ab", u - 3))
                    elif u >= 2 and s == 0:
                        pe.wait_ge(sig("wyh_ready"), at("wyh_ready", u - 1))
                    b = bank[4 + u % 4]
                    mm(b, selr[:, :], rows[:, s * 512:(s + 1) * 512], start=True, stop=False, skip_group_check=True)
                    mm(b, x[:, 2 * u * N:(2 * u + 2) * N], tmw[:, s * 768:s * 768 + 512], start=False, stop=True,
                       skip_group_check=True).then_inc(sig(f"{st}_abproj"), 1)

            def gate_projection(st, s, src, src_name, b0):
                for ch in range(2):
                    pe.wait_ge(sig(src_name), at(src_name, ch + 1))
                    mm(bank[b0 + ch], tmw[:, s * 768 + 512:s * 768 + 640], half(src, ch), start=True, stop=True).then_inc(sig(f"{st}_gproj"), 1)

            def triangle(st, lhs_kind):
                pe.wait_ge(sig(f"{st}_ab"), at(f"{st}_ab", 8))
                for c in range(C):
                    hf, cc = c // CH, c % CH
                    kept = ab[64 * hf:64 * hf + 64, :].rearrange("p (m k) -> p m k", k=C)
                    moved = ab[64 * hf:64 * hf + 64, :].rearrange("p (r g k) -> p g r k", g=GB, k=C)
                    last = mm(bank[4 + c // 8][0:64, (c % 8) * N:(c % 8 + 1) * N].rearrange("p (g r) -> p g r", g=GB),
                              kept[:, :, lhs_kind * CH + cc], moved[:, :, :, (1 - lhs_kind) * CH + cc], start=True, stop=True)
                    if c % 8 == 7:
                        last.then_inc(sig(f"{st}_t"), 1)

            def triangle_back(st, s, in_gap):
                if st == "tm0":
                    pe.wait_ge(sig("tm0_lng_logv"), at("tm0_lng_logv", 2))
                    pe.wait_ge(sig("in_tmw"), at("in_tmw", 16))
                    pe.wait_ge(sig("in_ptw"), at("in_ptw", 16))
                    pe.wait_ge(sig("in_vec"), at("in_vec", 16))
                    for tm in range(2):
                        mm(bank[3][:, tm:tm + 1], tmw[:, tm * 768 + 640:tm * 768 + 768], V(f"tm{tm}_lnout_b"), start=True, stop=True,
                           skip_group_check=True)
                    mm(bank[3][:, 2:3], ptw[0:C, 0:128], V("pt_b")[0:C, :], start=True, stop=True,
                       skip_group_check=True).then_inc(sig("bias_products"), 1)
                keep_warm(2, 1 if st == "tm0" else WARM_TRIANGLE)
                pe.wait_ge(sig(f"{st}_tP_act"), at(f"{st}_tP_act", 2))
                pe.wait_ge(sig(f"{st}_tP_dve"), at(f"{st}_tP_dve", 2))
                for n in range(RB):
                    if n == HB:
                        pe.wait_ge(sig("folded"), 1)
                    last = nc.tensor.transpose(bank[2 + n // HB][:, (n % HB) * N:(n % HB + 1) * N],
                                               tP[:, n * 128:(n + 1) * 128], K("ident")[0:64, 0:64])
                    if n % HB == HB - 1:
                        last.then_inc(sig(f"{st}_ttr"), 1)
                layer_norm(f"{st}_lno", ([(f"{st}_tB_act", 1)], [(f"{st}_tB_dve", 1)]), 1)
                in_gap()
                for ch in range(2):
                    pe.wait_ge(sig(f"{st}_lno_x"), at(f"{st}_lno_x", ch + 1))
                    mm(bank[6 + ch][:, :], tmw[:, s * 768 + 640:s * 768 + 768], half(y, ch), start=True, stop=True).then_inc(sig(f"{st}_zo"), 1)

            ab_projections("tm0", 0, range(0, 4))
            centre("tm0_lng", ([("in_z0T", 16), ("tm0_ln_x", 2)], []))
            ab_projections("tm0", 0, range(4, 8))
            variance("tm0_lng")
            triangle("tm0", 0)

            triangle_back("tm0", 0, lambda: gate_projection("tm0", 0, xg, "tm0_lng_x", 2))
            centre_residual("tm1_ln", z0T)
            layer_norm("tm1_ln", ([("tm0_upd", 1)], [("tm0_upd", 2)]))
            ab_projections("tm1", 1, range(8))
            gate_projection("tm1", 1, x, "tm1_ln_x", 0)
            triangle("tm1", 1)

            def in_gap():
                pe.wait_ge(sig("tm1_gtanh"), at("tm1_gtanh", 2))
                pe.wait_ge(sig("z1_settled"), at("z1_settled", 1))
                centre_residual("ta0_ln", z1R)

            triangle_back("tm1", 1, in_gap)

            def attention(st, s, swap, ln_waits):
                w0 = s * TAW
                layer_norm(f"{st}_ln", ln_waits)
                pe.wait_ge(sig("in_taw"), at("in_taw", 16))
                for ch in range(2):
                    pe.wait_ge(sig(f"{st}_ln_x"), at(f"{st}_ln_x", ch + 1))
                    mm(bank[4 + ch][0:16, :], taw[:, w0 + 256:w0 + 272], half(x, ch), start=True, stop=True).then_inc(sig(f"{st}_bproj"), 1)

                for ch in range(2):
                    for h in range(H):
                        if ch == 1 and YBANKS[ch][h] >= 4:
                            pe.wait_ge(sig(f"{st}_brow"), at(f"{st}_brow", YBANKS[ch][h] - 3))
                        mm(bank[YBANKS[ch][h]], wyh[:, s * 512 + h * 128:s * 512 + (h + 1) * 128], half(x, ch),
                           start=True, stop=True).then_inc(sig(f"{st}_yproj"), 1)

                def fill(kind):
                    m, n = FILL.index(kind), int(kind[1])
                    if m >= 2:
                        pe.wait_ge(sig(f"{st}_fill_act"), at(f"{st}_fill_act", m - 1))
                    b = bank[6 + m % 2]
                    pe.wait_ge(sig("wvg_ready"), at("wvg_ready", 1))
                    pe.wait_ge(sig(f"{st}_xstacked"), at(f"{st}_xstacked", 16 * GB * 4))
                    if kind[0] == "v":
                        for g in range(GB):
                            x0 = g * F + 2 * n * N
                            last = mm(b[:, 128 * g:128 * g + 128], xstack[:, x0:x0 + 128], wvg[:, s * 256:s * 256 + 128],
                                      start=True, stop=True)
                    else:
                        last = mm(b, wvg[:, s * 256 + 128:s * 256 + 256], xstack[:, n * HALF:(n + 1) * HALF], start=True, stop=True)
                    last.then_inc(sig(f"{st}_fill"), 1)

                pe.wait_ge(sig(f"{st}_y_act"), at(f"{st}_y_act", 4))
                pe.wait_ge(sig(f"{st}_y_dve"), at(f"{st}_y_dve", 4))
                pe.wait_ge(sig(f"{st}_xbd"), at(f"{st}_xbd", 2))
                keep_warm(7, WARM_HOP)
                pe.wait_ge(sig(f"{st}_bst"), at(f"{st}_bst", 2))
                pe.wait_ge(sig("pair_ready"), at("pair_ready", 1))
                pe.wait_ge(sig(f"{st}_brow"), at(f"{st}_brow", 2))
                def out_projection(t):
                    if t not in OUT_STEPS[swap]:
                        return
                    g0, g1, r0, r1, tiles = OUT_PARTS[swap][OUT_STEPS[swap].index(t)]
                    gs, rs = slice(g0, g1), slice(r0, r1)
                    pe.wait_ge(sig("wo_ready"), at("wo_ready", 2))
                    pe.wait_ge(sig(f"{st}_og"), at(f"{st}_og", tiles))
                    pe.wait_ge(sig(f"{st}_fill_act"), at(f"{st}_fill_act", len(FILL)))
                    for ch in range(2):
                        for b in range(GB):
                            o = bank[6 + ch][C * b:C * b + C, :]
                            if swap:
                                q = og[:, :].rearrange("p (g r q) -> p q g r", g=GB, r=RB)[:, b * RB + ch * HB:b * RB + (ch + 1) * HB, gs, rs]
                                o = o.rearrange("p (q g r) -> p q g r", g=GB, r=RB)[:, :, gs, rs]
                            elif gs.start <= b < gs.stop and rs.start <= ch * HB < rs.stop:
                                q = og[:, b * F + ch * HALF:b * F + (ch + 1) * HALF]
                            else:
                                continue
                            last = mm(o, wohalf[:, s * C:(s + 1) * C], q, start=True, stop=True, skip_group_check=True)
                        if g1 == GB and (t is None if swap else r0 == ch * HB):
                            last.then_inc(sig(f"{st}_oproj"), 1)

                for t in range(TILES + LAG_A):
                    if t < TILES:
                        gp, r0 = tile_of(t)
                        if t >= 2:
                            pe.wait_ge(sig(f"{st}_shifted"), at(f"{st}_shifted", t - 1))
                        b = bank[t % 2]
                        mm(b, pairr[:, :], bst[:, :], start=True, stop=False, skip_group_check=True)
                        for i2 in range(2):
                            r = r0 + i2
                            last = mm(b.rearrange("p (h a k) -> p h a k", h=H, a=2)[:, :, i2, :],
                                      xbd[64 * gp:64 * gp + 64, r * 128:(r + 1) * 128],
                                      Y[64 * gp:64 * gp + 64, :].rearrange("p (h f) -> p h f", h=H)[:, :, r * N:(r + 1) * N],
                                      start=False, stop=True, skip_group_check=True)
                        last.then_inc(sig(f"{st}_scores"), 1)
                    if t < LAG_P:
                        keep_warm(4, WARM_HEAD)
                    if t < len(FILL_STEPS):
                        for kind in FILL_STEPS[t]:
                            fill(kind)
                    if LAG_P <= t < TILES + LAG_P:
                        u = t - LAG_P
                        if u >= 2:
                            pe.wait_ge(sig(f"{st}_PT"), at(f"{st}_PT", u - 1))
                        keep_warm(2 + u % 2, WARM_STEP[t])
                        pe.wait_ge(sig(f"{st}_probs"), at(f"{st}_probs", u + 1))
                        for k in range(4):
                            last = nc.tensor.transpose(bank[2 + u % 2][:, 128 * k:128 * k + 128],
                                                       PN[u % 2][:, 128 * k:128 * k + 128], K("ident"))
                        last.then_inc(sig(f"{st}_ptrans"), 1)
                    if t >= LAG_A:
                        u = t - LAG_A
                        gp, r0 = tile_of(u)
                        if t >= TILES:
                            pe.wait_ge(sig(f"{st}_shifted"), at(f"{st}_shifted", TILES))
                            keep_warm(0, WARM_TAIL[t - TILES])
                        pe.wait_ge(sig(f"{st}_PT"), at(f"{st}_PT", u + 1))
                        pe.wait_ge(sig(f"{st}_fill_act"), at(f"{st}_fill_act", filled(f"v{u % 8}")))
                        if u >= 1:
                            pe.wait_ge(sig(f"{st}_avout"), at(f"{st}_avout", u))
                        for i2 in range(2):
                            for g2 in range(2):
                                for h in range(H):
                                    v0 = ((u % 8) * GB + 2 * gp + g2) * 128 + h * C
                                    p0 = h * 128 + g2 * 64
                                    o0 = g2 * 64
                                    last = mm(bank[4 + i2][C * h:C * h + C, o0:o0 + 64], vals[64 * i2:64 * i2 + 64, v0:v0 + C],
                                              PT[u % 2][64 * i2:64 * i2 + 64, p0:p0 + 64], start=True, stop=True, skip_group_check=True)
                        last.then_inc(sig(f"{st}_av"), 1)
                    out_projection(t)
                keep_warm(0, WARM_END)
                out_projection(None)

            attention("ta0", 0, True, ([("tm1_upd", 1)], [("tm1_upd", 2)]))
            attention("ta1", 1, False, ([("ta0_z", 1)], [("ta0_z", 2)]))
            layer_norm("pt_ln", ([("ta1_z", 1)], [("ta1_z", 2)]))
            pe.wait_ge(sig("in_ptw"), at("in_ptw", 16))
            def hidden(ns):
                for n in ns:
                    pe.wait_ge(sig("pt_ln_x"), at("pt_ln_x", n // 4 + 1))
                    if n >= 4:
                        pe.wait_ge(sig("pt_hdve" if n % 2 else "pt_hact"), (n - 4) // 2 + 1)
                    mm(bank[4 + n % 4], ptw[:, (n % 4) * 128:(n % 4 + 1) * 128], half(x, n // 4), start=True, stop=True,
                       ).then_inc(sig("pt_hproj"), 1)

            def second_layer(ch):
                pe.wait_ge(sig("pt_hact"), 2 * ch + 2)
                pe.wait_ge(sig("pt_hdve"), 2 * ch + 2)
                for g in range(GB):
                    last = mm(bank[ch][C * g:C * g + C, :], ptw[:, 512:512 + C], hid[4 * ch + g], start=True, stop=True,
                              skip_group_check=True)
                last.then_inc(sig("pt_hused"), 1)

            hidden((0, 1, 2, 3, 4))
            second_layer(0)
            hidden((5, 6, 7))
            pe.wait_ge(sig("in_ivw1"), at("in_ivw1", 16))
            for ch in range(2):
                if ch == 1:
                    second_layer(1)
                pe.wait_ge(sig("pt_z"), at("pt_z", ch + 1))
                mm(rows8(bank[2 + ch][:, :]), ivw1[:, :], window(ch, 0, 0), start=True, stop=True).then_inc(sig("inv_zproj"), 1)
            keep_warm(4, WARM_KERNEL)
            pe.wait_ge(sig("w2_ready"), at("w2_ready", 1))
            pe.wait_ge(sig("inv_zr"), 2)
            LAG = 2
            kern = 0
            for j in range(len(SUMS) + LAG):
                while kern < TAPS and (j >= len(SUMS) or kern <= SUMS[j][-1]):
                    p = TAP_ORDER[kern]
                    if kern >= 3:
                        pe.wait_ge(sig("inv_prod"), kern - 2)
                    for ch in range(2):
                        pe.wait_ge(sig("inv_zst"), ch + 1)
                        last = mm(half(kern_banks(kern), ch), w2s[:, p * 128:(p + 1) * 128], half(zst, ch), start=True, stop=True)
                    last.then_inc(sig("inv_kern"), 1)
                    kern += 1
                if j < LAG:
                    continue
                taps = SUMS[j - LAG]
                if len(taps) == 2:
                    pe.wait_ge(sig("inv_sum"), j - LAG - HEAD_SINGLES + 1)
                    term = psums[(j - LAG - HEAD_SINGLES) % NSUM]
                else:
                    pe.wait_ge(sig("inv_prod"), taps[0] + 1)
                    term = prod[taps[0] % NPROD]
                for ch in range(2):
                    last = mm(bank[ch], K("ident"), half(term, ch), start=(j == LAG), stop=(j == len(SUMS) + LAG - 1))
                last.then_inc(sig("inv_acc"), 1)


def kernel(**inputs):
    import numpy as np
    import concourse.bacc as bacc
    from concourse.bass_utils import run_bass_kernel_spmd

    a = {k.replace("L0_conv_", "").replace("L1_conv_", "inv_"): np.asarray(v) for k, v in inputs.items()}
    f4 = a["x"].dtype

    def blocked(m):
        return np.ascontiguousarray(m.reshape(GB, RB, N, C).transpose(0, 3, 1, 2).reshape(128, F))

    def diag(w):
        o = np.zeros((GB, C, GB, w.shape[1]), f4)
        for g in range(GB):
            o[g, :, g] = w
        return o.reshape(128, -1)

    def rep(v):
        return np.tile(v, (GB,) + (1,) * (v.ndim - 1))

    z = a["x"][0]
    vecs = np.zeros((128, NVEC), f4)

    def put(name, v):
        vecs[:, VEC[name]] = v

    def zparts(v):
        return np.tile(v, 128 // G8)

    p = np.arange(128)
    for s in range(2):
        put(f"tm{s}_lnin_w", rep(a["tm_ln_in_w"][s])); put(f"tm{s}_lnin_b", rep(a["tm_ln_in_b"][s]))
        put(f"tm{s}_lnout_w", rep(a["tm_lnout_w"][s])); put(f"tm{s}_lnout_b", rep(a["tm_lnout_b"][s]))
        put(f"fold_tm{s}", rep(a["tm_zo_b"][s])); put(f"tm{s}_gb", rep(a["tm_g_b"][s]))
        put(f"ta{s}_ln_w", rep(a["ta_ln_w"][s])); put(f"ta{s}_ln_b", rep(a["ta_ln_b"][s]))
        put(f"ta{s}_ob", rep(a["ta_o_b"][s])); put(f"ta{s}_gb", a["ta_g_b"][s])
    put("pt_w", rep(a["pt_ln_w"])); put("pt_b", rep(a["pt_ln_b"]))
    put("fold_pt", a["pt_1_b"]); put("pt_b2", rep(a["pt_2_b"]))
    for n, k in (("bn_b1", "inv_b1"), ("bn_gamma", "inv_gamma"), ("bn_beta", "inv_beta"), ("bn_mean", "inv_mean"), ("bn_var", "inv_var")):
        put(n, zparts(a[k]))
    put("eps5", 1e-5); put("eps5x16", 16e-5); put("eps3", 1e-3)
    put("mask_g0", (p // C) % 2 == 0); put("mask_g1", (p // C) % 2 == 1)
    put("lo_z", -1.0 * ((p // G8) % 4 >= 2))
    put("lo_w", -1.0 * ((p // G8) % 2 == 1))
    put("lo_q", -1.0 * ((p // C) % 2 == 1))
    put("lo_pair", -1.0 * (p >= N))
    put("lo_row", -1.0 * (p % 2 == 1))
    vecs[:, VEC["b2"]:VEC["b2"] + TAPS] = np.tile(a["inv_b2"].reshape(TAPS, G8).T, (128 // G8, 1))

    eye = np.eye(128, dtype=f4)
    mean = diag(np.full((C, C), 1.0 / C, f4))
    pair = (p[:, None] % N == p[None, :] % N).astype(f4)
    bdscale = diag(np.full((C, C), 1.0 / np.sqrt(C), f4))
    consts = np.concatenate([{"ident": eye, "center": eye - mean, "mean": mean, "bdscale": bdscale, "pair": pair}[k] for k in CONST], 1)
    selrow = np.ones((2, 128), f4)

    tm_w, tm_rows = [], []
    for s in range(2):
        def columns(w):
            halves = [w[k][..., CH * ch:CH * ch + CH] for kinds in (("ap", "bp"), ("ag", "bg")) for ch in range(2) for k in kinds]
            return np.concatenate(halves, -1)

        tm_w.append(diag(columns({k: a[f"tm_{k}_w"][s] for k in ("ap", "bp", "ag", "bg")})))
        tm_w += [diag(a["tm_g_w"][s]), diag(a["tm_zo_w"][s])]
        row = np.tile(columns({k: a[f"tm_{k}_b"][s] for k in ("ap", "bp", "ag", "bg")}), GB)
        tm_rows.append(np.stack([row, row]))
    ta_w, ta_qk = [], []
    for s in range(2):
        ta_w.append(rep(a["ta_v_w"][s]))
        pair_w = diag(a["ta_b_w"][s]).reshape(128, GB, H).transpose(0, 2, 1).reshape(128, GB * H)
        ta_w += [rep(a["ta_g_w"][s]), pair_w, a["ta_o_w"][s]]
        for k in ("ta_k_w", "ta_q_w"):
            w = a[k][s].reshape(C, H, C).transpose(2, 1, 0)
            ta_qk.append(np.tile(w[:, :, None, :], (1, 1, GB, 1)).reshape(C, H * 128))
    w2 = a["inv_w2"].reshape(G8, TAPS, G8)
    w2s = np.zeros((GB, 4, G8, TAPS, GB, 4, G8), f4)
    for g in range(GB):
        w2s[g, :, :, :, g] = w2[None, :, :, None, :]
    w1s = np.zeros((GB, C, GB, 4, G8), f4)
    for g in range(GB):
        w1s[g, :, g] = a["inv_w1"][:, None, :]

    arrays = {
        "z_rows": blocked(z), "z_cols": blocked(z.transpose(1, 0, 2)), "vecs": vecs, "consts": consts, "selrow": selrow,
        "tm_w": np.concatenate(tm_w, 1), "tm_rows": np.concatenate(tm_rows, 1),
        "ta_w": np.concatenate(ta_w, 1), "ta_qk": np.concatenate(ta_qk, 1),
        "pt_w": np.concatenate([diag(a["pt_1_w"]), a["pt_2_w"]], 1),
        "inv_w1": w1s.reshape(128, 128), "inv_w2": w2s.reshape(128, TAPS * 128),
    }
    nc = bacc.Bacc("TRN2", target_bir_lowering=False, num_devices=1)
    args = []
    for name, v in arrays.items():
        arrays[name] = np.ascontiguousarray(v)
        args.append(nc.dram_tensor(name, v.shape, F32, kind="ExternalInput").ap())
    args.append(nc.dram_tensor("result", (128, F), F32, kind="ExternalOutput").ap())
    build_program(nc, *args)
    r = run_bass_kernel_spmd(nc, [arrays], core_ids=[0]).results[0]["result"]
    return np.ascontiguousarray(r.reshape(GB, C, RB, N).transpose(3, 0, 2, 1).reshape(1, N, N, C))
```
